# Optimizing a Trainium2 kernel written in Bass

```python
import numpy as np
import jax
import jax.numpy as jnp

def _softmax(x, axis=-1):
    return jax.nn.softmax(x, axis=axis)

def _gelu(x):
    return jax.nn.gelu(x, approximate=True)

def _silu(x):
    return jax.nn.silu(x)

def _sigmoid(x):
    return jax.nn.sigmoid(x)

def _layernorm(x, axis=-1, eps=1e-05):
    m = jnp.mean(x, axis=axis, keepdims=True)
    v = jnp.var(x, axis=axis, keepdims=True)
    return (x - m) / jnp.sqrt(v + eps)

def _scatter_add(tgt, idx, src, axis=0):
    return tgt.at[idx].add(src)

def _segment_sum(src, seg, n):
    return jax.ops.segment_sum(src, seg, n)
kernel_name = 'mk_gnn_preln_d4_gnn_r64_c1bc0d'

def setup_inputs(seed: int=0):
    np.random.seed(seed)
    _w = jnp.asarray

    def _rec_inputs():
        import jax
        import jax.numpy as jnp
        _gk = jax.random.key(seed)
        x = -0.000202 + 1 * jax.random.normal(jax.random.fold_in(_gk, 1), (100000, 128), jnp.float32)
        src = jax.random.randint(jax.random.fold_in(_gk, 2), (25000,), 0, 100000, jnp.int32)
        dst = jnp.minimum((100000 * jax.random.uniform(jax.random.fold_in(_gk, 3), (25000,)) ** 2.0).astype(jnp.int32), 99999)
        _o = jnp.argsort(dst, stable=True)
        src = src[_o]
        dst = dst[_o]
        edge_attr_128 = -8.16379e-05 + 0.999858 * jax.random.normal(jax.random.fold_in(_gk, 12), (25000, 128), jnp.float32)
        edge_type_9 = jax.random.randint(jax.random.fold_in(_gk, 14), (25000,), 0, 9, jnp.int32)
        return (x, src, dst, edge_attr_128, edge_type_9)
    x, src, dst, edge_attr_128, edge_type_9 = _rec_inputs()

    def _L0_gnn_setup():
        import jax, jax.numpy as jnp
        import numpy as np
        N_NODES = 50000
        N_EDGES = 25000
        D_IN = 128
        D_HID = 128
        D_OUT = 128

        def _sage_mean(h, src, dst, inv_deg, W_neigh, W_self, b_self):
            neigh_sum = jax.ops.segment_sum(h[src], dst, num_segments=h.shape[0])
            h_neigh = neigh_sum * inv_deg
            return h @ W_self.T + b_self + h_neigh @ W_neigh.T
        key = jax.random.key(seed)
        ks = jax.random.split(key, 12)
        s = 0.05
        return {'x': jax.random.normal(ks[0], (N_NODES, D_IN), jnp.float32), 'src': jax.random.randint(ks[1], (N_EDGES,), 0, N_NODES), 'dst': jax.random.randint(ks[2], (N_EDGES,), 0, N_NODES), 'W_neigh1': jax.random.normal(ks[3], (D_HID, D_IN), jnp.float32) * s, 'W_self1': jax.random.normal(ks[4], (D_HID, D_IN), jnp.float32) * s, 'b_self1': jnp.zeros((D_HID,), jnp.float32), 'W_neigh2': jax.random.normal(ks[5], (D_HID, D_HID), jnp.float32) * s, 'W_self2': jax.random.normal(ks[6], (D_HID, D_HID), jnp.float32) * s, 'b_self2': jnp.zeros((D_HID,), jnp.float32), 'W_neigh3': jax.random.normal(ks[7], (D_OUT, D_HID), jnp.float32) * s, 'W_self3': jax.random.normal(ks[8], (D_OUT, D_HID), jnp.float32) * s, 'b_self3': jnp.zeros((D_OUT,), jnp.float32)}
    _L0_gnn_all = _L0_gnn_setup()
    _L0_gnn_in = {k: v for k, v in _L0_gnn_all.items() if k in ('W_neigh1', 'W_self1', 'b_self1', 'W_neigh2', 'W_self2', 'b_self2', 'W_neigh3', 'W_self3', 'b_self3')}
    del _L0_gnn_all

    def _L1_gnn_setup():
        import jax, jax.numpy as jnp
        import numpy as np
        N, E, DIN, DOUT = (100000, 12500, 128, 128)
        BN_EPS = 1e-05

        def _mean_agg(msg, seg_ids, n):
            summed = jax.ops.segment_sum(msg, seg_ids, num_segments=n)
            cnt = jax.ops.segment_sum(jnp.ones((msg.shape[0],), msg.dtype), seg_ids, num_segments=n)
            return summed / jnp.maximum(cnt, 1.0)[:, None]
        key = jax.random.key(seed)
        ks = jax.random.split(key, 10)
        node_embs = jax.random.normal(ks[0], (N, DIN), jnp.float32)
        edge_embs = jax.random.normal(ks[1], (E, DIN), jnp.float32)
        src = jax.random.randint(ks[2], (E,), 0, N, jnp.int32)
        dst = jax.random.randint(ks[3], (E,), 0, N, jnp.int32)
        s = 1.0 / np.sqrt(DIN)
        W_O = jax.random.uniform(ks[4], (DOUT, DIN), jnp.float32, -s, s)
        b_O = jax.random.uniform(ks[5], (DOUT,), jnp.float32, -s, s)
        W_I = jax.random.uniform(ks[6], (DOUT, DIN), jnp.float32, -s, s)
        b_I = jax.random.uniform(ks[7], (DOUT,), jnp.float32, -s, s)
        W_S = jax.random.uniform(ks[8], (DOUT, DIN), jnp.float32, -s, s)
        b_S = jax.random.uniform(ks[9], (DOUT,), jnp.float32, -s, s)
        gamma = jnp.ones((DOUT,), jnp.float32)
        beta = jnp.zeros((DOUT,), jnp.float32)
        return dict(node_embs=node_embs, edge_embs=edge_embs, src=src, dst=dst, W_O=W_O, b_O=b_O, W_I=W_I, b_I=b_I, W_S=W_S, b_S=b_S, gamma=gamma, beta=beta)
    _L1_gnn_all = _L1_gnn_setup()
    _L1_gnn_in = {k: v for k, v in _L1_gnn_all.items() if k in ('W_O', 'b_O', 'W_I', 'b_I', 'W_S', 'b_S', 'gamma', 'beta')}
    del _L1_gnn_all

    def _L2_gnn_setup():
        import jax, jax.numpy as jnp
        import numpy as np
        NUM_EDGE_TYPES = 8
        HIDDEN = 128
        N_NODES = 50000
        N_EDGES = 9375

        def _gru_cell(x, h, W_ih, W_hh, b_ih, b_hh):
            H = h.shape[-1]
            gi = x @ W_ih.T + b_ih
            gh = h @ W_hh.T + b_hh
            i_r, i_z, i_n = (gi[:, :H], gi[:, H:2 * H], gi[:, 2 * H:])
            h_r, h_z, h_n = (gh[:, :H], gh[:, H:2 * H], gh[:, 2 * H:])
            r = jax.nn.sigmoid(i_r + h_r)
            z = jax.nn.sigmoid(i_z + h_z)
            n = jnp.tanh(i_n + r * h_n)
            return (1.0 - z) * n + z * h
        key = jax.random.key(seed)
        ks = jax.random.split(key, 10)
        H = HIDDEN
        h = jax.random.normal(ks[0], (N_NODES, H), dtype=jnp.float32)
        edge_index = jax.random.randint(ks[1], (2, N_EDGES), 0, N_NODES, dtype=jnp.int32)
        edge_type = jax.random.randint(ks[2], (N_EDGES,), 0, NUM_EDGE_TYPES + 1, dtype=jnp.int32)
        s = 1.0 / np.sqrt(H)
        W_msg = jax.random.uniform(ks[3], (H, H), jnp.float32, -s, s)
        b_msg = jax.random.uniform(ks[4], (H,), jnp.float32, -s, s)
        edge_embed = jax.random.normal(ks[5], (NUM_EDGE_TYPES + 1, H), dtype=jnp.float32)
        W_ih = jax.random.uniform(ks[6], (3 * H, H), jnp.float32, -s, s)
        W_hh = jax.random.uniform(ks[7], (3 * H, H), jnp.float32, -s, s)
        b_ih = jax.random.uniform(ks[8], (3 * H,), jnp.float32, -s, s)
        b_hh = jax.random.uniform(ks[9], (3 * H,), jnp.float32, -s, s)
        return {'h': h, 'edge_index': edge_index, 'edge_type': edge_type, 'num_nodes': N_NODES, 'W_msg': W_msg, 'b_msg': b_msg, 'edge_embed': edge_embed, 'W_ih': W_ih, 'W_hh': W_hh, 'b_ih': b_ih, 'b_hh': b_hh}
    _L2_gnn_all = _L2_gnn_setup()
    _L2_gnn_in = {k: v for k, v in _L2_gnn_all.items() if k in ('W_msg', 'b_msg', 'edge_embed', 'W_ih', 'W_hh', 'b_ih', 'b_hh')}
    del _L2_gnn_all

    def _L3_gnn_setup():
        import jax, jax.numpy as jnp
        import numpy as np
        N = 100000
        E = 25000
        D = 128
        key = jax.random.key(seed)
        k1, k2, k3, k4 = jax.random.split(key, 4)
        features = jax.random.normal(k1, (N, D), dtype=jnp.float32)
        W = jax.random.normal(k2, (D, D), dtype=jnp.float32) / np.sqrt(D).astype(np.float32)
        b = jax.random.normal(k3, (D,), dtype=jnp.float32) * 0.01
        edge_index = jax.random.randint(k4, (2, E), 0, N, dtype=jnp.int64)
        return {'features': features, 'W': W, 'b': b, 'edge_index': edge_index}
    _L3_gnn_all = _L3_gnn_setup()
    _L3_gnn_in = {k: v for k, v in _L3_gnn_all.items() if k in ('W', 'b')}
    del _L3_gnn_all
    return {'x': x, 'src': src, 'dst': dst, 'edge_attr_128': edge_attr_128, 'edge_type_9': edge_type_9, 'L0_gnn_W_neigh1': _L0_gnn_in['W_neigh1'], 'L0_gnn_W_self1': _L0_gnn_in['W_self1'], 'L0_gnn_b_self1': _L0_gnn_in['b_self1'], 'L0_gnn_W_neigh2': _L0_gnn_in['W_neigh2'], 'L0_gnn_W_self2': _L0_gnn_in['W_self2'], 'L0_gnn_b_self2': _L0_gnn_in['b_self2'], 'L0_gnn_W_neigh3': _L0_gnn_in['W_neigh3'], 'L0_gnn_W_self3': _L0_gnn_in['W_self3'], 'L0_gnn_b_self3': _L0_gnn_in['b_self3'], 'L1_gnn_W_O': _L1_gnn_in['W_O'], 'L1_gnn_b_O': _L1_gnn_in['b_O'], 'L1_gnn_W_I': _L1_gnn_in['W_I'], 'L1_gnn_b_I': _L1_gnn_in['b_I'], 'L1_gnn_W_S': _L1_gnn_in['W_S'], 'L1_gnn_b_S': _L1_gnn_in['b_S'], 'L1_gnn_gamma': _L1_gnn_in['gamma'], 'L1_gnn_beta': _L1_gnn_in['beta'], 'L2_gnn_W_msg': _L2_gnn_in['W_msg'], 'L2_gnn_b_msg': _L2_gnn_in['b_msg'], 'L2_gnn_edge_embed': _L2_gnn_in['edge_embed'], 'L2_gnn_W_ih': _L2_gnn_in['W_ih'], 'L2_gnn_W_hh': _L2_gnn_in['W_hh'], 'L2_gnn_b_ih': _L2_gnn_in['b_ih'], 'L2_gnn_b_hh': _L2_gnn_in['b_hh'], 'L3_gnn_W': _L3_gnn_in['W'], 'L3_gnn_b': _L3_gnn_in['b']}

def reference(x, src, dst, edge_attr_128, edge_type_9, L0_gnn_W_neigh1, L0_gnn_W_self1, L0_gnn_b_self1, L0_gnn_W_neigh2, L0_gnn_W_self2, L0_gnn_b_self2, L0_gnn_W_neigh3, L0_gnn_W_self3, L0_gnn_b_self3, L1_gnn_W_O, L1_gnn_b_O, L1_gnn_W_I, L1_gnn_b_I, L1_gnn_W_S, L1_gnn_b_S, L1_gnn_gamma, L1_gnn_beta, L2_gnn_W_msg, L2_gnn_b_msg, L2_gnn_edge_embed, L2_gnn_W_ih, L2_gnn_W_hh, L2_gnn_b_ih, L2_gnn_b_hh, L3_gnn_W, L3_gnn_b):
    import jax
    import jax.numpy as jnp

    def _L0_gnn_ref(x, src, dst, W_neigh1, W_self1, b_self1, W_neigh2, W_self2, b_self2, W_neigh3, W_self3, b_self3):
        import jax, jax.numpy as jnp
        import numpy as np
        N_NODES = 50000
        N_EDGES = 25000
        D_IN = 128
        D_HID = 128
        D_OUT = 128

        def _sage_mean(h, src, dst, inv_deg, W_neigh, W_self, b_self):
            neigh_sum = jax.ops.segment_sum(h[src], dst, num_segments=h.shape[0])
            h_neigh = neigh_sum * inv_deg
            return h @ W_self.T + b_self + h_neigh @ W_neigh.T
        n = x.shape[0]
        deg = jax.ops.segment_sum(jnp.ones((src.shape[0],), x.dtype), dst, num_segments=n)
        inv_deg = (1.0 / jnp.maximum(deg, 1.0))[:, None]
        h = jax.nn.relu(_sage_mean(x, src, dst, inv_deg, W_neigh1, W_self1, b_self1))
        h = jax.nn.relu(_sage_mean(h, src, dst, inv_deg, W_neigh2, W_self2, b_self2))
        h = _sage_mean(h, src, dst, inv_deg, W_neigh3, W_self3, b_self3)
        return h

    def _L1_gnn_ref(node_embs, edge_embs, src, dst, W_O, b_O, W_I, b_I, W_S, b_S, gamma, beta):
        import jax, jax.numpy as jnp
        import numpy as np
        N, E, DIN, DOUT = (100000, 12500, 128, 128)
        BN_EPS = 1e-05

        def _mean_agg(msg, seg_ids, n):
            summed = jax.ops.segment_sum(msg, seg_ids, num_segments=n)
            cnt = jax.ops.segment_sum(jnp.ones((msg.shape[0],), msg.dtype), seg_ids, num_segments=n)
            return summed / jnp.maximum(cnt, 1.0)[:, None]
        n = node_embs.shape[0]
        ho = _mean_agg(node_embs[src] - edge_embs, dst, n)
        hi = _mean_agg(node_embs[dst] - edge_embs, src, n)
        h = (ho @ W_O.T + b_O + hi @ W_I.T + b_I + node_embs @ W_S.T + b_S) / 3.0
        mu = jnp.mean(h, axis=0)
        var = jnp.mean(jnp.square(h - mu), axis=0)
        return (h - mu) / jnp.sqrt(var + BN_EPS) * gamma + beta

    def _L2_gnn_ref(h, edge_index, edge_type, num_nodes, W_msg, b_msg, edge_embed, W_ih, W_hh, b_ih, b_hh):
        import jax, jax.numpy as jnp
        import numpy as np
        NUM_EDGE_TYPES = 8
        HIDDEN = 128
        N_NODES = 50000
        N_EDGES = 9375

        def _gru_cell(x, h, W_ih, W_hh, b_ih, b_hh):
            H = h.shape[-1]
            gi = x @ W_ih.T + b_ih
            gh = h @ W_hh.T + b_hh
            i_r, i_z, i_n = (gi[:, :H], gi[:, H:2 * H], gi[:, 2 * H:])
            h_r, h_z, h_n = (gh[:, :H], gh[:, H:2 * H], gh[:, 2 * H:])
            r = jax.nn.sigmoid(i_r + h_r)
            z = jax.nn.sigmoid(i_z + h_z)
            n = jnp.tanh(i_n + r * h_n)
            return (1.0 - z) * n + z * h
        src = edge_index[0]
        dst = edge_index[1]
        src_h = h[src] @ W_msg.T + b_msg
        emb = edge_embed[jnp.clip(edge_type, 0, NUM_EDGE_TYPES)]
        msg = src_h + emb
        messages = jax.ops.segment_sum(msg, dst, num_segments=num_nodes)
        h_new = _gru_cell(messages, h[:num_nodes], W_ih, W_hh, b_ih, b_hh)
        result = jnp.zeros_like(h).at[:num_nodes].set(h_new)
        return result

    def _L3_gnn_ref(features, W, b, edge_index):
        import jax, jax.numpy as jnp
        import numpy as np
        N = 100000
        E = 25000
        D = 128
        n = features.shape[0]
        h = features @ W.T + b
        src, dst = (edge_index[0], edge_index[1])
        msgs = jnp.take(h, dst, axis=0)
        agg = jax.ops.segment_sum(msgs, src, num_segments=n)
        deg = jax.ops.segment_sum(jnp.ones((src.shape[0],), h.dtype), src, num_segments=n)
        return jnp.where(deg[:, None] > 0, agg / deg[:, None], jnp.zeros_like(agg))
    edge_index = jnp.stack([src, dst])
    h = jnp.maximum(_layernorm(x, axis=-1), 0.0)
    x = x + _L0_gnn_ref(h, src, dst, L0_gnn_W_neigh1, L0_gnn_W_self1, L0_gnn_b_self1, L0_gnn_W_neigh2, L0_gnn_W_self2, L0_gnn_b_self2, L0_gnn_W_neigh3, L0_gnn_W_self3, L0_gnn_b_self3)
    h = jnp.maximum(_layernorm(x, axis=-1), 0.0)
    x = x + _L1_gnn_ref(h, edge_attr_128, src, dst, L1_gnn_W_O, L1_gnn_b_O, L1_gnn_W_I, L1_gnn_b_I, L1_gnn_W_S, L1_gnn_b_S, L1_gnn_gamma, L1_gnn_beta)
    h = jnp.maximum(_layernorm(x, axis=-1), 0.0)
    x = x + _L2_gnn_ref(h, edge_index, edge_type_9, 100000, L2_gnn_W_msg, L2_gnn_b_msg, L2_gnn_edge_embed, L2_gnn_W_ih, L2_gnn_W_hh, L2_gnn_b_ih, L2_gnn_b_hh)
    h = jnp.maximum(_layernorm(x, axis=-1), 0.0)
    x = x + _L3_gnn_ref(h, L3_gnn_W, L3_gnn_b, edge_index)
    return x

_drawn_inputs = setup_inputs


def setup_inputs(seed=0):
    import zlib

    import numpy as np

    out = dict(_drawn_inputs(seed))
    spreads = {'L0_gnn_b_self1': (0.0, 0.505),
     'L0_gnn_b_self2': (0.0, 0.1),
     'L0_gnn_b_self3': (0.0, 0.1),
     'L1_gnn_gamma': (1.0, 0.2),
     'L1_gnn_beta': (0.0, 0.1)}
    factors = {'L1_gnn_b_O': 64.0,
     'L1_gnn_b_I': 64.0,
     'L1_gnn_b_S': 64.0,
     'L2_gnn_b_msg': 8.0,
     'L2_gnn_b_ih': 3.559,
     'L2_gnn_b_hh': 6.217,
     'L3_gnn_b': 21.45}
    for name, (base, spread) in spreads.items():
        noise = np.random.default_rng([zlib.crc32(name.encode()), seed]).standard_normal(out[name].shape)
        drawn = base * np.exp(spread * noise) if base else spread * noise
        out[name] = jnp.asarray(drawn.astype(out[name].dtype))
    for name, factor in factors.items():
        out[name] = (out[name] * factor).astype(out[name].dtype)
    return out
```

```python
from contextlib import ExitStack

import concourse.bass as bass
from concourse import mybir

F32 = mybir.dt.float32
BF16 = mybir.dt.bfloat16
I32 = mybir.dt.int32
ALU = mybir.AluOpType
ACT = mybir.ActivationFunctionType
AX = mybir.AxisListType

D = 128
TILE = 4
ROWS = TILE * 128
EP = 125
EG = TILE * EP
LN_EPS = 1e-5


class Steps:

    def __init__(self, eng, sem, base):
        self.eng, self.sem, self.value = eng, sem, base

    def did(self, instruction):
        instruction.then_inc(self.sem, 1)
        self.value = self.value + 1

    def wait(self):
        self.eng.wait_ge(self.sem, self.value)


def sweep(eng, first, n, last, body, unroll=4, back=3, ahead=3, special=1):
    start = unroll * -(-(back + 1) // unroll)
    end = start + unroll * max(0, (n - special - ahead - start) // unroll)
    for i in range(first, min(start, last + 1)):
        body(i, i % unroll, lambda g: 0 <= g < n)
    if end > start:
        with eng.Fori(start // unroll, end // unroll) as k:
            for u in range(unroll):
                body(k * unroll + u, u, lambda g: True)
    for i in range(end, last + 1):
        body(i, i % unroll, lambda g: 0 <= g < n)


def slot_value(g, s, slots=4):
    return (g - s) * (16 // slots) + 16


class Net:

    def __init__(self, nc, ctx, N, E):
        self.nc, self.ctx, self.N, self.E = nc, ctx, N, E

    def sb(self, name, shape, dt=F32):
        return self.ctx.enter_context(self.nc.sbuf_tensor(name, shape, dt))

    def sem(self, name):
        return self.ctx.enter_context(self.nc.semaphore(name))

    def hold(self, eng, sem, value):
        eng.wait_ge(sem, value)
        eng.sem_inc(self.passed, 1)

    def sems(self, name, n):
        return [self.sem(f"{name}{k}") for k in range(n)]


def load_weights(nc, m, a):
    mats = [("self1", a["L0_gnn_W_self1"], 0), ("self2", a["L0_gnn_W_self2"], 0), ("self3", a["L0_gnn_W_self3"], 0),
            ("neigh1", a["L0_gnn_W_neigh1"], 0), ("neigh2", a["L0_gnn_W_neigh2"], 0), ("neigh3", a["L0_gnn_W_neigh3"], 0),
            ("O", a["L1_gnn_W_O"], 0), ("I", a["L1_gnn_W_I"], 0), ("S", a["L1_gnn_W_S"], 0), ("msg", a["L2_gnn_W_msg"], 0),
            ("ih_r", a["L2_gnn_W_ih"], 0), ("ih_z", a["L2_gnn_W_ih"], 1), ("ih_n", a["L2_gnn_W_ih"], 2),
            ("hh_r", a["L2_gnn_W_hh"], 0), ("hh_z", a["L2_gnn_W_hh"], 1), ("hh_n", a["L2_gnn_W_hh"], 2),
            ("out", a["L3_gnn_W"], 0)]
    cols = [("b1", a["L0_gnn_b_self1"], 0), ("b2", a["L0_gnn_b_self2"], 0), ("b3", a["L0_gnn_b_self3"], 0),
            ("bO", a["L1_gnn_b_O"], 0), ("bI", a["L1_gnn_b_I"], 0), ("bS", a["L1_gnn_b_S"], 0),
            ("gamma", a["L1_gnn_gamma"], 0), ("beta", a["L1_gnn_beta"], 0), ("bmsg", a["L2_gnn_b_msg"], 0),
            ("bih_r", a["L2_gnn_b_ih"], 0), ("bih_z", a["L2_gnn_b_ih"], 1), ("bih_n", a["L2_gnn_b_ih"], 2),
            ("bhh_r", a["L2_gnn_b_hh"], 0), ("bhh_z", a["L2_gnn_b_hh"], 1), ("bhh_n", a["L2_gnn_b_hh"], 2),
            ("bout", a["L3_gnn_b"], 0)]
    m.WT = m.sb("weightsT", [128, len(mats), D])
    m.w = {name: m.WT[:, k, :] for k, (name, _, _) in enumerate(mats)}
    m.COL = m.sb("bias_columns", [128, 24])
    m.col = {name: m.COL[:, k:k + 1] for k, (name, _, _) in enumerate(cols)}
    for k, name in enumerate(["b_r", "b_z", "eps"]):
        m.col[name] = m.COL[:, 17 + k:18 + k]
    m.b3row = m.sb("b3row", [128, D])
    m.ident = m.sb("ident", [128, 128])
    m.embed = m.sb("embed", [9, D])
    m.boutrow = m.sb("boutrow", [128, D])
    m.minus_half = m.sb("minus_half", [128, TILE])
    m.type_id = m.sb("type_id", [9, 1])
    m.Arow, m.Brow = m.sb("bn_scale", [128, D]), m.sb("bn_shift", [128, D])
    m.ones = m.sb("ones", [128, 128])
    early = ExitStack()
    raw = early.enter_context(nc.sbuf_tensor("weights_raw", [128, len(mats), D], F32))
    bmsg = early.enter_context(nc.sbuf_tensor("bmsg_rows", [9, D], F32))
    s_in, s_ms, s_id = m.sem("w_in"), m.sem("w_consts"), m.sem("w_ident")
    s_t, s_c, s_b = m.sem("w_turned"), m.sem("w_copied"), m.sem("w_gate_bias")
    m.passed = m.sem("passed")
    with nc.Block() as block:
        @block.sync
        def _(sp):
            for k, (_, ap, part) in enumerate(mats):
                sp.dma_start(raw[:, k, :], ap[part * D:(part + 1) * D, :]).then_inc(s_in, 16)
            for k, (_, ap, part) in enumerate(cols):
                sp.dma_start(m.COL[:, k:k + 1], ap[part * D:(part + 1) * D].rearrange("(p a) -> p a", a=1)).then_inc(s_in, 16)
            sp.dma_start(m.embed[:], a["L2_gnn_edge_embed"]).then_inc(s_in, 16)
            sp.dma_start(bmsg[:], a["L2_gnn_b_msg"].rearrange("(a n) -> a n", a=1).to_broadcast([9, D])).then_inc(s_in, 16)
            sp.dma_start(m.boutrow[:], a["L3_gnn_b"].rearrange("(a n) -> a n", a=1).to_broadcast([128, D])).then_inc(s_in, 16)
            sp.dma_start(m.b3row[:], a["L0_gnn_b_self3"].rearrange("(a n) -> a n", a=1).to_broadcast([128, D])).then_inc(s_in, 16)

        @block.gpsimd
        def _(pool):
            nc.gpsimd.memset(m.ident[:], 0.0).then_inc(s_ms, 1)
            nc.gpsimd.memset(m.ones[:], 1.0).then_inc(s_ms, 1)
            nc.gpsimd.memset(m.col["eps"], LN_EPS).then_inc(s_ms, 1)
            nc.gpsimd.memset(m.minus_half[:], -0.5).then_inc(s_ms, 1)
            nc.gpsimd.iota(m.type_id[:], [[0, 1]], base=0, channel_multiplier=1, allow_small_or_imprecise_dtypes=True).then_inc(s_ms, 1)
            pool.wait_ge(s_ms, 5)
            nc.gpsimd.affine_select(out=m.ident[:], in_=m.ident[:], compare_op=ALU.not_equal, fill=1.0, base=0,
                                    pattern=[[-1, 128]], channel_multiplier=1).then_inc(s_id, 1)

        @block.tensor
        def _(pe):
            pe.wait_ge(s_id, 1)
            pe.wait_ge(s_in, 16 * (len(mats) + len(cols) + 4))
            for k in range(len(mats)):
                if k >= 8:
                    pe.wait_ge(s_c, k - 7)
                nc.tensor.transpose(m.bank[k % 8][:, 0:128], raw[:, k, :], m.ident[:]).then_inc(s_t, 1)

        @block.vector
        def _(dve):
            for k in range(len(mats)):
                dve.wait_ge(s_t, k + 1)
                nc.vector.tensor_copy(m.WT[:, k, :], m.bank[k % 8][:, 0:128]).then_inc(s_c, 1)
            nc.vector.tensor_tensor(m.col["b_r"], m.col["bih_r"], m.col["bhh_r"], ALU.add).then_inc(s_b, 1)
            nc.vector.tensor_tensor(m.col["b_z"], m.col["bih_z"], m.col["bhh_z"], ALU.add).then_inc(s_b, 1)
            nc.vector.tensor_tensor(m.embed[:], m.embed[:], bmsg[:], ALU.add).then_inc(s_b, 1)
    early.close()


def dense_first(nc, m, a):
    N = m.N
    n = -(-N // ROWS)
    x_dram = a["x"]
    keep = ExitStack()

    def sb(name, shape):
        return keep.enter_context(nc.sbuf_tensor("d1_" + name, shape, F32))

    x = [sb(f"x{k}", [128, TILE, D]) for k in range(4)]
    xb = [sb(f"xb{k}", [128, TILE, D]) for k in range(4)]
    n1 = [sb(f"n1_{k}", [128, TILE, D]) for k in range(2)]
    n2 = [sb(f"n2_{k}", [128, TILE, D]) for k in range(2)]
    h0T = [sb(f"h0T{k}", [128, ROWS]) for k in range(2)]
    a1T = [sb(f"a1T{k}", [128, ROWS]) for k in range(2)]
    a2T = [sb(f"a2T{k}", [128, ROWS]) for k in range(2)]
    hT = [sb(f"hT{k}", [128, ROWS]) for k in range(2)]
    xg = [sb(f"xg{k}", [128, TILE, 2 * D]) for k in range(4)]
    st = [sb(f"st{k}", [128, 8, 6]) for k in range(2)]
    mv = [sb(f"mv{k}", [128, 8, 2]) for k in range(2)]
    sd = [sb(f"sd{k}", [128, 8]) for k in range(2)]
    rs = [sb(f"rs{k}", [128, 8]) for k in range(2)]
    nb = [sb(f"nb{k}", [128, 8]) for k in range(2)]
    pT1, pA, pB, pC, pG, pT2 = m.bank[0:6]

    s_x = m.sems("d1_x_in", 4)
    s_st = m.sems("d1_xg_out", 4)
    s_xb, s_n1, s_n2 = m.sem("d1_xb"), m.sem("d1_n1"), m.sem("d1_n2")
    s_T1, s_A, s_B, s_C, s_G, s_T2 = (m.sem("d1_" + k) for k in ("T1", "A", "B", "C", "G", "T2"))
    s_h0, s_a1, s_a2, s_h, s_g = (m.sem("d1_" + k) for k in ("h0T", "a1T", "a2T", "hT", "g"))
    s_x1, s_sd, s_dv, s_mv = m.sem("d1_x1"), m.sem("d1_sd"), m.sem("d1_dve"), m.sem("d1_mv")
    FIRST, LAST = -3, n + 2

    def base_of(g):
        return min(g * ROWS, N - ROWS) if isinstance(g, int) else g * ROWS

    with keep, nc.Block() as block:
        @block.sync
        def _(sp):
            def body(i, u, has):
                if has(i + 3):
                    if has(i - 1):
                        sp.wait_ge(s_n1, i)
                        sp.wait_ge(s_xb, i)
                    v = (u + 3) % 4
                    sp.dma_start(x[v][:], x_dram[bass.ds(base_of(i + 3), ROWS), :].rearrange("(p j) f -> p j f", j=TILE))\
                      .then_inc(s_x[v], 16)
                if has(i - 3):
                    v = (u + 1) % 4
                    sp.wait_ge(s_g, i - 2)
                    sp.wait_ge(s_x1, i - 2)
                    lo = 0
                    if isinstance(i, int) and i - 3 == n - 1:
                        lo = ((n - 1) * ROWS - (N - ROWS)) // TILE
                    sp.dma_start(m.XG[bass.ds(base_of(i - 3) + lo * TILE, ROWS - lo * TILE), :].rearrange("(p j) f -> p j f", j=TILE),
                                 xg[v][lo:128, :, :]).then_inc(s_st[v], 16)

            sweep(sp, FIRST, n, LAST, body)
            for v in range(4):
                sp.wait_ge(s_st[v], 16 * len(range(v, n, 4)))

        @block.vector
        def _(dve):
            def body(i, u, has):
                p, q = u % 2, (u + 1) % 2
                if has(i + 1) or has(i - 2):
                    dve.wait_ge(s_sd, i + 2)
                    if has(i - 4):
                        dve.wait_ge(s_n2, i - 3)
                    nc.vector.reciprocal(rs[q][:], sd[q][:]).then_inc(s_dv, 1)
                    dve.wait_ge(s_dv, 2 * (i + 2) + 1)
                    nc.vector.scalar_tensor_tensor(nb[q][:], mv[q][:, :, 0], -1.0, rs[q][:], ALU.mult, ALU.mult).then_inc(s_dv, 1)
                    dve.wait_ge(s_dv, 2 * (i + 2) + 2)
                if has(i + 1):
                    if has(i - 1):
                        dve.wait_ge(s_T1, i)
                    for j in range(TILE):
                        last = nc.vector.tensor_scalar(n1[q][:, j, :], x[(u + 1) % 4][:, j, :], rs[q][:, 4 + j:5 + j],
                                                       nb[q][:, 4 + j:5 + j], ALU.mult, ALU.add)
                    last.then_inc(s_n1, 1)
                if has(i - 1):
                    v = (u + 3) % 4
                    dve.wait_ge(s_C, i)
                    dve.wait_ge(s_xb, i)
                    if has(i - 5):
                        dve.wait_ge(s_st[v], slot_value(i - 5, v))
                    nc.vector.tensor_tensor(xg[v][:, :, 0:D], pC[:].rearrange("p (j f) -> p j f", j=TILE), xb[v][:], ALU.add)\
                      .then_inc(s_x1, 1)
                    dve.wait_ge(s_x1, i)
                if has(i + 2):
                    dve.wait_ge(s_x[(u + 2) % 4], slot_value(i + 2, (u + 2) % 4))
                for j in range(TILE):
                    if has(i - 1):
                        last = nc.vector.bn_stats(st[p][:, j, :], xg[(u + 3) % 4][:, j, 0:D])
                    if has(i + 2):
                        last = nc.vector.bn_stats(st[p][:, 4 + j, :], x[(u + 2) % 4][:, j, :])
                if has(i - 1) or has(i + 2):
                    last.then_inc(s_mv, 1)
                    m.hold(dve, s_mv, 2 * (i + 2) + 1)
                    for j in range(8):
                        if has(i - 1) if j < 4 else has(i + 2):
                            last = nc.vector.bn_aggr(mv[p][:, j, :], st[p][:, j, :])
                    last.then_inc(s_mv, 1)

            def setup():
                nc.vector.memset(mv[0][:], 1.0).then_inc(s_dv, 1)
                nc.vector.memset(mv[1][:], 1.0).then_inc(s_dv, 1)
                dve.wait_ge(s_dv, 2)

            setup()
            sweep(dve, FIRST + 1, n, LAST, body)

        @block.scalar
        def _(act):
            def evac(out, in_, func, done, ready, g, sem, **kw):
                act.wait_ge(ready, g + 1)
                nc.scalar.activation(out, in_, func, **kw).then_inc(sem, 1)

            def body(i, u, has):
                p = u % 2
                if has(i):
                    if has(i - 2):
                        act.wait_ge(s_A, i - 1)
                    evac(h0T[p][:], pT1[:], ACT.Relu, None, s_T1, i, s_h0)
                    if has(i - 2):
                        act.wait_ge(s_B, i - 1)
                    evac(a1T[p][:], pA[:], ACT.Relu, None, s_A, i, s_a1, bias=m.col["b1"])
                if has(i - 3):
                    act.wait_ge(s_x1, i - 2)
                    evac(xg[(u + 1) % 4][:, :, D:2 * D], pG[:].rearrange("p (j f) -> p j f", j=TILE), ACT.Copy, None,
                         s_G, i - 3, s_g, scale=1.0 / 3.0)
                if has(i):
                    if has(i - 2):
                        act.wait_ge(s_C, i - 1)
                    evac(a2T[p][:], pB[:], ACT.Relu, None, s_B, i, s_a2, bias=m.col["b2"])
                if has(i - 2):
                    if has(i - 4):
                        act.wait_ge(s_G, i - 3)
                    evac(hT[p][:], pT2[:], ACT.Relu, None, s_T2, i - 2, s_h)
                if has(i - 1) or has(i + 2):
                    act.wait_ge(s_mv, 2 * (i + 3))
                    nc.scalar.activation(sd[p][:], mv[p][:, :, 1], ACT.Sqrt, bias=m.col["eps"]).then_inc(s_sd, 1)

            sweep(act, FIRST + 1, n, LAST, body)

        @block.gpsimd
        def _(pool):
            def body(i, u, has):
                q = (u + 1) % 2
                if has(i - 2):
                    if has(i - 4):
                        pool.wait_ge(s_T2, i - 3)
                    m.hold(pool, s_dv, 2 * (i + 2) + 2)
                    for j in range(TILE):
                        last = nc.gpsimd.tensor_scalar(n2[p_of(u)][:, j, :], xg[(u + 2) % 4][:, j, 0:D], rs[q][:, j:j + 1],
                                                       nb[q][:, j:j + 1], ALU.mult, ALU.add)
                    last.then_inc(s_n2, 1)
                if has(i + 2):
                    v = (u + 2) % 4
                    if has(i - 2):
                        pool.wait_ge(s_x1, i - 1)
                    pool.wait_ge(s_x[v], slot_value(i + 2, v))
                    nc.gpsimd.tensor_tensor(xb[v][:], x[v][:], m.b3row[:].unsqueeze(1).to_broadcast([128, TILE, D]), ALU.add)\
                      .then_inc(s_xb, 1)

            def p_of(u):
                return u % 2

            sweep(pool, FIRST + 1, n, LAST, body)

        @block.tensor
        def _(pe):
            def body(i, u, has):
                p, q = u % 2, (u + 1) % 2
                if has(i):
                    pe.wait_ge(s_n1, i + 1)
                    if has(i - 1):
                        pe.wait_ge(s_h0, i)
                    for j in range(TILE):
                        last = nc.tensor.transpose(pT1[:, j * 128:(j + 1) * 128], n1[p][:, j, :], m.ident[:])
                    last.then_inc(s_T1, 1)
                if has(i - 1):
                    pe.wait_ge(s_a2, i)
                    if has(i - 2):
                        pe.wait_ge(s_x1, i - 1)
                    for j in range(TILE):
                        last = nc.tensor.matmul(pC[:, j * D:(j + 1) * D], a2T[q][:, j * 128:(j + 1) * 128], m.w["self3"],
                                                start=True, stop=True)
                    last.then_inc(s_C, 1)
                if has(i):
                    pe.wait_ge(s_h0, i + 1)
                    if has(i - 1):
                        pe.wait_ge(s_a1, i)
                    nc.tensor.matmul(pA[:], m.w["self1"], h0T[p][:], start=True, stop=True).then_inc(s_A, 1)
                if has(i - 3):
                    pe.wait_ge(s_h, i - 2)
                    if has(i - 4):
                        pe.wait_ge(s_g, i - 3)
                    for j in range(TILE):
                        last = nc.tensor.matmul(pG[:, j * D:(j + 1) * D], hT[q][:, j * 128:(j + 1) * 128], m.w["S"],
                                                start=True, stop=True)
                    last.then_inc(s_G, 1)
                if has(i):
                    pe.wait_ge(s_a1, i + 1)
                    if has(i - 1):
                        pe.wait_ge(s_a2, i)
                    nc.tensor.matmul(pB[:], m.w["self2"], a1T[p][:], start=True, stop=True).then_inc(s_B, 1)
                if has(i - 2):
                    pe.wait_ge(s_n2, i - 1)
                    if has(i - 3):
                        pe.wait_ge(s_h, i - 2)
                    for j in range(TILE):
                        last = nc.tensor.transpose(pT2[:, j * 128:(j + 1) * 128], n2[p][:, j, :], m.ident[:])
                    last.then_inc(s_T2, 1)

            sweep(pe, FIRST + 1, n, LAST, body)


class Phase:

    def __init__(self, m, name):
        self.m, self.name, self.stack, self.used = m, name, ExitStack(), []

    def sb(self, name, shape, dt=F32):
        return self.stack.enter_context(self.m.nc.sbuf_tensor(f"{self.name}_{name}", shape, dt))

    def slots(self, name, shape, dt=F32, count=4):
        return [self.sb(f"{name}_{k}", shape, dt) for k in range(count)]

    def sem(self, name):
        self.used.append(self.m.nc.alloc_semaphore(f"{self.name}_{name}"))
        return self.used[-1]

    def sems(self, name, count=4):
        return [self.sem(f"{name}_{k}") for k in range(count)]

    def __enter__(self):
        return self

    def __exit__(self, *err):
        self.stack.close()
        self.m.nc.clear_and_free_semaphores(self.used)
        self.m.nc.all_engine_barrier()


class Flow:

    def __init__(self, eng, has, m=None):
        self.eng, self.has, self.m = eng, has, m

    def wait(self, sem, value):
        if self.m is None or isinstance(value, int):
            self.eng.wait_ge(sem, value)
        else:
            self.m.hold(self.eng, sem, value)

    def after(self, sem, g):
        if self.has(g):
            self.wait(sem, g + 1)

    def landed(self, sems, g, v, per=16):
        if self.has(g):
            self.wait(sems[v % 4], (g - v % 4) * (per // 4) + per)


def edge_rows(table, i):
    return table[bass.ds(i * EG, EG), :].rearrange("(c p) f -> p c f", p=EP)


def finish(eng, sems, n, per=16):
    for v in range(4):
        if len(range(v, n, 4)):
            eng.wait_ge(sems[v], per * len(range(v, n, 4)))


def order_edges(nc, m, a):
    E = m.E
    T = E // EP
    n = T // TILE
    SPAN = E // EP
    PIECE = E // 5
    COPIES = 10
    tables = {k: nc.dram_tensor("sorted_" + k, [E, 1], I32, kind="Internal").ap() for k in ("dst", "src", "edge_type_9")}
    m.edge = {k: t.rearrange("e o -> (e o)") for k, t in tables.items()}
    m.edge["ea"] = nc.dram_tensor("sorted_edge_attr", [E, D], F32, kind="Internal").ap()
    m.ea_copied = 16 * COPIES
    m.s_ea = m.nc.alloc_semaphore("edge_attr_copied")
    with Phase(m, "order") as P:
        d, late = P.sb("keys", [EP, SPAN], I32), P.sb("descents", [EP, SPAN])
        b, blate = P.sb("borders", [EP - 1, 2], I32), P.sb("border_descents", [EP - 1, 1])
        total, flag = P.sb("descents_of_row", [EP, 1]), P.sb("unsorted", [1, 1], I32)
        s_d, s_v, s_t, s_c = P.sem("keys"), P.sem("dve"), P.sem("pe"), P.sem("copied")
        with nc.Block() as block:
            @block.sync
            def _(sp):
                sp.dma_start(d[:], a["dst"].rearrange("(p t) -> p t", p=EP)).then_inc(s_d, 16)
                sp.dma_start(b[:], a["dst"][SPAN - 1:SPAN - 1 + (EP - 1) * SPAN].rearrange("(p t) -> p t", t=SPAN)[:, 0:2]).then_inc(s_d, 16)
                for k in ("dst", "src", "edge_type_9"):
                    sp.dma_start(m.edge[k].rearrange("(p t) -> p t", p=EP), a[k].rearrange("(p t) -> p t", p=EP)).then_inc(s_c, 16)
                for k in range(COPIES):
                    r = slice(k * E // COPIES, (k + 1) * E // COPIES)
                    sp.dma_start(m.edge["ea"][r, :], a["edge_attr_128"][r, :]).then_inc(m.s_ea, 16)
                sp.wait_ge(s_c, 48)

            @block.vector
            def _(dve):
                dve.wait_ge(s_d, 32)
                nc.vector.tensor_tensor(late[:, 0:SPAN - 1], d[:, 1:SPAN], d[:, 0:SPAN - 1], ALU.is_lt).then_inc(s_v, 1)
                nc.vector.tensor_tensor(blate[:], b[:, 1:2], b[:, 0:1], ALU.is_lt).then_inc(s_v, 1)
                dve.wait_ge(s_v, 2)
                nc.vector.tensor_reduce(total[:], late[:, 0:SPAN - 1], op=ALU.add, axis=AX.X).then_inc(s_v, 1)
                dve.wait_ge(s_t, 1)
                nc.vector.tensor_scalar(flag[:], m.bank[0][0:1, 0:1], 1.0, None, ALU.min).then_inc(s_v, 1)
                dve.wait_ge(s_v, 4)

            @block.tensor
            def _(pe):
                pe.wait_ge(s_v, 3)
                nc.tensor.matmul(m.bank[0][0:1, 0:1], total[:], m.ones[0:EP, 0:1], start=True, stop=False)
                nc.tensor.matmul(m.bank[0][0:1, 0:1], blate[:], m.ones[0:EP - 1, 0:1], start=False, stop=True).then_inc(s_t, 1)

        unsorted = nc.values_load(flag[0:1, 0:1], min_val=0, max_val=1)
        keys, less = P.sb("all_keys", [EP, E]), P.sb("less", [EP, PIECE])
        raw = P.sb("raw_keys", [EP, PIECE], I32)
        cols = {k: P.sb("column_" + k, [EP, T], I32) for k in ("dst", "src", "edge_type_9")}
        kcol = P.sb("key_columns", [EP, T])
        earlier = P.sb("earlier", [EP, EP])
        part, rank, rank_i = P.sb("rank_parts", [EP, 6]), P.sb("rank", [EP, T]), P.sb("rank_i", [EP, T], I32)
        idx = P.sb("idx", [EP, TILE], I32)
        word = {k: P.sb("words_" + k, [EP, TILE], I32) for k in tables}
        ea = P.sb("ea", [EP, TILE, D])
        s_l, s_r, s_k, s_p, s_q, s_a, s_e, s_o = (P.sem("r_" + k) for k in ("cols", "raw", "keys", "ones", "rank", "all", "ea", "out"))
        s_w = P.sem("r_words")
        with nc.Block() as block:
            @block.sync
            def _(sp):
                with sp.If(unsorted > 0):
                    sp.wait_ge(m.s_ea, 16 * COPIES)
                    for k in tables:
                        sp.dma_start(cols[k][:], a[k].rearrange("(p t) -> p t", p=EP)).then_inc(s_l, 16)
                    for c in range(5):
                        if c:
                            sp.wait_ge(s_k, c)
                        sp.dma_start(raw[:], a["dst"][c * PIECE:(c + 1) * PIECE].rearrange("(a n) -> a n", a=1).to_broadcast([EP, PIECE]))\
                          .then_inc(s_r, 16)
                    with sp.Fori(0, n) as i:
                        sp.wait_ge(s_w, i * 2 + 1)
                        sp.dma_start(ea[:], a["edge_attr_128"].rearrange("(p t) f -> p t f", t=T)[:, bass.ds(i * TILE, TILE), :]).then_inc(s_e, 16)

            @block.vector
            def _(dve):
                with dve.If(unsorted > 0):
                    dve.wait_ge(s_p, 2)
                    dve.wait_ge(s_l, 16 * 3)
                    nc.vector.tensor_copy(kcol[:], cols["dst"][:])
                    for c in range(5):
                        dve.wait_ge(s_r, 16 * (c + 1))
                        nc.vector.tensor_copy(keys[:, c * PIECE:(c + 1) * PIECE], raw[:]).then_inc(s_k, 1)
                    dve.wait_ge(s_k, 5)
                    by_column = keys[:].rearrange("q (p t) -> q p t", t=T)
                    with dve.Fori(0, T) as t:
                        tc = bass.ds(t, 1)
                        own = by_column[:, :, tc].rearrange("q p o -> q (p o)")
                        for c in range(5):
                            nc.vector.tensor_scalar(less[:], keys[:, c * PIECE:(c + 1) * PIECE], kcol[:, tc], None, ALU.is_lt, ALU.add,
                                                    accum_out=part[:, c:c + 1]).then_inc(s_q, 1)
                            dve.wait_ge(s_q, t * 8 + c + 1)
                        nc.vector.scalar_tensor_tensor(less[:, 0:EP], own, kcol[:, tc], earlier[:], ALU.is_equal, ALU.mult,
                                                       accum_out=part[:, 5:6]).then_inc(s_q, 1)
                        dve.wait_ge(s_q, t * 8 + 6)
                        nc.vector.tensor_reduce(rank[:, tc], part[:], op=ALU.add, axis=AX.X).then_inc(s_q, 1)
                        nc.vector.tensor_scalar(own, own, -0.5, None, ALU.add).then_inc(s_q, 1)
                        dve.wait_ge(s_q, t * 8 + 8)
                    nc.vector.tensor_copy(rank_i[:], rank[:]).then_inc(s_a, 1)

            @block.gpsimd
            def _(pool):
                with pool.If(unsorted > 0):
                    nc.gpsimd.memset(earlier[:], 1.0).then_inc(s_p, 1)
                    pool.wait_ge(s_p, 1)
                    nc.gpsimd.affine_select(out=earlier[:], in_=earlier[:], compare_op=ALU.is_gt, fill=0.0, base=0,
                                            pattern=[[-1, EP]], channel_multiplier=1).then_inc(s_p, 1)
                    pool.wait_ge(s_a, 1)
                    with pool.Fori(0, n) as i:
                        nc.gpsimd.memset(idx[:], 0).then_inc(s_w, 1)
                        m.hold(pool, s_w, i * 2 + 1)
                        nc.gpsimd.tensor_copy(idx[:], rank_i[:, bass.ds(i * TILE, TILE)]).then_inc(s_a, 1)
                        for k in tables:
                            nc.gpsimd.tensor_copy(word[k][:], cols[k][:, bass.ds(i * TILE, TILE)]).then_inc(s_a, 1)
                        m.hold(pool, s_a, i * 4 + 5)
                        m.hold(pool, s_e, i * 16 + 16)
                        for c in range(TILE):
                            to = bass.IndirectOffsetOnAxis(ap=idx[:, c:c + 1], axis=0)
                            for k, table in tables.items():
                                pool.indirect_dma_start(out=table, out_offset=to, in_=word[k][:, c:c + 1], in_offset=None).then_inc(s_o, 16)
                            pool.indirect_dma_start(out=m.edge["ea"], out_offset=to, in_=ea[:, c, :], in_offset=None).then_inc(s_o, 16)
                        m.hold(pool, s_o, i * 256 + 256)
                        nc.gpsimd.memset(idx[:], 0).then_inc(s_w, 1)
                        m.hold(pool, s_w, i * 2 + 2)


def edges_setup(nc, m, a):
    N, E = m.N, m.E
    T = E // EP
    TC = T // 2
    NH = -(-N // 128)
    NH2 = NH // 2 if NH % 2 == 0 else (NH + 1) // 2
    BIG = float(1 << 22)
    m.T, m.TC, m.NH = T, TC, NH
    m.kext = m.sb("dst_keys", [128, T])
    m.inv_d = m.sb("inverse_degree_dst", [128, T])
    m.inv_s = m.sb("inverse_degree_src", [128, T])
    m.ind = m.sb("first_last_indicators", [128, T, 2])
    m.M1 = [m.sb(f"earlier_tiles{c}", [TC, T]) for c in range(2)]
    m.M2 = [m.sb(f"later_tiles{c}", [TC, T]) for c in range(2)]
    m.csrc = m.sb("src_keys", [EP, T])
    m.i_src = m.sb("i_src", [EP, T], I32)
    m.i_dst = m.sb("i_dst", [EP, T], I32)
    m.i_src2 = m.sb("i_src2", [EP, T], I32)
    m.i_dst2f = m.sb("i_dst2f", [EP, T], I32)
    m.i_dst2f1 = m.sb("i_dst2f1", [EP, T], I32)
    m.i_dstf = m.sb("i_dstf", [EP, T], I32)
    m.i_tb = m.sb("i_tb", [EP, T], I32)
    m.i_src2f1 = m.sb("i_src2f1", [EP, T], I32)
    m.i_srcf = m.sb("i_srcf", [EP, T], I32)
    m.VT = nc.dram_tensor("values", [T * 128, D], F32, kind="Internal").ap()
    m.XD = nc.dram_tensor("x_of_dst", [E, D], F32, kind="Internal").ap()
    m.H1 = nc.dram_tensor("h1_of_dst", [E, D], F32, kind="Internal").ap()
    m.LT = nc.dram_tensor("leaving_values", [E, D], F32, kind="Internal").ap()
    m.TB1 = nc.dram_tensor("layer1_rows", [2 * E, D], F32, kind="Internal").ap()
    m.TB2 = nc.dram_tensor("layer2_rows", [2 * E, D], F32, kind="Internal").ap()
    m.HDa = nc.dram_tensor("hidden_a", [T // TILE * 128, EG], F32, kind="Internal").ap()
    m.HDb = nc.dram_tensor("hidden_b", [T // TILE * 128, EG], F32, kind="Internal").ap()
    m.KD = nc.dram_tensor("keys_dst", [T, EP], F32, kind="Internal").ap()
    m.KS = nc.dram_tensor("keys_src", [T, EP], F32, kind="Internal").ap()
    m.KT = nc.dram_tensor("keys_type", [T, EP], F32, kind="Internal").ap()
    POS = nc.dram_tensor("position_of_node", [NH * 128, 1], I32, kind="Internal").ap()
    INVS = nc.dram_tensor("inverse_degree_table", [128 * NH, 1], F32, kind="Internal").ap()

    keep = ExitStack()

    def sb(name, shape, dt=F32):
        return keep.enter_context(nc.sbuf_tensor("es_" + name, shape, dt))

    ri = [[sb(f"r_{k}{c}", [TC, EP], I32) for c in range(2)] for k in ("dst", "src", "typ", "prev")]
    rf = [[sb(f"f_{k}{c}", [TC, EP]) for c in range(2)] for k in ("dst", "src", "typ", "prev")]
    notfirst = [sb(f"notfirst{c}", [TC, EP]) for c in range(2)]
    corr = [sb(f"corr{c}", [TC, EP]) for c in range(2)]
    corr2 = [sb(f"corrb{c}", [TC, EP]) for c in range(2)]
    ish = [sb(f"ish{c}", [TC, EP]) for c in range(2)]
    ist = [sb(f"ist{c}", [TC, EP]) for c in range(2)]
    hcnt = [sb(f"hcnt{c}", [TC, 1]) for c in range(2)]
    lcnt = [sb(f"lcnt{c}", [TC, 1]) for c in range(2)]
    pq = [sb(f"pq{c}", [TC, 2]) for c in range(2)]
    headT = [sb(f"head{c}", [TC, TC]) for c in range(2)]
    tailT = [sb(f"tail{c}", [TC, TC]) for c in range(2)]
    cdst, cnf, ccorr = (sb(k, [EP, T]) for k in ("cdst", "cnf", "ccorr"))
    csrc = m.csrc
    within, total = sb("within", [EP, T]), sb("total", [EP, T])
    t1, t2, t3 = (sb(k, [EP, T]) for k in ("t1", "t2", "t3"))
    posf, epos = sb("posf", [EP, T]), sb("epos", [EP, T])
    poscol, tb = sb("poscol", [EP, T], I32), sb("tb", [EP, T], I32)
    minus = sb("minus", [128, NH], I32)
    lo_i, hi_i = sb("lo_i", [EP, T], I32), sb("hi_i", [EP, T], I32)
    lo_f, hi_f = sb("lo_f", [EP, T]), sb("hi_f", [EP, T])
    i_hist = sb("i_hist", [EP, T], I32)
    io_lo, io_hi = sb("io_lo", [128, 128]), sb("io_hi", [128, NH2 * 2])
    before = sb("before", [EP, TILE, EG])
    krow = [sb(f"krow{k}", [128, EG]) for k in range(4)]
    srow = [sb(f"srow{k}", [128, EG]) for k in range(4)]
    oh_lo = [sb(f"oh_lo{k}", [EP, TILE, 128], BF16) for k in range(2)]
    oh_hi = [sb(f"oh_hi{k}", [EP, TILE, NH2 * 2], BF16) for k in range(2)]
    scr = sb("scr", [128, EG])
    scr2 = [sb(f"scr2_{k}", [128, EG]) for k in range(2)]
    seen = sb("seen", [EP, T])
    hist = sb("hist", [128, NH])
    histm = sb("histm", [128, NH])
    n = T // TILE

    s_ld = m.sem("es_ld")
    s_p, s_v, s_t, s_st = m.sem("es_pool"), m.sem("es_dve"), m.sem("es_pe"), m.sem("es_out")
    s_ms = m.sem("es_minus")
    V_MASKS = 30
    ccr = [sb(f"ccr{c}", [TC, EP]) for c in range(2)]
    c_pos = [sb(f"c_pos{k}", [EP, TILE], I32) for k in range(4)]
    with nc.Block() as block:
        @block.sync
        def _(sp):
            for c in range(2):
                for k, name in enumerate(("dst", "src", "edge_type_9")):
                    sp.dma_start(ri[k][c][:], m.edge[name].rearrange("(t p) -> t p", p=EP)[c * TC:(c + 1) * TC, :]).then_inc(s_ld, 16)
            sp.wait_ge(s_p, 1)
            flat = m.edge["dst"]
            sp.dma_start(ri[3][0][0:1, 1:EP], flat[0:EP - 1].rearrange("(a n) -> a n", a=1)).then_inc(s_ld, 16)
            sp.dma_start(ri[3][0][1:TC, :], flat[EP - 1:EP - 1 + (TC - 1) * EP].rearrange("(t p) -> t p", p=EP)).then_inc(s_ld, 16)
            sp.dma_start(ri[3][1][:, :], flat[TC * EP - 1:TC * EP - 1 + TC * EP].rearrange("(t p) -> t p", p=EP)).then_inc(s_ld, 16)
            sp.wait_ge(s_v, 8)
            for c in range(2):
                for k, table in ((0, m.KD), (1, m.KS), (2, m.KT)):
                    sp.dma_start(table[c * TC:(c + 1) * TC, :], rf[k][c][:]).then_inc(s_st, 16)
            sp.wait_ge(s_ms, 1)
            sp.dma_start(POS.rearrange("(p a) o -> p (a o)", p=128), minus[:]).then_inc(s_st, 16)
            sp.wait_ge(s_st, 16 * 7)

        @block.gpsimd
        def _(pool):
            nc.gpsimd.memset(ri[3][0][0:1, :], -1).then_inc(s_p, 1)
            nc.gpsimd.memset(minus[:], -1).then_inc(s_ms, 1)
            nc.gpsimd.iota(posf[:], [[EP, T]], base=0, channel_multiplier=1, allow_small_or_imprecise_dtypes=True).then_inc(s_p, 1)
            nc.gpsimd.iota(poscol[:], [[EP, T]], base=0, channel_multiplier=1).then_inc(s_p, 1)
            nc.gpsimd.iota(epos[:], [[EP, T]], base=E, channel_multiplier=1, allow_small_or_imprecise_dtypes=True).then_inc(s_p, 1)
            nc.gpsimd.iota(io_lo[:], [[1, 128]], base=0, channel_multiplier=0, allow_small_or_imprecise_dtypes=True).then_inc(s_p, 1)
            nc.gpsimd.iota(io_hi[:], [[1, NH2 * 2]], base=0, channel_multiplier=0, allow_small_or_imprecise_dtypes=True).then_inc(s_p, 1)
            nc.gpsimd.memset(before[:], 1.0).then_inc(s_p, 1)
            nc.gpsimd.memset(m.kext[:], -5.0).then_inc(s_p, 1)
            nc.gpsimd.memset(m.inv_d[:], 0.0).then_inc(s_p, 1)
            nc.gpsimd.memset(m.ind[:], 0.0).then_inc(s_p, 1)
            pool.wait_ge(s_p, 10)
            for c in range(TILE):
                nc.gpsimd.affine_select(out=before[:, c, :], in_=before[:, c, :], compare_op=ALU.is_gt, fill=0.0,
                                        base=c * EP, pattern=[[-1, EG]], channel_multiplier=1).then_inc(s_p, 1)
            pool.wait_ge(s_v, V_MASKS)
            for c in range(2):
                nc.gpsimd.affine_select(out=m.M1[c][:], in_=m.M1[c][:], compare_op=ALU.is_gt, fill=0.0,
                                        base=-c * TC, pattern=[[1, T]], channel_multiplier=-1).then_inc(s_p, 1)
                nc.gpsimd.affine_select(out=m.M2[c][:], in_=m.M2[c][:], compare_op=ALU.is_gt, fill=0.0,
                                        base=c * TC, pattern=[[-1, T]], channel_multiplier=1).then_inc(s_p, 1)

        @block.vector
        def _(dve):
            dve.wait_ge(s_ld, 16 * 9)
            for k in range(4):
                for c in range(2):
                    if k == 2:
                        nc.vector.tensor_scalar(rf[k][c][:], ri[k][c][:], 0.0, 8.0, ALU.max, ALU.min).then_inc(s_v, 1)
                    else:
                        nc.vector.tensor_copy(rf[k][c][:], ri[k][c][:]).then_inc(s_v, 1)
            dve.wait_ge(s_v, 8)
            for c in range(2):
                nc.vector.tensor_tensor(notfirst[c][:], rf[0][c][:], rf[3][c][:], ALU.is_equal).then_inc(s_v, 1)
                nc.vector.tensor_scalar(ish[c][:], rf[0][c][:], rf[0][c][:, 0:1], None, ALU.is_equal).then_inc(s_v, 1)
                nc.vector.tensor_scalar(ist[c][:], rf[0][c][:], rf[0][c][:, EP - 1:EP], None, ALU.is_equal).then_inc(s_v, 1)
                dve.wait_ge(s_v, 8 + 5 * c + 3)
                nc.vector.tensor_reduce(hcnt[c][:], ish[c][:], op=ALU.add, axis=AX.X).then_inc(s_v, 1)
                nc.vector.tensor_reduce(lcnt[c][:], ist[c][:], op=ALU.add, axis=AX.X).then_inc(s_v, 1)
            dve.wait_ge(s_t, 4)
            for c in range(2):
                nc.vector.tensor_copy(headT[c][:], m.bank[c][0:TC, 0:TC]).then_inc(s_v, 1)
                nc.vector.tensor_copy(tailT[c][:], m.bank[2 + c][0:TC, 0:TC]).then_inc(s_v, 1)
            dve.wait_ge(s_v, 22)
            for c in range(2):
                for d in range(2):
                    nc.vector.tensor_scalar(m.M1[c][:, d * TC:(d + 1) * TC], headT[d][:], rf[0][c][:, EP - 1:EP], None, ALU.is_equal).then_inc(s_v, 1)
                    nc.vector.tensor_scalar(m.M2[c][:, d * TC:(d + 1) * TC], tailT[d][:], rf[0][c][:, 0:1], None, ALU.is_equal).then_inc(s_v, 1)
            dve.wait_ge(s_t, 6)
            for c in range(2):
                nc.vector.tensor_copy(pq[c][:], m.bank[4 + c][0:TC, 0:2]).then_inc(s_v, 1)
            dve.wait_ge(s_v, 32)
            for c in range(2):
                nc.vector.tensor_scalar(corr[c][:], ish[c][:], pq[c][:, 0:1], None, ALU.mult).then_inc(s_v, 1)
                nc.vector.tensor_scalar(corr2[c][:], ist[c][:], pq[c][:, 1:2], None, ALU.mult).then_inc(s_v, 1)
            dve.wait_ge(s_v, 36)
            for c in range(2):
                nc.vector.tensor_tensor(ccr[c][:], corr[c][:], corr2[c][:], ALU.add).then_inc(s_v, 1)
            dve.wait_ge(s_t, 7)
            b = m.bank[0]
            cols = (cdst, csrc, cnf, ccorr)
            for k in range(4):
                nc.vector.tensor_copy(cols[k][:], m.bank[k][0:EP, 0:T]).then_inc(s_v, 1)
            dve.wait_ge(s_p, 10)
            nc.vector.tensor_copy(m.kext[0:EP, :], m.bank[0][0:EP, 0:T]).then_inc(s_v, 1)
            for k in range(2):
                nc.vector.tensor_copy(m.ind[0:EP, :, k], m.bank[4 + k][0:EP, 0:T]).then_inc(s_v, 1)
            dve.wait_ge(s_v, 45)
            nc.vector.tensor_copy(m.i_src[:], csrc[:]).then_inc(s_v, 1)
            nc.vector.tensor_copy(m.i_dst[:], cdst[:]).then_inc(s_v, 1)
            nc.vector.tensor_scalar(m.i_src2[:], csrc[:], 2.0, None, ALU.mult).then_inc(s_v, 1)
            nc.vector.tensor_scalar(t1[:], cnf[:], BIG, None, ALU.mult).then_inc(s_v, 1)
            dve.wait_ge(s_v, 49)
            nc.vector.tensor_tensor(m.i_dstf[:], cdst[:], t1[:], ALU.add).then_inc(s_v, 1)
            nc.vector.scalar_tensor_tensor(t2[:], cdst[:], 2.0, t1[:], ALU.mult, ALU.add).then_inc(s_v, 1)
            dve.wait_ge(s_v, 51)
            nc.vector.tensor_copy(m.i_dst2f[:], t2[:]).then_inc(s_v, 1)
            nc.vector.tensor_scalar(m.i_dst2f1[:], t2[:], 1.0, None, ALU.add).then_inc(s_v, 1)
            nc.vector.tensor_scalar(hi_i[:], m.i_src[:], 7, None, ALU.logical_shift_right).then_inc(s_v, 1)
            nc.vector.tensor_scalar(lo_i[:], m.i_src[:], 127, None, ALU.bitwise_and).then_inc(s_v, 1)
            dve.wait_ge(s_v, 55)
            nc.vector.tensor_copy(hi_f[:], hi_i[:]).then_inc(s_v, 1)
            nc.vector.tensor_copy(lo_f[:], lo_i[:]).then_inc(s_v, 1)
            dve.wait_ge(s_v, 57)
            nc.vector.scalar_tensor_tensor(i_hist[:], lo_f[:], float(NH), hi_f[:], ALU.mult, ALU.add).then_inc(s_v, 1)

        @block.tensor
        def _(pe):
            pe.wait_ge(s_v, 18)
            for c in range(2):
                nc.tensor.matmul(m.bank[c][0:TC, 0:TC], rf[0][c][:, 0:1].to_broadcast([TC, TC]), m.ident[0:TC, 0:TC],
                                 start=True, stop=True).then_inc(s_t, 1)
                nc.tensor.matmul(m.bank[2 + c][0:TC, 0:TC], rf[0][c][:, EP - 1:EP].to_broadcast([TC, TC]), m.ident[0:TC, 0:TC],
                                 start=True, stop=True).then_inc(s_t, 1)
            pe.wait_ge(s_p, 18)
            for c in range(2):
                cs = slice(c * TC, (c + 1) * TC)
                for k, (mask, cnt) in enumerate(((m.M1, lcnt), (m.M2, hcnt))):
                    nc.tensor.matmul(m.bank[4 + c][0:TC, k:k + 1], mask[0][:, cs], cnt[0][:], start=True, stop=False)
                    last = nc.tensor.matmul(m.bank[4 + c][0:TC, k:k + 1], mask[1][:, cs], cnt[1][:], start=False, stop=True)
                last.then_inc(s_t, 1)
            pe.wait_ge(s_v, 38)
            for k, rows in enumerate((rf[0], rf[1], notfirst, ccr, ish, ist)):
                for c in range(2):
                    last = nc.tensor.transpose(m.bank[k][0:EP, c * TC:(c + 1) * TC], rows[c][:], m.ident[0:TC, 0:TC])
            last.then_inc(s_t, 1)

    s_kr, s_sr = m.sems("es_krow", 4), m.sems("es_srow", 4)
    s_w, s_oh, s_hm, s_pos, s_tbl = m.sem("es_within"), m.sem("es_onehot"), m.sem("es_hist"), m.sem("es_pos"), m.sem("es_tb")
    s_c = m.sem("es_chain")
    c_dst = [sb(f"i_pos{k}", [EP, TILE], I32) for k in range(4)]
    s_pi, s_pg, s_pd = m.sem("es_pi"), m.sems("es_pg", 4), m.sem("es_pd")
    with nc.Block() as block:
        @block.sync
        def _(sp):
            def body(i, u, has):
                f = Flow(sp, has)
                f.after(s_w, i - 4)
                kd = m.KD.rearrange("t p -> (t p)")[bass.ds(i * EG, EG)].rearrange("(a n) -> a n", a=1)
                ks = m.KS.rearrange("t p -> (t p)")[bass.ds(i * EG, EG)].rearrange("(a n) -> a n", a=1)
                sp.dma_start(krow[u][:], kd.to_broadcast([128, EG])).then_inc(s_kr[u], 16)
                sp.dma_start(srow[u][:], ks.to_broadcast([128, EG])).then_inc(s_sr[u], 16)

            sweep(sp, 0, n, n - 1, body, back=4, ahead=0, special=0)

        @block.vector
        def _(dve):
            def body(i, u, has):
                f = Flow(dve, has)
                p = u % 2
                f.landed(s_kr, i, u)
                f.landed(s_sr, i, u)
                f.after(s_hm, i - 2)
                for c in range(TILE):
                    nc.vector.tensor_scalar(scr2[0][0:EP, 0:EP], krow[u][0:EP, c * EP:(c + 1) * EP], m.kext[0:EP, bass.ds(i * 4 + c, 1)], None,
                                            ALU.is_equal, ALU.add, accum_out=within[:, bass.ds(i * 4 + c, 1)]).then_inc(s_c, 1)
                    nc.vector.scalar_tensor_tensor(scr[0:EP, :], srow[u][0:EP, :], csrc[:, bass.ds(i * 4 + c, 1)], before[:, c, :],
                                                   ALU.is_equal, ALU.mult, accum_out=seen[:, bass.ds(i * 4 + c, 1)]).then_inc(s_c, 1)
                    nc.vector.tensor_scalar(oh_lo[p][:, c, :], io_lo[0:EP, :], lo_f[:, bass.ds(i * 4 + c, 1)], None, ALU.is_equal)
                    last = nc.vector.tensor_scalar(oh_hi[p][:, c, :], io_hi[0:EP, :], hi_f[:, bass.ds(i * 4 + c, 1)], None, ALU.is_equal)
                    dve.wait_ge(s_c, i * 8 + 2 * c + 2)
                last.then_inc(s_oh, 1)
                nc.vector.memset(scr2[1][:, 0:1], 0.0).then_inc(s_w, 1)

            sweep(dve, 0, n, n - 1, body, back=4, ahead=0, special=0)
            dve.wait_ge(s_w, n)
            k0 = 8 * n
            nc.vector.tensor_tensor(total[:], within[:], ccorr[:], ALU.add).then_inc(s_c, 1)
            nc.vector.tensor_scalar(t3[:], seen[:], 0.5, BIG, ALU.is_gt, ALU.mult).then_inc(s_c, 1)
            dve.wait_ge(s_c, k0 + 2)
            nc.vector.reciprocal(m.inv_d[0:EP, :], total[:]).then_inc(s_c, 1)
            nc.vector.tensor_tensor(m.i_srcf[:], csrc[:], t3[:], ALU.add).then_inc(s_c, 1)
            nc.vector.scalar_tensor_tensor(t2[:], csrc[:], 2.0, t3[:], ALU.mult, ALU.add).then_inc(s_c, 1)
            dve.wait_ge(s_c, k0 + 5)
            nc.vector.tensor_scalar(m.i_src2f1[:], t2[:], 1.0, None, ALU.add).then_inc(s_c, 1)
            dve.wait_ge(s_hm, n)
            for h in range(2):
                lo, hi = h * NH2, min((h + 1) * NH2, NH)
                nc.vector.tensor_scalar(hist[:, lo:hi], m.bank[h][:, 0:hi - lo], 1.0, None, ALU.max).then_inc(s_c, 1)
            dve.wait_ge(s_c, k0 + 8)
            nc.vector.reciprocal(histm[:], hist[:]).then_inc(s_c, 1)

        @block.tensor
        def _(pe):
            def body(i, u, has):
                f = Flow(pe, has)
                p = u % 2
                f.after(s_oh, i)
                for c in range(TILE):
                    first = isinstance(i, int) and i == 0 and c == 0
                    end = isinstance(i, int) and i == n - 1 and c == TILE - 1
                    for h in range(2):
                        last = nc.tensor.matmul(m.bank[h][:, 0:NH2], oh_lo[p][:, c, :], oh_hi[p][:, c, h * NH2:(h + 1) * NH2],
                                                start=first, stop=end, skip_group_check=True)
                last.then_inc(s_hm, 1)

            sweep(pe, 0, n, n - 1, body, back=4, ahead=0, special=1)

        @block.gpsimd
        def _(pool):
            def body(i, u, has):
                f = Flow(pool, has, m)
                f.landed(s_pg, i - 4, u, 64)
                nc.gpsimd.tensor_copy(c_dst[u][:], m.i_dstf[:, bass.ds(i * 4, 4)]).then_inc(s_pi, 1)
                f.after(s_pi, i)
                if True:
                    nc.gpsimd.tensor_copy(c_pos[u][:], poscol[:, bass.ds(i * 4, 4)]).then_inc(s_pd, 1)
                    f.after(s_pd, i)
                for c in range(TILE):
                    pool.indirect_dma_start(out=POS, out_offset=bass.IndirectOffsetOnAxis(ap=c_dst[u][:, c:c + 1], axis=0),
                                            in_=c_pos[u][:, c:c + 1], in_offset=None, bounds_check=N - 1, oob_is_err=False)                        .then_inc(s_pg[u], 16)

            sweep(pool, 0, n, n - 1, body, back=4, ahead=0, special=0)
            finish(pool, s_pg, n, 64)

    s_ext, s_lk, s_i2 = m.sem("es_ext"), m.sems("es_lookup", 4), m.sem("es_i2")
    s_f = m.sem("es_final")
    c_h = [sb(f"c_h{k}", [EP, TILE], I32) for k in range(4)]
    g_tb = [sb(f"g_tb{k}", [EP, TILE], I32) for k in range(4)]
    g_iv = [sb(f"g_iv{k}", [EP, TILE]) for k in range(4)]
    s_cp = m.sem("es_cp")
    with nc.Block() as block:
        @block.sync
        def _(sp):
            sp.dma_start(INVS.rearrange("(p a) o -> p (a o)", p=128), histm[:]).then_inc(s_ext, 16)
            for arr in (m.kext, m.inv_d):
                sp.dma_start(arr[EP:EP + 1, :], arr[0:1, :]).then_inc(s_ext, 16)
                sp.dma_start(arr[EP + 1:EP + 2, :], arr[EP - 1:EP, :]).then_inc(s_ext, 16)
            sp.wait_ge(s_ext, 16 * 5)

        @block.gpsimd
        def _(pool):
            pool.wait_ge(s_ext, 16 * 5)

            def body(i, u, has):
                f = Flow(pool, has, m)
                f.landed(s_lk, i - 4, u, 128)
                f.after(s_cp, i - 4)
                nc.gpsimd.tensor_copy(c_dst[u][:], m.i_src[:, bass.ds(i * 4, 4)]).then_inc(s_i2, 1)
                nc.gpsimd.tensor_copy(c_h[u][:], i_hist[:, bass.ds(i * 4, 4)]).then_inc(s_i2, 1)
                f.wait(s_i2, i * 2 + 2)
                for c in range(TILE):
                    pool.indirect_dma_start(out=g_tb[u][:, c:c + 1], out_offset=None, in_=POS,
                                            in_offset=bass.IndirectOffsetOnAxis(ap=c_dst[u][:, c:c + 1], axis=0)).then_inc(s_lk[u], 16)
                    pool.indirect_dma_start(out=g_iv[u][:, c:c + 1], out_offset=None, in_=INVS,
                                            in_offset=bass.IndirectOffsetOnAxis(ap=c_h[u][:, c:c + 1], axis=0)).then_inc(s_lk[u], 16)

            sweep(pool, 0, n, n - 1, body, back=4, ahead=0, special=0)
            finish(pool, s_lk, n, 128)

        @block.vector
        def _(dve):
            def body(i, u, has):
                f = Flow(dve, has)
                f.landed(s_lk, i, u, 128)
                nc.vector.tensor_copy(tb[:, bass.ds(i * 4, 4)], g_tb[u][:])
                nc.vector.tensor_copy(m.inv_s[0:EP, bass.ds(i * 4, 4)], g_iv[u][:]).then_inc(s_cp, 1)

            sweep(dve, 0, n, n - 1, body, back=4, ahead=0, special=0)
            dve.wait_ge(s_cp, n)
            nc.vector.tensor_copy(t1[:], tb[:]).then_inc(s_f, 1)
            dve.wait_ge(s_f, 1)
            nc.vector.tensor_scalar(t2[:], t1[:], -0.5, None, ALU.is_gt).then_inc(s_f, 1)
            nc.vector.tensor_tensor(t3[:], t1[:], epos[:], ALU.subtract).then_inc(s_f, 1)
            dve.wait_ge(s_f, 3)
            nc.vector.tensor_tensor(total[:], t2[:], t3[:], ALU.mult).then_inc(s_f, 1)
            dve.wait_ge(s_f, 4)
            nc.vector.tensor_tensor(m.i_tb[:], total[:], epos[:], ALU.add).then_inc(s_f, 1)
    keep.close()


def gather(nc, pool, f, index, idx, s_idx, i, u, table, rows, landed):
    nc.gpsimd.tensor_copy(idx[u][:], index[:, bass.ds(i * TILE, TILE)]).then_inc(s_idx, 1)
    f.after(s_idx, i)
    for c in range(TILE):
        pool.indirect_dma_start(out=rows[u][0:EP, c, :], out_offset=None, in_=table,
                                in_offset=bass.IndirectOffsetOnAxis(ap=idx[u][:, c:c + 1], axis=0)).then_inc(landed[u], 16)


def scatter(nc, pool, f, index, idx, s_idx, i, u, table, rows, landed, add=False):
    nc.gpsimd.tensor_copy(idx[u][:], index[:, bass.ds(i * TILE, TILE)]).then_inc(s_idx, 1)
    f.after(s_idx, i)
    for c in range(TILE):
        pool.indirect_dma_start(out=table, out_offset=bass.IndirectOffsetOnAxis(ap=idx[u][:, c:c + 1], axis=0),
                                in_=rows[u][0:EP, c, :], in_offset=None, bounds_check=table.shape[0] - 1, oob_is_err=False,
                                **({"compute_op": ALU.add} if add else {})).then_inc(landed[u], 16)


def value_tiles(m, i):
    return m.VT[bass.ds(i * TILE * 128, TILE * 128), :].rearrange("(c p) f -> p c f", p=128)


def turned(table, i):
    return table[bass.ds(i * 128, 128), :]


def first_last_sums(nc, m, V, i):
    for c in range(TILE):
        last = nc.tensor.matmul(m.bank[7][:, bass.ds((i * TILE + c) * 2, 2)], V[0:EP, c, :],
                                m.ind[0:EP, bass.ds(i * TILE + c, 1), :].rearrange("p a k -> p (a k)"),
                                start=True, stop=True, skip_group_check=True)
    return last


def share_segments(nc, m, name):
    TC, T = m.TC, m.T
    with Phase(m, name) as P:
        HL = P.sb("first_last", [128, 2, T])
        X = [[P.sb(f"rows{k}{c}", [TC, D]) for c in range(2)] for k in range(2)]
        R = [[P.sb(f"shared{k}{c}", [TC, D]) for c in range(2)] for k in range(2)]
        s_hl, s_t, s_x, s_m, s_r, s_out = (P.sem(k) for k in ("hl", "turned", "rows", "summed", "shared", "out"))
        with nc.Block() as block:
            @block.vector
            def _(dve):
                nc.vector.tensor_copy(HL[:].rearrange("p k t -> p t k"), m.bank[7][:, 0:2 * T].rearrange("p (t k) -> p t k", k=2))\
                  .then_inc(s_hl, 1)
                for k in range(2):
                    for c in range(2):
                        dve.wait_ge(s_t, 2 * k + c + 1)
                        nc.vector.tensor_copy(X[k][c][:], m.bank[2 * k + c][0:TC, 0:D]).then_inc(s_x, 1)
                for k in range(2):
                    for c in range(2):
                        dve.wait_ge(s_m, 2 * k + c + 1)
                        nc.vector.tensor_copy(R[k][c][:], m.bank[4 * (1 - k) + c][0:TC, 0:D]).then_inc(s_r, 1)

            @block.tensor
            def _(pe):
                pe.wait_ge(s_hl, 1)
                for k in range(2):
                    for c in range(2):
                        nc.tensor.transpose(m.bank[2 * k + c][0:TC, 0:D], HL[:, k, c * TC:(c + 1) * TC], m.ident[:]).then_inc(s_t, 1)
                pe.wait_ge(s_x, 4)
                for k, masks in ((0, m.M1), (1, m.M2)):
                    for c in range(2):
                        for e in range(2):
                            last = nc.tensor.matmul(m.bank[4 * (1 - k) + c][0:TC, 0:D], masks[e][:, c * TC:(c + 1) * TC],
                                                    X[1 - k][e][:], start=(e == 0), stop=(e == 1), skip_group_check=True)
                        last.then_inc(s_m, 1)

            @block.sync
            def _(sp):
                table = m.VT.rearrange("(t p) f -> t p f", p=128)
                for k in range(2):
                    for c in range(2):
                        sp.wait_ge(s_r, 2 * k + c + 1)
                        sp.dma_start(table[c * TC:(c + 1) * TC, EP + k, :], R[k][c][:]).then_inc(s_out, 16)
                sp.wait_ge(s_out, 64)


class Norm:

    def __init__(self, nc, m, P, tiles, name="ln"):
        self.nc, self.m, self.tiles = nc, m, tiles
        self.st = P.slots(name + "_st", [128, tiles, 6])
        self.mv = P.slots(name + "_mv", [128, tiles, 2])
        self.sd = P.slots(name + "_sd", [128, tiles])
        self.rs = P.slots(name + "_rs", [128, tiles])
        self.nb = P.slots(name + "_nb", [128, tiles])
        self.s_st, self.s_mv, self.s_sd, self.s_rs, self.s_nb = (P.sem(f"{name}_{k}") for k in ("st", "mv", "sd", "rs", "nb"))

    def stats(self, dve, f, i, v, rows, np_=EP):
        nc = self.nc
        for j, r in enumerate(rows):
            last = nc.vector.bn_stats(self.st[v][0:np_, j, :], r)
        last.then_inc(self.s_st, 1)
        Flow(dve, f.has, self.m).after(self.s_st, i)
        for j in range(self.tiles):
            last = nc.vector.bn_aggr(self.mv[v][0:np_, j, :], self.st[v][0:np_, j, :])
        last.then_inc(self.s_mv, 1)

    def root(self, f, i, v, np_=EP):
        f.after(self.s_mv, i)
        self.nc.scalar.activation(self.sd[v][0:np_, :], self.mv[v][0:np_, :, 1], ACT.Sqrt, bias=self.m.col["eps"][0:np_, :])\
            .then_inc(self.s_sd, 1)

    def finish(self, f, i, v, np_=EP):
        nc = self.nc
        f.after(self.s_sd, i)
        nc.vector.reciprocal(self.rs[v][0:np_, :], self.sd[v][0:np_, :]).then_inc(self.s_rs, 1)
        f.after(self.s_rs, i)
        nc.vector.scalar_tensor_tensor(self.nb[v][0:np_, :], self.mv[v][0:np_, :, 0], -1.0, self.rs[v][0:np_, :], ALU.mult, ALU.mult)\
            .then_inc(self.s_nb, 1)

    def relu(self, out, rows, v, first=0, np_=EP):
        for j, r in enumerate(rows):
            k = first + j
            last = self.nc.scalar.activation(out[0:np_, j, :], r, ACT.Relu, scale=self.rs[v][0:np_, k:k + 1],
                                             bias=self.nb[v][0:np_, k:k + 1])
        return last


def edges_start(nc, m, a):
    n, E = m.T // TILE, m.E
    with Phase(m, "A") as P:
        idx_s, idx_d = P.slots("idx_s", [EP, TILE], I32), P.slots("idx_d", [EP, TILE], I32)
        xs, xd = P.slots("x_src", [EP, TILE, D]), P.slots("x_dst", [EP, TILE, D])
        hs, hd = P.slots("h_src", [EP, TILE, D]), P.slots("h_dst", [EP, TILE, D])
        hsT, hdT = P.slots("h_srcT", [128, EG]), P.slots("h_dstT", [128, EG])
        a1T, a2T = P.slots("a1T", [128, EG]), P.slots("a2T", [128, EG])
        a1, a2 = P.slots("a1", [EP, TILE, D]), P.slots("a2", [EP, TILE, D])
        ln = Norm(nc, m, P, 2 * TILE)
        s_is, s_id, s_gs, s_gd = P.sem("idx_s"), P.sem("idx_d"), P.sems("got_src"), P.sems("got_dst")
        s_xo, s_vo, s_ho, s_1o, s_2o = (P.sems(k) for k in ("xd_out", "v_out", "hd_out", "a1_out", "a2_out"))
        s_h, s_T, s_hsT, s_hdT, s_hl = (P.sem(k) for k in ("h", "T", "hsT", "hdT", "firstlast"))
        s_m1, s_a1T, s_m2, s_a2T, s_b1, s_a1, s_b2, s_a2 = (P.sem(k) for k in ("m1", "a1T", "m2", "a2T", "b1", "a1", "b2", "a2"))
        bS, bD, b1, b2, r1, r2 = m.bank[0:6]
        with nc.Block() as block:
            @block.gpsimd
            def _(pool):
                def body(i, u, has):
                    f = Flow(pool, has, m)
                    f.after(s_h, i - 4)
                    f.landed(s_xo, i - 4, u)
                    gather(nc, pool, f, m.i_src, idx_s, s_is, i, u, a["x"], xs, s_gs)
                    gather(nc, pool, f, m.i_dst, idx_d, s_id, i, u, a["x"], xd, s_gd)

                sweep(pool, 0, n, n - 1, body, back=4, ahead=0, special=0)

            @block.sync
            def _(sp):
                def body(i, u, has):
                    f = Flow(sp, has)
                    if has(i):
                        f.landed(s_gd, i, u, 64)
                        sp.dma_start(edge_rows(m.XD, i), xd[u][:]).then_inc(s_xo[u], 16)
                    if has(i - 1):
                        v = (u - 1) % 4
                        f.after(s_h, i - 1)
                        sp.dma_start(value_tiles(m, i - 1)[0:EP], hs[v][:]).then_inc(s_vo[v], 16)
                    if has(i - 2):
                        v = (u - 2) % 4
                        f.after(s_hdT, i - 2)
                        sp.dma_start(turned(m.HDa, i - 2), hdT[v][:]).then_inc(s_ho[v], 16)
                    if has(i - 4):
                        v = u
                        f.after(s_a1, i - 4)
                        sp.dma_start(edge_rows(m.TB1[E:2 * E, :], i - 4), a1[v][:]).then_inc(s_1o[v], 16)
                    if has(i - 5):
                        v = (u - 5) % 4
                        f.after(s_a2, i - 5)
                        sp.dma_start(edge_rows(m.TB2[E:2 * E, :], i - 5), a2[v][:]).then_inc(s_2o[v], 16)

                sweep(sp, 0, n, n + 4, body, back=5, ahead=0, special=0)
                for sems in (s_xo, s_vo, s_ho, s_1o, s_2o):
                    finish(sp, sems, n)

            @block.vector
            def _(dve):
                def body(i, u, has):
                    f = Flow(dve, has)
                    if has(i):
                        f.landed(s_gs, i, u, 64)
                        f.landed(s_gd, i, u, 64)
                        ln.stats(dve, f, i, u, [t[u][:, c, :] for t in (xs, xd) for c in range(TILE)])
                    if has(i - 1):
                        ln.finish(f, i - 1, (u - 1) % 4)
                    if has(i - 2):
                        v = (u - 2) % 4
                        f.after(s_T, i - 2)
                        f.landed(s_ho, i - 6, v)
                        nc.vector.tensor_copy(hdT[v][:], bD[:, 0:EG]).then_inc(s_hdT, 1)
                    if has(i - 4):
                        f.after(s_b1, i - 4)
                        f.landed(s_1o, i - 8, u)
                        nc.vector.tensor_copy(a1[u][:], r1[0:EP, :].rearrange("p (c f) -> p c f", c=TILE)).then_inc(s_a1, 1)
                    if has(i - 5):
                        v = (u - 5) % 4
                        f.after(s_b2, i - 5)
                        f.landed(s_2o, i - 9, v)
                        nc.vector.tensor_copy(a2[v][:], r2[0:EP, :].rearrange("p (c f) -> p c f", c=TILE)).then_inc(s_a2, 1)

                sweep(dve, 0, n, n + 4, body, back=9, ahead=0, special=0)

            @block.scalar
            def _(act):
                def body(i, u, has):
                    f = Flow(act, has)
                    if has(i):
                        ln.root(f, i, u)
                    if has(i - 1):
                        v = (u - 1) % 4
                        f.after(ln.s_nb, i - 1)
                        f.after(s_T, i - 5)
                        f.after(s_hl, i - 5)
                        f.landed(s_vo, i - 5, v)
                        ln.relu(hs[v], [xs[v][:, c, :] for c in range(TILE)], v)
                        ln.relu(hd[v], [xd[v][:, c, :] for c in range(TILE)], v, TILE).then_inc(s_h, 1)
                    if has(i - 2):
                        v = (u - 2) % 4
                        f.after(s_T, i - 2)
                        f.after(s_m1, i - 6)
                        nc.scalar.activation(hsT[v][:], bS[:, 0:EG], ACT.Copy).then_inc(s_hsT, 1)
                    if has(i - 3):
                        v = (u - 3) % 4
                        f.after(s_m1, i - 3)
                        f.after(s_b1, i - 7)
                        nc.scalar.activation(a1T[v][:], b1[:, 0:EG], ACT.Relu, bias=m.col["b1"]).then_inc(s_a1T, 1)
                    if has(i - 4):
                        f.after(s_m2, i - 4)
                        f.after(s_b2, i - 8)
                        nc.scalar.activation(a2T[u][:], b2[:, 0:EG], ACT.Relu, bias=m.col["b2"]).then_inc(s_a2T, 1)

                sweep(act, 0, n, n + 3, body, back=8, ahead=0, special=0)

            @block.tensor
            def _(pe):
                def body(i, u, has):
                    f = Flow(pe, has)
                    if has(i - 4):
                        f.after(s_a1T, i - 4)
                        f.after(s_a2T, i - 5)
                        nc.tensor.matmul(b2[:, 0:EG], m.w["self2"], a1T[u][:], start=True, stop=True).then_inc(s_m2, 1)
                    if has(i - 3):
                        f.after(s_hsT, i - 3)
                        f.after(s_a1T, i - 4)
                        nc.tensor.matmul(b1[:, 0:EG], m.w["self1"], hsT[(u - 3) % 4][:], start=True, stop=True).then_inc(s_m1, 1)
                    if has(i - 2):
                        v = (u - 2) % 4
                        f.after(s_h, i - 2)
                        f.after(s_hsT, i - 3)
                        f.after(s_hdT, i - 3)
                        first_last_sums(nc, m, hs[v], i - 2).then_inc(s_hl, 1)
                        for c in range(TILE):
                            nc.tensor.transpose(bS[:, c * EP:(c + 1) * EP], hs[v][:, c, :], m.ident[0:EP, 0:EP])
                            last = nc.tensor.transpose(bD[:, c * EP:(c + 1) * EP], hd[v][:, c, :], m.ident[0:EP, 0:EP])
                        last.then_inc(s_T, 1)
                    if has(i - 4):
                        f.after(s_a1, i - 5)
                        for c in range(TILE):
                            last = nc.tensor.transpose(r1[0:EP, c * D:(c + 1) * D], a1T[u][:, c * EP:(c + 1) * EP], m.ident[:])
                        last.then_inc(s_b1, 1)
                    if has(i - 5):
                        f.after(s_a2T, i - 5)
                        f.after(s_a2, i - 6)
                        for c in range(TILE):
                            last = nc.tensor.transpose(r2[0:EP, c * D:(c + 1) * D], a2T[(u - 5) % 4][:, c * EP:(c + 1) * EP], m.ident[:])
                        last.then_inc(s_b2, 1)

                sweep(pe, 0, n, n + 4, body, back=6, ahead=0, special=0)
    share_segments(nc, m, "A_shared")


def sum_loads(sp, m, f, i, u, V, krow, s_V, s_k, s_sel, s_agg):
    f.after(s_agg, i - 4)
    sp.dma_start(V[u][:], value_tiles(m, i)[0:EP + 2]).then_inc(s_V[u], 16)
    f.after(s_sel, i - 4)
    keys = m.KD.rearrange("t p -> (t p)")[bass.ds(i * EG, EG)].rearrange("(a n) -> a n", a=1)
    sp.dma_start(krow[u][:], keys.to_broadcast([EP + 2, EG])).then_inc(s_k[u], 16)


def selectors(nc, m, f, i, u, krow, S, s_k, s_sel, s_agg, mean=True):
    f.landed(s_k, i, u)
    f.after(s_agg, i - 4)
    for c in range(TILE):
        t = bass.ds(i * TILE + c, 1)
        cs = slice(c * EP, (c + 1) * EP)
        if mean:
            last = nc.vector.tensor_scalar(S[u][:, cs], krow[u][:, cs], m.kext[0:EP + 2, t], m.inv_d[0:EP + 2, t], ALU.is_equal, ALU.mult)
        else:
            last = nc.vector.tensor_scalar(S[u][:, cs], krow[u][:, cs], m.kext[0:EP + 2, t], None, ALU.is_equal)
    last.then_inc(s_sel, 1)


def add_up(nc, m, f, i, u, V, S, bank, s_V, s_sel, s_agg):
    f.landed(s_V, i, u)
    f.after(s_sel, i)
    for c in range(TILE):
        cs = slice(c * EP, (c + 1) * EP)
        last = nc.tensor.matmul(bank[:, cs], V[u][:, c, :], S[u][:, cs], start=True, stop=True)
    last.then_inc(s_agg, 1)


def layer(nc, m, k, H_in, H_out, table):
    n = m.T // TILE
    with Phase(m, f"B{k}") as P:
        V, krow, S = P.slots("V", [EP + 2, TILE, D]), P.slots("krow", [EP + 2, EG]), P.slots("S", [EP + 2, EG])
        h, agg, o, rows = P.slots("h", [128, EG]), P.slots("agg", [128, EG]), P.slots("o", [128, EG]), P.slots("rows", [EP, TILE, D])
        s_V, s_k, s_h, s_oo, s_ro = (P.sems(x) for x in ("V", "k", "h", "o_out", "rows_out"))
        s_sel, s_agg, s_ac, s_m, s_o, s_T, s_r = (P.sem(x) for x in ("sel", "agg", "aggcopy", "m", "o", "T", "r"))
        with nc.Block() as block:
            @block.sync
            def _(sp):
                def load(f, i, u):
                    sum_loads(sp, m, f, i, u, V, krow, s_V, s_k, s_sel, s_agg)
                    f.after(s_m, i - 4)
                    sp.dma_start(h[u][:], turned(H_in, i)).then_inc(s_h[u], 16)

                def body(i, u, has):
                    f = Flow(sp, has)
                    if has(i + 3):
                        load(f, i + 3, (u + 3) % 4)
                    if has(i - 3):
                        v = (u - 3) % 4
                        f.after(s_o, i - 3)
                        sp.dma_start(turned(H_out, i - 3), o[v][:]).then_inc(s_oo[v], 16)
                        f.after(s_r, i - 3)
                        sp.dma_start(edge_rows(table, i - 3), rows[v][:]).then_inc(s_ro[v], 16)

                sweep(sp, -3, n, n + 2, body, back=4, ahead=3, special=0)
                finish(sp, s_oo, n)
                finish(sp, s_ro, n)

            @block.vector
            def _(dve):
                def body(i, u, has):
                    f = Flow(dve, has)
                    if has(i + 1):
                        selectors(nc, m, f, i + 1, (u + 1) % 4, krow, S, s_k, s_sel, s_agg)
                    if has(i - 2):
                        v = (u - 2) % 4
                        f.after(s_T, i - 2)
                        f.landed(s_ro, i - 6, v)
                        nc.vector.tensor_copy(rows[v][:], m.bank[4 + v % 2][0:EP, :].rearrange("p (c f) -> p c f", c=TILE)).then_inc(s_r, 1)

                sweep(dve, -1, n, n + 1, body, back=6, ahead=1, special=0)

            @block.scalar
            def _(act):
                def body(i, u, has):
                    f = Flow(act, has)
                    if has(i):
                        f.after(s_agg, i)
                        f.after(s_m, i - 4)
                        nc.scalar.activation(agg[u][:], m.bank[u % 2][:, 0:EG], ACT.Copy).then_inc(s_ac, 1)
                    if has(i - 1):
                        v = (u - 1) % 4
                        f.after(s_m, i - 1)
                        f.after(s_T, i - 5)
                        f.landed(s_oo, i - 5, v)
                        nc.scalar.activation(o[v][:], m.bank[2 + v % 2][:, 0:EG], ACT.Relu, bias=m.col[f"b{k}"]).then_inc(s_o, 1)

                sweep(act, 0, n, n, body, back=5, ahead=0, special=0)

            @block.tensor
            def _(pe):
                def body(i, u, has):
                    f = Flow(pe, has)
                    if has(i):
                        f.after(s_ac, i - 2)
                        add_up(nc, m, f, i, u, V, S, m.bank[u % 2], s_V, s_sel, s_agg)
                    if has(i - 1):
                        v = (u - 1) % 4
                        f.landed(s_h, i - 1, v)
                        f.after(s_ac, i - 1)
                        f.after(s_o, i - 3)
                        nc.tensor.matmul(m.bank[2 + v % 2][:, 0:EG], m.w[f"self{k}"], h[v][:], start=True, stop=False)
                        nc.tensor.matmul(m.bank[2 + v % 2][:, 0:EG], m.w[f"neigh{k}"], agg[v][:], start=False, stop=True).then_inc(s_m, 1)
                    if has(i - 2):
                        v = (u - 2) % 4
                        f.after(s_o, i - 2)
                        f.after(s_r, i - 4)
                        for c in range(TILE):
                            last = nc.tensor.transpose(m.bank[4 + v % 2][0:EP, c * D:(c + 1) * D], o[v][:, c * EP:(c + 1) * EP], m.ident[:])
                        last.then_inc(s_T, 1)

                sweep(pe, 0, n, n + 1, body, back=4, ahead=0, special=0)


def take(nc, m, k, table):
    n = m.T // TILE
    with Phase(m, f"G{k}") as P:
        idx, V = P.slots("idx", [EP, TILE], I32), P.slots("V", [EP, TILE, D])
        s_i, s_g, s_vo, s_hl = P.sem("idx"), P.sems("got"), P.sems("v_out"), P.sem("firstlast")
        with nc.Block() as block:
            @block.gpsimd
            def _(pool):
                def body(i, u, has):
                    f = Flow(pool, has, m)
                    f.landed(s_vo, i - 4, u)
                    f.after(s_hl, i - 4)
                    gather(nc, pool, f, m.i_tb, idx, s_i, i, u, table, V, s_g)

                sweep(pool, 0, n, n - 1, body, back=4, ahead=0, special=0)

            @block.sync
            def _(sp):
                def body(i, u, has):
                    f = Flow(sp, has)
                    f.landed(s_g, i, u, 64)
                    sp.dma_start(value_tiles(m, i)[0:EP], V[u][:]).then_inc(s_vo[u], 16)

                sweep(sp, 0, n, n - 1, body, back=4, ahead=0, special=0)
                finish(sp, s_vo, n)

            @block.tensor
            def _(pe):
                def body(i, u, has):
                    f = Flow(pe, has)
                    f.landed(s_g, i, u, 64)
                    first_last_sums(nc, m, V[u], i).then_inc(s_hl, 1)

                sweep(pe, 0, n, n - 1, body, back=4, ahead=0, special=0)
    share_segments(nc, m, f"G{k}_shared")


def third_layer(nc, m, a):
    n = m.T // TILE
    with Phase(m, "B3") as P:
        V, krow, S = P.slots("V", [EP + 2, TILE, D]), P.slots("krow", [EP + 2, EG]), P.slots("S", [EP + 2, EG])
        h, agg = P.slots("h", [128, EG]), P.slots("agg", [128, EG])
        xd, xb, x1, h1, h1T = (P.slots(x, [EP, TILE, D]) for x in ("xd", "xb", "x1", "h1", "unused"))
        h1T = P.slots("h1T", [128, EG])
        idx = P.slots("idx", [EP, TILE], I32)
        ln = Norm(nc, m, P, TILE)
        s_V, s_k, s_h, s_x, s_ho, s_To, s_sc = (P.sems(x) for x in ("V", "k", "h", "x", "h1_out", "h1T_out", "x1_out"))
        s_sel, s_agg, s_ac, s_m, s_xb, s_x1, s_h1, s_T, s_hT, s_i = \
            (P.sem(x) for x in ("sel", "agg", "aggcopy", "m", "xb", "x1", "h1", "T", "h1T", "idx"))
        with nc.Block() as block:
            @block.sync
            def _(sp):
                def load(f, i, u):
                    sum_loads(sp, m, f, i, u, V, krow, s_V, s_k, s_sel, s_agg)
                    f.after(s_m, i - 4)
                    sp.dma_start(h[u][:], turned(m.HDa, i)).then_inc(s_h[u], 16)
                    f.after(s_xb, i - 4)
                    sp.dma_start(xd[u][:], edge_rows(m.XD, i)).then_inc(s_x[u], 16)

                def body(i, u, has):
                    f = Flow(sp, has)
                    if has(i + 3):
                        load(f, i + 3, (u + 3) % 4)
                    if has(i - 4):
                        f.after(s_h1, i - 4)
                        sp.dma_start(edge_rows(m.H1, i - 4), h1[u][:]).then_inc(s_ho[u], 16)
                    if has(i - 5):
                        v = (u - 5) % 4
                        f.after(s_hT, i - 5)
                        sp.dma_start(turned(m.HDb, i - 5), h1T[v][:]).then_inc(s_To[v], 16)

                sweep(sp, -3, n, n + 4, body, back=5, ahead=3, special=0)
                finish(sp, s_ho, n)
                finish(sp, s_To, n)

            @block.gpsimd
            def _(pool):
                def body(i, u, has):
                    if has(i):
                        f = Flow(pool, has)
                        f.landed(s_x, i, u)
                        f.after(s_x1, i - 4)
                        nc.gpsimd.tensor_tensor(xb[u][:], xd[u][:], m.b3row[0:EP, :].unsqueeze(1).to_broadcast([EP, TILE, D]), ALU.add)\
                          .then_inc(s_xb, 1)
                    if has(i - 3):
                        f = Flow(pool, has, m)
                        f.after(s_x1, i - 3)
                        f.landed(s_sc, i - 7, u + 1, 64)
                        scatter(nc, pool, f, m.i_dst2f, idx, s_i, i - 3, (u - 3) % 4, m.XH, x1, s_sc)

                sweep(pool, 0, n, n + 2, body, back=7, ahead=0, special=0)
                finish(pool, s_sc, n, 64)

            @block.vector
            def _(dve):
                def body(i, u, has):
                    f = Flow(dve, has)
                    if has(i - 1):
                        v = (u - 1) % 4
                        f.after(s_agg, i - 1)
                        f.after(s_m, i - 5)
                        nc.vector.tensor_copy(agg[v][:], m.bank[v % 2][:, 0:EG]).then_inc(s_ac, 1)
                    if has(i + 1):
                        selectors(nc, m, f, i + 1, (u + 1) % 4, krow, S, s_k, s_sel, s_agg)
                    if has(i - 3):
                        ln.finish(f, i - 3, (u - 3) % 4)
                    if has(i - 2):
                        v = (u - 2) % 4
                        f.after(s_m, i - 2)
                        f.after(s_xb, i - 2)
                        f.landed(s_sc, i - 6, v, 64)
                        f.after(s_h1, i - 6)
                        nc.vector.tensor_tensor(x1[v][:], m.bank[2 + v % 2][0:EP, :].rearrange("p (c f) -> p c f", c=TILE), xb[v][:], ALU.add)\
                          .then_inc(s_x1, 1)
                        f.after(s_x1, i - 2)
                        ln.stats(dve, f, i - 2, v, [x1[v][:, c, :] for c in range(TILE)])

                sweep(dve, -1, n, n + 2, body, back=6, ahead=1, special=0)

            @block.scalar
            def _(act):
                def body(i, u, has):
                    f = Flow(act, has)
                    if has(i - 2):
                        ln.root(f, i - 2, (u - 2) % 4)
                    if has(i - 3):
                        v = (u - 3) % 4
                        f.after(ln.s_nb, i - 3)
                        f.after(s_T, i - 7)
                        f.landed(s_ho, i - 7, v)
                        ln.relu(h1[v], [x1[v][:, c, :] for c in range(TILE)], v).then_inc(s_h1, 1)
                    if has(i - 4):
                        f.after(s_T, i - 4)
                        f.landed(s_To, i - 8, u)
                        nc.scalar.activation(h1T[u][:], m.bank[4 + u % 2][:, 0:EG], ACT.Copy).then_inc(s_hT, 1)

                sweep(act, 0, n, n + 3, body, back=8, ahead=0, special=0)

            @block.tensor
            def _(pe):
                def body(i, u, has):
                    f = Flow(pe, has)
                    if has(i):
                        f.after(s_ac, i - 2)
                        add_up(nc, m, f, i, u, V, S, m.bank[u % 2], s_V, s_sel, s_agg)
                    if has(i - 1):
                        v = (u - 1) % 4
                        f.landed(s_h, i - 1, v)
                        f.after(s_ac, i - 1)
                        f.after(s_x1, i - 3)
                        for c in range(TILE):
                            cs, o = slice(c * EP, (c + 1) * EP), m.bank[2 + v % 2][0:EP, c * D:(c + 1) * D]
                            nc.tensor.matmul(o, h[v][:, cs], m.w["self3"], start=True, stop=False)
                            last = nc.tensor.matmul(o, agg[v][:, cs], m.w["neigh3"], start=False, stop=True)
                        last.then_inc(s_m, 1)
                    if has(i - 4):
                        f.after(s_h1, i - 4)
                        f.after(s_hT, i - 6)
                        for c in range(TILE):
                            last = nc.tensor.transpose(m.bank[4 + u % 2][:, c * EP:(c + 1) * EP], h1[u][:, c, :], m.ident[0:EP, 0:EP])
                        last.then_inc(s_T, 1)

                sweep(pe, 0, n, n + 3, body, back=6, ahead=0, special=0)


def incoming(nc, m, a):
    n = m.T // TILE
    with Phase(m, "G3") as P:
        idx, x, h, V, ea = P.slots("idx", [EP, TILE], I32), *(P.slots(k, [EP, TILE, D]) for k in ("x", "h", "V", "ea"))
        ln = Norm(nc, m, P, TILE)
        s_i, s_h, s_v, s_hl = (P.sem(k) for k in ("idx", "h", "v", "firstlast"))
        s_g, s_e, s_vo = (P.sems(k) for k in ("got", "ea", "v_out"))
        with nc.Block() as block:
            @block.gpsimd
            def _(pool):
                def body(i, u, has):
                    f = Flow(pool, has, m)
                    f.after(s_h, i - 4)
                    gather(nc, pool, f, m.i_src2, idx, s_i, i, u, m.XH, x, s_g)

                sweep(pool, 0, n, n - 1, body, back=4, ahead=0, special=0)

            @block.sync
            def _(sp):
                def load(f, i, u):
                    f.after(s_v, i - 4)
                    sp.dma_start(ea[u][:], edge_rows(m.edge["ea"], i)).then_inc(s_e[u], 16)

                def body(i, u, has):
                    f = Flow(sp, has)
                    if has(i + 3):
                        load(f, i + 3, (u + 3) % 4)
                    if has(i - 3):
                        v = (u - 3) % 4
                        f.after(s_v, i - 3)
                        sp.dma_start(value_tiles(m, i - 3)[0:EP], V[v][:]).then_inc(s_vo[v], 16)

                sp.wait_ge(m.s_ea, m.ea_copied)
                sweep(sp, -3, n, n + 2, body, back=4, ahead=3, special=0)
                finish(sp, s_vo, n)

            @block.vector
            def _(dve):
                def body(i, u, has):
                    f = Flow(dve, has)
                    if has(i - 1):
                        ln.finish(f, i - 1, (u - 1) % 4)
                    if has(i):
                        f.landed(s_g, i, u, 64)
                        ln.stats(dve, f, i, u, [x[u][:, c, :] for c in range(TILE)])
                    if has(i - 2):
                        v = (u - 2) % 4
                        f.after(s_h, i - 2)
                        f.landed(s_e, i - 2, v)
                        f.landed(s_vo, i - 6, v)
                        f.after(s_hl, i - 6)
                        nc.vector.tensor_tensor(V[v][:], h[v][:], ea[v][:], ALU.subtract).then_inc(s_v, 1)

                sweep(dve, 0, n, n + 1, body, back=6, ahead=0, special=0)

            @block.scalar
            def _(act):
                def body(i, u, has):
                    f = Flow(act, has)
                    if has(i):
                        ln.root(f, i, u)
                    if has(i - 1):
                        v = (u - 1) % 4
                        f.after(ln.s_nb, i - 1)
                        f.after(s_v, i - 5)
                        ln.relu(h[v], [x[v][:, c, :] for c in range(TILE)], v).then_inc(s_h, 1)

                sweep(act, 0, n, n, body, back=5, ahead=0, special=0)

            @block.tensor
            def _(pe):
                def body(i, u, has):
                    f = Flow(pe, has)
                    f.after(s_v, i)
                    first_last_sums(nc, m, V[u], i).then_inc(s_hl, 1)

                sweep(pe, 0, n, n - 1, body, back=4, ahead=0, special=0)
    share_segments(nc, m, "G3_shared")


def outgoing_self(nc, m, a):
    n = m.T // TILE
    with Phase(m, "B4") as P:
        V, krow, S = P.slots("V", [EP + 2, TILE, D]), P.slots("krow", [EP + 2, EG]), P.slots("S", [EP + 2, EG])
        h, agg, g = P.slots("h", [128, EG]), P.slots("agg", [128, EG]), P.slots("g", [EP, TILE, D])
        idx = P.slots("idx", [EP, TILE], I32)
        s_V, s_k, s_h, s_sc = (P.sems(x) for x in ("V", "k", "h", "g_out"))
        s_sel, s_agg, s_ac, s_m, s_g, s_i = (P.sem(x) for x in ("sel", "agg", "aggcopy", "m", "g", "idx"))
        with nc.Block() as block:
            @block.sync
            def _(sp):
                def body(i, u, has):
                    f = Flow(sp, has)
                    sum_loads(sp, m, f, i, u, V, krow, s_V, s_k, s_sel, s_agg)
                    f.after(s_m, i - 4)
                    sp.dma_start(h[u][:], turned(m.HDb, i)).then_inc(s_h[u], 16)

                sweep(sp, 0, n, n - 1, body, back=4, ahead=0, special=0)

            @block.gpsimd
            def _(pool):
                def body(i, u, has):
                    f = Flow(pool, has, m)
                    f.after(s_g, i)
                    f.landed(s_sc, i - 4, u, 64)
                    scatter(nc, pool, f, m.i_dst2f1, idx, s_i, i, u, m.XH, g, s_sc)

                sweep(pool, 0, n, n - 1, body, back=4, ahead=0, special=0)
                finish(pool, s_sc, n, 64)

            @block.vector
            def _(dve):
                def body(i, u, has):
                    f = Flow(dve, has)
                    if has(i - 1):
                        v = (u - 1) % 4
                        f.after(s_agg, i - 1)
                        f.after(s_m, i - 5)
                        nc.vector.tensor_copy(agg[v][:], m.bank[v % 2][:, 0:EG]).then_inc(s_ac, 1)
                    if has(i + 1):
                        selectors(nc, m, f, i + 1, (u + 1) % 4, krow, S, s_k, s_sel, s_agg)

                sweep(dve, -1, n, n, body, back=5, ahead=1, special=0)

            @block.scalar
            def _(act):
                def body(i, u, has):
                    f = Flow(act, has)
                    f.after(s_m, i)
                    f.landed(s_sc, i - 4, u, 64)
                    nc.scalar.activation(g[u][:], m.bank[2 + u % 2][0:EP, :].rearrange("p (c f) -> p c f", c=TILE), ACT.Copy,
                                         scale=1.0 / 3.0).then_inc(s_g, 1)

                sweep(act, 0, n, n - 1, body, back=4, ahead=0, special=0)

            @block.tensor
            def _(pe):
                def body(i, u, has):
                    f = Flow(pe, has)
                    if has(i):
                        f.after(s_ac, i - 2)
                        add_up(nc, m, f, i, u, V, S, m.bank[u % 2], s_V, s_sel, s_agg)
                    if has(i - 1):
                        v = (u - 1) % 4
                        f.landed(s_h, i - 1, v)
                        f.after(s_ac, i - 1)
                        f.after(s_g, i - 3)
                        for c in range(TILE):
                            cs, o = slice(c * EP, (c + 1) * EP), m.bank[2 + v % 2][0:EP, c * D:(c + 1) * D]
                            nc.tensor.matmul(o, h[v][:, cs], m.w["S"], start=True, stop=False)
                            last = nc.tensor.matmul(o, agg[v][:, cs], m.w["O"], start=False, stop=True)
                        last.then_inc(s_m, 1)

                sweep(pe, 0, n, n, body, back=4, ahead=0, special=0)


def add_to_src(nc, m, name, load, table, index, weight=None):
    n = m.T // TILE
    with Phase(m, name) as P:
        r = P.slots("r", [EP, TILE, D])
        ea = P.slots("ea", [EP, TILE, D]) if weight else None
        val = P.slots("val", [EP, TILE, D]) if weight else r
        out = P.slots("out", [EP, TILE, D])
        krow, eq = P.slots("srow", [EP, EG]), P.slots("eq", [EP, TILE, EG])
        sumT = P.slots("sumT", [128, EG])
        idx = P.slots("idx", [EP, TILE], I32)
        s_l, s_e, s_k, s_sc = (P.sems(x) for x in ("r", "ea", "k", "out"))
        s_v, s_eq, s_m, s_sT, s_w, s_o, s_i = (P.sem(x) for x in ("val", "eq", "m", "sumT", "w", "o", "idx"))
        with nc.Block() as block:
            @block.sync
            def _(sp):
                def body(i, u, has):
                    f = Flow(sp, has)
                    f.after(s_v if weight else s_m, i - 4)
                    sp.dma_start(r[u][:], edge_rows(load, i)).then_inc(s_l[u], 16)
                    if weight:
                        sp.dma_start(ea[u][:], edge_rows(m.edge["ea"], i)).then_inc(s_e[u], 16)
                    Flow(sp, has, m).after(s_eq, i - 4)
                    keys = m.KS.rearrange("t p -> (t p)")[bass.ds(i * EG, EG)].rearrange("(a n) -> a n", a=1)
                    sp.dma_start(krow[u][:], keys.to_broadcast([EP, EG])).then_inc(s_k[u], 16)

                sweep(sp, 0, n, n - 1, body, back=4, ahead=0, special=0)

            @block.vector
            def _(dve):
                def body(i, u, has):
                    f = Flow(dve, has)
                    f.landed(s_k, i, u)
                    f.after(s_m, i - 4)
                    for c in range(TILE):
                        t = bass.ds(i * TILE + c, 1)
                        last = nc.vector.tensor_scalar(eq[u][:, c, :], krow[u][:], m.csrc[:, t], m.inv_s[0:EP, t], ALU.is_equal, ALU.mult)
                    last.then_inc(s_eq, 1)
                    if weight:
                        f.landed(s_l, i, u)
                        f.landed(s_e, i, u)
                        f.after(s_m, i - 4)
                        nc.vector.tensor_tensor(val[u][:], r[u][:], ea[u][:], ALU.subtract).then_inc(s_v, 1)

                sweep(dve, 0, n, n - 1, body, back=4, ahead=0, special=0)

            @block.tensor
            def _(pe):
                def body(i, u, has):
                    f = Flow(pe, has)
                    if has(i):
                        f.after(s_eq, i)
                        if weight:
                            f.after(s_v, i)
                            f.after(s_sT, i - 2)
                            for c in range(TILE):
                                last = nc.tensor.matmul(m.bank[u % 2][:, 0:EG], val[u][:, c, :], eq[u][:, c, :],
                                                        start=(c == 0), stop=(c == TILE - 1))
                        else:
                            f.landed(s_l, i, u)
                            f.after(s_o, i - 2)
                            for d in range(TILE):
                                for c in range(TILE):
                                    last = nc.tensor.matmul(m.bank[2 + u % 2][0:EP, d * D:(d + 1) * D], eq[u][:, c, d * EP:(d + 1) * EP],
                                                            r[u][:, c, :], start=(c == 0), stop=(c == TILE - 1))
                        last.then_inc(s_m, 1)
                    if weight and has(i - 1):
                        v = (u - 1) % 4
                        f.after(s_sT, i - 1)
                        f.after(s_o, i - 3)
                        for c in range(TILE):
                            last = nc.tensor.matmul(m.bank[2 + v % 2][0:EP, c * D:(c + 1) * D], sumT[v][:, c * EP:(c + 1) * EP],
                                                    weight, start=True, stop=True)
                        last.then_inc(s_w, 1)

                sweep(pe, 0, n, n if weight else n - 1, body, back=4, ahead=0, special=0)

            @block.scalar
            def _(act):
                def body(i, u, has):
                    f = Flow(act, has)
                    if weight and has(i):
                        f.after(s_m, i)
                        f.after(s_w, i - 4)
                        nc.scalar.activation(sumT[u][:], m.bank[u % 2][:, 0:EG], ACT.Copy, scale=1.0 / 3.0).then_inc(s_sT, 1)
                    if has(i - 1):
                        v = (u - 1) % 4
                        f.after(s_w if weight else s_m, i - 1)
                        f.landed(s_sc, i - 5, v, 64)
                        nc.scalar.activation(out[v][:], m.bank[2 + v % 2][0:EP, :].rearrange("p (c f) -> p c f", c=TILE), ACT.Copy)\
                          .then_inc(s_o, 1)

                sweep(act, 0, n, n, body, back=5, ahead=0, special=0)

            @block.gpsimd
            def _(pool):
                def body(i, u, has):
                    f = Flow(pool, has, m)
                    f.after(s_o, i)
                    f.landed(s_sc, i - 1, u - 1, 64)
                    scatter(nc, pool, f, index, idx, s_i, i, u, table, out, s_sc, add=True)

                sweep(pool, 0, n, n - 1, body, back=4, ahead=0, special=0)
                finish(pool, s_sc, n, 64)


def batch_norm(nc, m, a):
    N = m.N
    n = -(-N // ROWS)
    with Phase(m, "BN") as P:
        g, st = P.slots("g", [128, TILE, D]), P.sb("stats", [128, n * 6])
        mv, c = P.sb("mv", [128, 2]), P.sb("c", [128, 8])
        s_in, s_T, s_s, s_v, s_a, s_r = P.sems("g_in"), P.sem("turned"), P.sem("stats"), P.sem("chain"), P.sem("sqrt"), P.sem("rows")
        rest = N - (n - 1) * ROWS

        def rows_of(i):
            count = rest if isinstance(i, int) and i == n - 1 else ROWS
            return m.XG[bass.ds(i * ROWS, count), D:2 * D].rearrange("(p j) f -> p j f", j=TILE), count // TILE

        with nc.Block() as block:
            @block.sync
            def _(sp):
                def body(i, u, has):
                    f = Flow(sp, has)
                    f.after(s_T, i - 4)
                    rows, q = rows_of(i)
                    sp.dma_start(g[u][0:q], rows).then_inc(s_in[u], 16)

                sweep(sp, 0, n, n - 1, body, back=4, ahead=0, special=1)

            @block.tensor
            def _(pe):
                def body(i, u, has):
                    f = Flow(pe, has)
                    f.landed(s_in, i, u)
                    f.after(s_s, i - 4)
                    q = rows_of(i)[1]
                    for j in range(TILE):
                        last = nc.tensor.transpose(m.bank[u][:, j * q:(j + 1) * q], g[u][0:q, j, :], m.ident[0:q, 0:q])
                    last.then_inc(s_T, 1)

                sweep(pe, 0, n, n - 1, body, back=4, ahead=0, special=1)
                pe.wait_ge(s_v, 8)
                for k in range(2):
                    last = nc.tensor.matmul(m.bank[4][:, k * D:(k + 1) * D], c[:, 3 + k:4 + k].to_broadcast([128, 128]), m.ident[:],
                                            start=True, stop=True)
                last.then_inc(s_r, 1)

            @block.vector
            def _(dve):
                def body(i, u, has):
                    f = Flow(dve, has)
                    f.after(s_T, i)
                    nc.vector.bn_stats(st[:, bass.ds(i * 6, 6)], m.bank[u][:, 0:TILE * rows_of(i)[1]]).then_inc(s_s, 1)

                sweep(dve, 0, n, n - 1, body, back=4, ahead=0, special=1)
                dve.wait_ge(s_s, n)
                nc.vector.bn_aggr(mv[:], st[:]).then_inc(s_v, 1)
                nc.vector.tensor_tensor(c[:, 5:6], m.col["bO"], m.col["bI"], ALU.add).then_inc(s_v, 1)
                dve.wait_ge(s_v, 2)
                nc.vector.tensor_tensor(c[:, 6:7], c[:, 5:6], m.col["bS"], ALU.add).then_inc(s_v, 1)
                dve.wait_ge(s_a, 1)
                nc.vector.reciprocal(c[:, 1:2], c[:, 0:1]).then_inc(s_v, 1)
                dve.wait_ge(s_v, 4)
                nc.vector.tensor_tensor(c[:, 3:4], c[:, 1:2], m.col["gamma"], ALU.mult).then_inc(s_v, 1)
                nc.vector.scalar_tensor_tensor(c[:, 2:3], c[:, 6:7], 1.0 / 3.0, mv[:, 0:1], ALU.mult, ALU.add).then_inc(s_v, 1)
                dve.wait_ge(s_v, 6)
                nc.vector.scalar_tensor_tensor(c[:, 7:8], c[:, 6:7], 1.0 / 3.0, c[:, 2:3], ALU.mult, ALU.subtract).then_inc(s_v, 1)
                dve.wait_ge(s_v, 7)
                nc.vector.scalar_tensor_tensor(c[:, 4:5], c[:, 7:8], c[:, 3:4], m.col["beta"], ALU.mult, ALU.add).then_inc(s_v, 1)
                dve.wait_ge(s_r, 1)
                nc.vector.tensor_copy(m.Arow[:], m.bank[4][:, 0:D])
                nc.vector.tensor_copy(m.Brow[:], m.bank[4][:, D:2 * D]).then_inc(s_v, 1)

            @block.scalar
            def _(act):
                act.wait_ge(s_v, 1)
                nc.scalar.activation(c[:, 0:1], mv[:, 1:2], ACT.Sqrt, bias=m.col["eps"]).then_inc(s_a, 1)


def messages(nc, m, a):
    n = m.T // TILE
    with Phase(m, "G4") as P:
        idx, x = P.slots("idx", [EP, TILE], I32), P.slots("x", [EP, TILE, 2 * D])
        t, t2, x2, h, V = (P.slots(k, [EP, TILE, D]) for k in ("t", "t2", "x2", "h", "V"))
        hT, trow, one = P.slots("hT", [128, EG]), P.slots("types", [9, EG]), P.slots("onehot", [9, EG])
        ln = Norm(nc, m, P, TILE)
        s_i, s_t, s_x2, s_h, s_T, s_hT, s_m, s_one, s_v, s_hl = \
            (P.sem(k) for k in ("idx", "t", "x2", "h", "T", "hT", "m", "onehot", "v", "firstlast"))
        s_g, s_ty, s_vo = (P.sems(k) for k in ("got", "types", "v_out"))
        rows = lambda r: r[0:EP, :].unsqueeze(1).to_broadcast([EP, TILE, D])
        with nc.Block() as block:
            @block.gpsimd
            def _(pool):
                def body(i, u, has):
                    f = Flow(pool, has, m)
                    f.after(s_x2, i - 4)
                    gather(nc, pool, f, m.i_src, idx, s_i, i, u, m.XG, x, s_g)

                sweep(pool, 0, n, n - 1, body, back=4, ahead=0, special=0)

            @block.sync
            def _(sp):
                def load(f, i, u):
                    f.after(s_one, i - 4)
                    keys = m.KT.rearrange("t p -> (t p)")[bass.ds(i * EG, EG)].rearrange("(a n) -> a n", a=1)
                    sp.dma_start(trow[u][:], keys.to_broadcast([9, EG])).then_inc(s_ty[u], 16)

                def body(i, u, has):
                    f = Flow(sp, has)
                    if has(i + 3):
                        load(f, i + 3, (u + 3) % 4)
                    if has(i - 4):
                        f.after(s_v, i - 4)
                        sp.dma_start(value_tiles(m, i - 4)[0:EP], V[u][:]).then_inc(s_vo[u], 16)

                sweep(sp, -3, n, n + 3, body, back=4, ahead=3, special=0)
                finish(sp, s_vo, n)

            @block.vector
            def _(dve):
                def body(i, u, has):
                    f = Flow(dve, has)
                    if has(i - 1):
                        ln.finish(f, i - 1, (u - 1) % 4)
                    if has(i):
                        f.landed(s_g, i, u, 64)
                        nc.vector.tensor_tensor(t[u][:], x[u][:, :, D:2 * D], rows(m.Arow), ALU.mult).then_inc(s_t, 1)
                        dve.wait_ge(s_t, 2 * i + 1)
                        nc.vector.tensor_tensor(t2[u][:], t[u][:], rows(m.Brow), ALU.add).then_inc(s_t, 1)
                        dve.wait_ge(s_t, 2 * i + 2)
                        nc.vector.tensor_tensor(x2[u][:], t2[u][:], x[u][:, :, 0:D], ALU.add).then_inc(s_x2, 1)
                        f.after(s_x2, i)
                        ln.stats(dve, f, i, u, [x2[u][:, c, :] for c in range(TILE)])
                        f.landed(s_ty, i, u)
                        f.after(s_m, i - 4)
                        nc.vector.tensor_scalar(one[u][:], trow[u][:], m.type_id[:], None, ALU.is_equal).then_inc(s_one, 1)
                    if has(i - 3):
                        v = (u - 3) % 4
                        f.after(s_m, i - 3)
                        f.landed(s_vo, i - 7, v)
                        f.after(s_hl, i - 7)
                        nc.vector.tensor_copy(V[v][:], m.bank[2 + v % 2][0:EP, :].rearrange("p (c f) -> p c f", c=TILE)).then_inc(s_v, 1)

                sweep(dve, 0, n, n + 2, body, back=7, ahead=0, special=0)

            @block.scalar
            def _(act):
                def body(i, u, has):
                    f = Flow(act, has)
                    if has(i):
                        ln.root(f, i, u)
                    if has(i - 1):
                        v = (u - 1) % 4
                        f.after(ln.s_nb, i - 1)
                        f.after(s_T, i - 5)
                        ln.relu(h[v], [x2[v][:, c, :] for c in range(TILE)], v).then_inc(s_h, 1)
                    if has(i - 2):
                        v = (u - 2) % 4
                        f.after(s_T, i - 2)
                        f.after(s_m, i - 6)
                        nc.scalar.activation(hT[v][:], m.bank[v % 2][:, 0:EG], ACT.Copy).then_inc(s_hT, 1)

                sweep(act, 0, n, n + 1, body, back=6, ahead=0, special=0)

            @block.tensor
            def _(pe):
                def body(i, u, has):
                    f = Flow(pe, has)
                    if has(i - 2):
                        v = (u - 2) % 4
                        f.after(s_h, i - 2)
                        f.after(s_hT, i - 4)
                        for c in range(TILE):
                            last = nc.tensor.transpose(m.bank[v % 2][:, c * EP:(c + 1) * EP], h[v][:, c, :], m.ident[0:EP, 0:EP])
                        last.then_inc(s_T, 1)
                    if has(i - 3):
                        v = (u - 3) % 4
                        f.after(s_hT, i - 3)
                        f.after(s_one, i - 3)
                        f.after(s_v, i - 5)
                        for c in range(TILE):
                            cs, o = slice(c * EP, (c + 1) * EP), m.bank[2 + v % 2][0:EP, c * D:(c + 1) * D]
                            nc.tensor.matmul(o, hT[v][:, cs], m.w["msg"], start=True, stop=False)
                            last = nc.tensor.matmul(o, one[v][:, cs], m.embed[:], start=False, stop=True)
                        last.then_inc(s_m, 1)
                    if has(i - 4):
                        f.after(s_v, i - 4)
                        first_last_sums(nc, m, V[u], i - 4).then_inc(s_hl, 1)

                sweep(pe, 0, n, n + 3, body, back=5, ahead=0, special=0)
    share_segments(nc, m, "G4_shared")


def gru(nc, m, a, sparse):
    N = m.N
    np_, W = (EP, EG) if sparse else (128, ROWS)
    n = m.T // TILE if sparse else -(-N // ROWS)
    span = W // TILE
    with Phase(m, "B5" if sparse else "P3") as P:
        x = P.slots("x", [np_, TILE, 2 * D])
        xb, t, h = (P.slots(k, [np_, TILE, D], count=2) for k in ("xb", "gA", "h"))
        x2 = P.slots("x2", [np_, TILE, D], count=8)
        out = P.slots("out", [np_, TILE, D])
        hT, r, z, rn, nT, dT, q, hn = (P.slots(k, [128, W], count=4 if k in ("hT", "z", "n") else 2)
                                       for k in ("hT", "r", "z", "rn", "n", "d", "q", "hnew"))
        st, mv, ve = P.slots("st", [np_, TILE, 6]), P.slots("mv", [np_, TILE, 2]), P.slots("ve", [np_, TILE])
        rs, nb = P.slots("rs", [np_, TILE]), P.slots("nb", [np_, TILE])
        s_x, s_o = P.sems("x_in"), P.sems("out")
        names = ("xb", "t", "x2", "st", "mv", "ve", "rs", "nb", "h", "T", "hT", "gates", "r", "z", "rn", "n", "d", "q", "hnew", "back", "fin")
        s = {k: P.sem(k) for k in names}
        bT, bB = m.bank[0:2]
        bR, bZ, bN = (m.bank[2:3], m.bank[3:4], m.bank[4:5]) if sparse else (m.bank[2:4], m.bank[4:6], m.bank[6:8])
        bI, bA = m.bank[5:7]
        B = len(bR)
        if sparse:
            V, krow, S = (P.slots("V", [EP + 2, TILE, D]), P.slots("krow", [EP + 2, EG]), P.slots("S", [EP + 2, EG]))
            agg, idx = P.slots("agg", [128, EG]), P.slots("idx", [EP, TILE], I32)
            hnm = P.slots("rnm", [128, W], count=2)
            s["t2"] = P.sem("t2")
            s_V, s_k = P.sems("V"), P.sems("k")
            s_sel, s_agg, s_ac, s_i = (P.sem(k) for k in ("sel", "agg", "aggcopy", "idx"))
        rows = lambda w: w[0:np_, :].unsqueeze(1).to_broadcast([np_, TILE, D])

        def base_of(g):
            return min(g * ROWS, N - ROWS) if isinstance(g, int) else g * ROWS

        special = 0 if sparse else 1
        per = 64 if sparse else 16
        with nc.Block() as block:
            @block.sync
            def _(sp):
                def load(f, i, u):
                    if sparse:
                        sum_loads(sp, m, f, i, u % 4, V, krow, s_V, s_k, s_sel, s_agg)
                    else:
                        f.after(s["x2"], i - 4)
                        sp.dma_start(x[u % 4][:], m.XG[bass.ds(base_of(i), ROWS), :].rearrange("(p j) f -> p j f", j=TILE))\
                          .then_inc(s_x[u % 4], 16)

                def body(i, u, has):
                    f = Flow(sp, has)
                    if has(i + 3):
                        load(f, i + 3, (u + 3) % 4)
                    if has(i - 8):
                        v = u % 4
                        f.after(s["fin"], i - 8)
                        if sparse:
                            sp.dma_start(edge_rows(m.XD, i - 8), out[v][:]).then_inc(s_o[v], 16)
                        else:
                            lo = ((n - 1) * ROWS - (N - ROWS)) // TILE if isinstance(i, int) and i - 8 == n - 1 else 0
                            sp.dma_start(m.out[bass.ds(base_of(i - 8) + lo * TILE, ROWS - lo * TILE), :].rearrange("(p j) f -> p j f", j=TILE),
                                         out[v][lo:128]).then_inc(s_o[v], 16)

                sweep(sp, -3, n, n + 7, body, unroll=8, back=8, ahead=3, special=special)
                finish(sp, s_o, n)

            @block.gpsimd
            def _(pool):
                def body(i, u, has):
                    f = Flow(pool, has)
                    if has(i - 1):
                        v = (u - 1) % 4
                        f.after(s["h"], i - 5)
                        f.after(s["ve"], i - 1)
                        nc.gpsimd.tensor_tensor(rs[v][:], ve[v][:], m.minus_half[0:np_, :], ALU.pow).then_inc(s["rs"], 1)
                    if has(i - 5):
                        v = (u - 5) % 4
                        f.after(s["n"], i - 5)
                        f.after(s["q"], i - 7)
                        nc.gpsimd.tensor_tensor(dT[v % 2][:], hT[v][:], nT[v][:], ALU.subtract).then_inc(s["d"], 1)
                    if has(i + 1):
                        v = (u + 1) % 4
                        if not sparse:
                            f.after(s["x2"], i - 1)
                            f.landed(s_x, i + 1, v, per)
                            nc.gpsimd.tensor_tensor(xb[v % 2][:], x[v][:, :, 0:D], rows(m.Brow), ALU.add).then_inc(s["xb"], 1)
                            nc.gpsimd.tensor_tensor(t[v % 2][:], x[v][:, :, D:2 * D], rows(m.Arow), ALU.mult).then_inc(s["t"], 1)
                    if sparse and has(i + 2):
                        g = Flow(pool, has, m)
                        g.after(s["x2"], i - 2)
                        gather(nc, pool, g, m.i_dst, idx, s_i, i + 2, (u + 2) % 4, m.XG, x, s_x)

                sweep(pool, -2 if sparse else -1, n, n + 4, body, unroll=8, back=7, ahead=2, special=special)

            @block.vector
            def _(dve):
                def body(i, u, has):
                    f = Flow(dve, has)
                    if has(i - 8):
                        v = u % 4
                        f.after(s["back"], i - 8)
                        f.landed(s_o, i - 12, v)
                        nc.vector.tensor_tensor(out[v][:], bB[0:np_, :].rearrange("p (c f) -> p c f", c=TILE), x2[u][:], ALU.add)\
                          .then_inc(s["fin"], 1)
                    if sparse and has(i + 1):
                        selectors(nc, m, f, i + 1, (u + 1) % 4, krow, S, s_k, s_sel, s_agg, mean=False)
                    if has(i):
                        v = u % 4
                        if sparse:
                            f.landed(s_x, i, v, per)
                            nc.vector.tensor_tensor(t[v % 2][:], x[v][:, :, D:2 * D], rows(m.Arow), ALU.mult).then_inc(s["t"], 1)
                            nc.vector.tensor_tensor(xb[v % 2][:], x[v][:, :, 0:D], rows(m.Brow), ALU.add).then_inc(s["xb"], 1)
                        f.after(s["t"], i)
                        f.after(s["xb"], i)
                        f.after(s["fin"], i - 8)
                        nc.vector.tensor_tensor(x2[u][:], t[v % 2][:], xb[v % 2][:], ALU.add).then_inc(s["x2"], 1)
                    if has(i - 6):
                        v = (u - 6) % 4
                        f.after(s["d"], i - 6)
                        nc.vector.tensor_tensor(q[v % 2][:], z[v][:], dT[v % 2][:], ALU.mult).then_inc(s["q"], 1)
                    if has(i):
                        v = u % 4
                        f.after(s["x2"], i)
                        for j in range(TILE):
                            last = nc.vector.bn_stats(st[v][:, j, :], x2[u][:, j, :])
                        last.then_inc(s["st"], 1)
                    if has(i - 6):
                        v = (u - 6) % 4
                        f.after(s["q"], i - 6)
                        f.after(s["back"], i - 8)
                        nc.vector.tensor_tensor(hn[v % 2][:], nT[v][:], q[v % 2][:], ALU.add).then_inc(s["hnew"], 1)
                    if has(i):
                        v = u % 4
                        Flow(dve, has, m).after(s["st"], i)
                        for j in range(TILE):
                            last = nc.vector.bn_aggr(mv[v][:, j, :], st[v][:, j, :])
                        last.then_inc(s["mv"], 1)
                        f.after(s["mv"], i)
                        nc.vector.tensor_scalar(ve[v][:], mv[v][:, :, 1], LN_EPS, None, ALU.add).then_inc(s["ve"], 1)
                    if has(i - 1):
                        v = (u - 1) % 4
                        f.after(s["rs"], i - 1)
                        nc.vector.scalar_tensor_tensor(nb[v][:], mv[v][:, :, 0], -1.0, rs[v][:], ALU.mult, ALU.mult).then_inc(s["nb"], 1)
                    if has(i - 4):
                        v = u % 4
                        f.after(s["r"], i - 4)
                        f.after(s["n"], i - 6)
                        rn_of = s["t2"] if sparse else s["rn"]
                        nc.vector.scalar_tensor_tensor(rn[v % 2][:], bN[v % B][:, 0:W], m.col["bhh_n"], r[v % 2][:], ALU.add, ALU.mult)\
                          .then_inc(rn_of, 1)
                        if sparse:
                            f.after(s["t2"], i - 4)
                            nc.vector.tensor_tensor(hnm[v % 2][:], rn[v % 2][:], bI[:, 0:W], ALU.add).then_inc(s["rn"], 1)

                sweep(dve, -1, n, n + 7, body, unroll=8, back=12, ahead=1, special=special)

            @block.scalar
            def _(act):
                def body(i, u, has):
                    f = Flow(act, has)
                    if sparse and has(i - 1):
                        v = (u - 1) % 4
                        f.after(s_agg, i - 1)
                        f.after(s["gates"], i - 5)
                        nc.scalar.activation(agg[v][:], bA[:, 0:EG], ACT.Copy).then_inc(s_ac, 1)
                    if has(i - 3):
                        v = (u - 3) % 4
                        f.after(s["T"], i - 3)
                        f.after(s["d"], i - 7)
                        nc.scalar.activation(hT[v][:], bT[:, 0:W], ACT.Copy).then_inc(s["hT"], 1)
                    if has(i - 5):
                        v = (u - 5) % 4
                        f.after(s["rn"], i - 5)
                        f.after(s["hnew"], i - 9)
                        nc.scalar.activation(nT[v][:], (hnm if sparse else rn)[v % 2][:], ACT.Tanh, bias=m.col["bih_n"]).then_inc(s["n"], 1)
                    if has(i - 2):
                        v = (u - 2) % 4
                        f.after(s["nb"], i - 2)
                        f.after(s["T"], i - 4)
                        for j in range(TILE):
                            last = nc.scalar.activation(h[v % 2][:, j, :], x2[(u - 2) % 8][:, j, :], ACT.Relu, scale=rs[v][:, j:j + 1], bias=nb[v][:, j:j + 1])
                        last.then_inc(s["h"], 1)
                    if has(i - 4):
                        v = u % 4
                        f.after(s["gates"], i - 4)
                        f.after(s["rn"], i - 6)
                        nc.scalar.activation(r[v % 2][:], bR[v % B][:, 0:W], ACT.Sigmoid, bias=m.col["b_r"]).then_inc(s["r"], 1)
                        f.after(s["q"], i - 8)
                        nc.scalar.activation(z[v][:], bZ[v % B][:, 0:W], ACT.Sigmoid, bias=m.col["b_z"]).then_inc(s["z"], 1)

                sweep(act, 0, n, n + 4, body, unroll=8, back=9, ahead=0, special=special)

            @block.tensor
            def _(pe):
                def body(i, u, has):
                    f = Flow(pe, has)
                    if has(i - 3):
                        v = (u - 3) % 4
                        f.after(s["h"], i - 3)
                        f.after(s["hT"], i - 4)
                        for c in range(TILE):
                            last = nc.tensor.transpose(bT[:, c * span:(c + 1) * span], h[v % 2][:, c, :], m.ident[0:span, 0:span])
                        last.then_inc(s["T"], 1)
                    if sparse and has(i):
                        f.after(s_ac, i - 1)
                        add_up(nc, m, f, i, u % 4, V, S, bA, s_V, s_sel, s_agg)
                    if has(i - 4):
                        v = u % 4
                        f.after(s["hT"], i - 4)
                        f.after(s["z"], i - 4 - B)
                        f.after(s["rn"], i - 4 - B)
                        if sparse:
                            f.after(s_ac, i - 4)
                            nc.tensor.matmul(bI[:, 0:W], m.w["ih_n"], agg[v][:], start=True, stop=True)
                        for bank, gate in ((bR, "r"), (bZ, "z"), (bN, "n")):
                            with_m = sparse and gate != "n"
                            last = nc.tensor.matmul(bank[v % B][:, 0:W], m.w["hh_" + gate], hT[v][:], start=True, stop=not with_m)
                            if with_m:
                                nc.tensor.matmul(bank[v % B][:, 0:W], m.w["ih_" + gate], agg[v][:], start=False, stop=True)
                        last.then_inc(s["gates"], 1)
                    if has(i - 7):
                        v = (u - 7) % 4
                        f.after(s["hnew"], i - 7)
                        f.after(s["fin"], i - 8)
                        for c in range(TILE):
                            last = nc.tensor.transpose(bB[0:np_, c * D:(c + 1) * D], hn[v % 2][:, c * span:(c + 1) * span], m.ident[:])
                        last.then_inc(s["back"], 1)

                sweep(pe, 0, n, n + 6, body, unroll=8, back=8, ahead=0, special=special)


def leaving(nc, m, a):
    n = m.T // TILE
    with Phase(m, "O1") as P:
        idx, x, h, L = P.slots("idx", [EP, TILE], I32), *(P.slots(k, [EP, TILE, D]) for k in ("x", "h", "L"))
        hT = P.slots("hT", [128, EG])
        ln = Norm(nc, m, P, TILE)
        s_i, s_h, s_T, s_hT, s_m, s_l = (P.sem(k) for k in ("idx", "h", "T", "hT", "m", "l"))
        s_x, s_lo, s_sc = (P.sems(k) for k in ("x", "l_out", "x3_out"))
        with nc.Block() as block:
            @block.gpsimd
            def _(pool):
                def body(i, u, has):
                    f = Flow(pool, has, m)
                    f.landed(s_x, i, u)
                    scatter(nc, pool, f, m.i_dstf, idx, s_i, i, u, m.out, x, s_sc)

                sweep(pool, 0, n, n - 1, body, back=4, ahead=0, special=0)
                finish(pool, s_sc, n, 64)

            @block.sync
            def _(sp):
                def load(f, i, u):
                    f.after(s_h, i - 4)
                    f.landed(s_sc, i - 4, u, 64)
                    sp.dma_start(x[u][:], edge_rows(m.XD, i)).then_inc(s_x[u], 16)

                def body(i, u, has):
                    f = Flow(sp, has)
                    if has(i + 3):
                        load(f, i + 3, (u + 3) % 4)
                    if has(i - 4):
                        f.after(s_l, i - 4)
                        sp.dma_start(edge_rows(m.LT, i - 4), L[u][:]).then_inc(s_lo[u], 16)

                sweep(sp, -3, n, n + 3, body, back=4, ahead=3, special=0)
                finish(sp, s_lo, n)

            @block.vector
            def _(dve):
                def body(i, u, has):
                    f = Flow(dve, has)
                    if has(i - 1):
                        ln.finish(f, i - 1, (u - 1) % 4)
                    if has(i):
                        f.landed(s_x, i, u)
                        ln.stats(dve, f, i, u, [x[u][:, c, :] for c in range(TILE)])
                    if has(i - 3):
                        v = (u - 3) % 4
                        f.after(s_m, i - 3)
                        f.landed(s_lo, i - 7, v)
                        nc.vector.tensor_tensor(L[v][:], m.bank[2 + v % 2][0:EP, :].rearrange("p (c f) -> p c f", c=TILE),
                                                m.boutrow[0:EP, :].unsqueeze(1).to_broadcast([EP, TILE, D]), ALU.add).then_inc(s_l, 1)

                sweep(dve, 0, n, n + 2, body, back=7, ahead=0, special=0)

            @block.scalar
            def _(act):
                def body(i, u, has):
                    f = Flow(act, has)
                    if has(i):
                        ln.root(f, i, u)
                    if has(i - 1):
                        v = (u - 1) % 4
                        f.after(ln.s_nb, i - 1)
                        f.after(s_T, i - 5)
                        ln.relu(h[v], [x[v][:, c, :] for c in range(TILE)], v).then_inc(s_h, 1)
                    if has(i - 2):
                        v = (u - 2) % 4
                        f.after(s_T, i - 2)
                        f.after(s_m, i - 6)
                        nc.scalar.activation(hT[v][:], m.bank[v % 2][:, 0:EG], ACT.Copy).then_inc(s_hT, 1)

                sweep(act, 0, n, n + 1, body, back=6, ahead=0, special=0)

            @block.tensor
            def _(pe):
                def body(i, u, has):
                    f = Flow(pe, has)
                    if has(i - 2):
                        v = (u - 2) % 4
                        f.after(s_h, i - 2)
                        f.after(s_hT, i - 4)
                        for c in range(TILE):
                            last = nc.tensor.transpose(m.bank[v % 2][:, c * EP:(c + 1) * EP], h[v][:, c, :], m.ident[0:EP, 0:EP])
                        last.then_inc(s_T, 1)
                    if has(i - 3):
                        v = (u - 3) % 4
                        f.after(s_hT, i - 3)
                        f.after(s_l, i - 5)
                        for c in range(TILE):
                            last = nc.tensor.matmul(m.bank[2 + v % 2][0:EP, c * D:(c + 1) * D], hT[v][:, c * EP:(c + 1) * EP], m.w["out"],
                                                    start=True, stop=True)
                        last.then_inc(s_m, 1)

                sweep(pe, 0, n, n + 2, body, back=5, ahead=0, special=0)


def network(nc, m, a):
    with ExitStack() as ctx:
        m.ctx = ctx
        m.bank = [ctx.enter_context(nc.psum_tensor(f"bank{k}", [128, 512], F32)) for k in range(8)]
        m.XG = nc.dram_tensor("node_table", [m.N, 2 * D], F32, kind="Internal").ap()
        m.XH = m.XG.rearrange("n (h f) -> (n h) f", h=2)
        load_weights(nc, m, a)
        order_edges(nc, m, a)
        edges_setup(nc, m, a)
        dense_first(nc, m, a)
        edges_start(nc, m, a)
        layer(nc, m, 1, m.HDa, m.HDb, m.TB1[0:m.E, :])
        take(nc, m, 1, m.TB1)
        layer(nc, m, 2, m.HDb, m.HDa, m.TB2[0:m.E, :])
        take(nc, m, 2, m.TB2)
        third_layer(nc, m, a)
        incoming(nc, m, a)
        outgoing_self(nc, m, a)
        add_to_src(nc, m, "H", m.H1, m.XH, m.i_src2f1, weight=m.w["I"])
        batch_norm(nc, m, a)
        messages(nc, m, a)
        gru(nc, m, a, False)
        gru(nc, m, a, True)
        leaving(nc, m, a)
        add_to_src(nc, m, "O2", m.LT, m.out, m.i_srcf)


def kernel(**inputs):
    import numpy as _np
    import concourse.bacc as _bacc
    from concourse import mybir as _mybir
    from concourse.bass_utils import run_bass_kernel_spmd as _run

    nc = _bacc.Bacc("TRN2", target_bir_lowering=False, num_devices=1)
    arrays, a = {}, {}
    for name, value in inputs.items():
        arrays[name] = _np.ascontiguousarray(value)
        a[name] = nc.dram_tensor(name, list(arrays[name].shape), _mybir.dt.from_np(arrays[name].dtype), kind="ExternalInput").ap()
    N, E = arrays["x"].shape[0], arrays["src"].shape[0]
    m = Net(nc, None, N, E)
    m.out = nc.dram_tensor("out", [N, D], _mybir.dt.float32, kind="ExternalOutput").ap()
    network(nc, m, a)
    r = _run(nc, [arrays], core_ids=[0])
    return r.results[0]["out"]
```

```python
from contextlib import ExitStack

import concourse.bass as bass
from concourse import mybir

F32 = mybir.dt.float32
BF16 = mybir.dt.bfloat16
I32 = mybir.dt.int32
ALU = mybir.AluOpType
ACT = mybir.ActivationFunctionType
AX = mybir.AxisListType

D = 128
TILE = 4
ROWS = TILE * 128
EP = 125
EG = TILE * EP
LN_EPS = 1e-5
TYPES = 9
CHUNKS = 4


def sweep(eng, first, n, last, body, unroll=4, back=3, ahead=3, special=1):
    together(eng, [(first, n, last, special, body)], unroll, back, ahead)


def together(eng, parts, unroll=4, back=3, ahead=3):
    start = unroll * -(-(back + 1) // unroll)
    end = start + unroll * max(0, min((n - special - ahead - start) // unroll for _, n, _, special, _ in parts))

    def step(i):
        for first, n, last, _, body in parts:
            if first <= i <= last:
                body(i, i % unroll, lambda g: 0 <= g < n)

    for i in range(min(p[0] for p in parts), start):
        step(i)
    if end > start:
        with eng.Fori(start // unroll, end // unroll) as k:
            for u in range(unroll):
                for _, _, _, _, body in parts:
                    body(k * unroll + u, u, lambda g: True)
    for i in range(end, max(p[2] for p in parts) + 1):
        step(i)


def slot_value(g, s, slots=4):
    return (g - s) * (16 // slots) + 16


class Net:

    def __init__(self, nc, ctx, N, E):
        self.nc, self.ctx, self.N, self.E = nc, ctx, N, E

    def sb(self, name, shape, dt=F32):
        return self.ctx.enter_context(self.nc.sbuf_tensor(name, shape, dt))

    def sem(self, name):
        return self.ctx.enter_context(self.nc.semaphore(name))

    def hold(self, eng, sem, value):
        eng.wait_ge(sem, value)
        eng.sem_inc(self.passed, 1)

    def sems(self, name, n):
        return [self.sem(f"{name}{k}") for k in range(n)]


def load_weights(nc, m, a):
    mats = [("self1", a["L0_gnn_W_self1"], 0), ("self2", a["L0_gnn_W_self2"], 0), ("self3", a["L0_gnn_W_self3"], 0),
            ("neigh1", a["L0_gnn_W_neigh1"], 0), ("neigh2", a["L0_gnn_W_neigh2"], 0), ("neigh3", a["L0_gnn_W_neigh3"], 0),
            ("O", a["L1_gnn_W_O"], 0), ("I", a["L1_gnn_W_I"], 0), ("S", a["L1_gnn_W_S"], 0), ("msg", a["L2_gnn_W_msg"], 0),
            ("ih_r", a["L2_gnn_W_ih"], 0), ("ih_z", a["L2_gnn_W_ih"], 1), ("ih_n", a["L2_gnn_W_ih"], 2),
            ("hh_r", a["L2_gnn_W_hh"], 0), ("hh_z", a["L2_gnn_W_hh"], 1), ("hh_n", a["L2_gnn_W_hh"], 2),
            ("out", a["L3_gnn_W"], 0)]
    cols = [("b1", a["L0_gnn_b_self1"], 0), ("b2", a["L0_gnn_b_self2"], 0), ("b3", a["L0_gnn_b_self3"], 0),
            ("bO", a["L1_gnn_b_O"], 0), ("bI", a["L1_gnn_b_I"], 0), ("bS", a["L1_gnn_b_S"], 0),
            ("gamma", a["L1_gnn_gamma"], 0), ("beta", a["L1_gnn_beta"], 0), ("bmsg", a["L2_gnn_b_msg"], 0),
            ("bih_r", a["L2_gnn_b_ih"], 0), ("bih_z", a["L2_gnn_b_ih"], 1), ("bih_n", a["L2_gnn_b_ih"], 2),
            ("bhh_r", a["L2_gnn_b_hh"], 0), ("bhh_z", a["L2_gnn_b_hh"], 1), ("bhh_n", a["L2_gnn_b_hh"], 2),
            ("bout", a["L3_gnn_b"], 0)]
    m.WT = m.sb("weightsT", [128, len(mats), D])
    m.w = {name: m.WT[:, k, :] for k, (name, _, _) in enumerate(mats)}
    m.COL = m.sb("bias_columns", [128, 24])
    m.col = {name: m.COL[:, k:k + 1] for k, (name, _, _) in enumerate(cols)}
    for k, name in enumerate(["b_r", "b_z", "eps"]):
        m.col[name] = m.COL[:, 17 + k:18 + k]
    m.b3row = m.sb("b3row", [128, D])
    m.ident = m.sb("ident", [128, 128])
    m.embed = m.sb("embed_parts", [3 * TYPES, D], BF16)
    m.boutrow = m.sb("boutrow", [128, D])
    m.minus_half = m.sb("minus_half", [128, TILE])
    m.type_id = m.sb("type_id", [3 * TYPES, 1])
    m.Arow, m.Brow = m.sb("bn_scale", [128, D]), m.sb("bn_shift", [128, D])
    m.ones = m.sb("ones", [128, 128])
    early = ExitStack()
    raw = early.enter_context(nc.sbuf_tensor("weights_raw", [128, len(mats), D], F32))
    bmsg = early.enter_context(nc.sbuf_tensor("bmsg_rows", [TYPES, D], F32))
    rest = [early.enter_context(nc.sbuf_tensor(f"embed_rest{k}", [TYPES, D], F32)) for k in range(3)]
    piece = [early.enter_context(nc.sbuf_tensor(f"embed_part{k}", [TYPES, D], BF16)) for k in range(3)]
    ids = early.enter_context(nc.sbuf_tensor("ids", [TYPES, 1], F32))
    s_in, s_ms, s_id = m.sem("w_in"), m.sem("w_consts"), m.sem("w_ident")
    s_t, s_c, s_b = m.sem("w_turned"), m.sem("w_copied"), m.sem("w_gate_bias")
    m.passed = m.sem("passed")
    with nc.Block() as block:
        @block.sync
        def _(sp):
            for k, (_, ap, part) in enumerate(mats):
                sp.dma_start(raw[:, k, :], ap[part * D:(part + 1) * D, :]).then_inc(s_in, 16)
            for k, (_, ap, part) in enumerate(cols):
                sp.dma_start(m.COL[:, k:k + 1], ap[part * D:(part + 1) * D].rearrange("(p a) -> p a", a=1)).then_inc(s_in, 16)
            sp.dma_start(rest[0][:], a["L2_gnn_edge_embed"]).then_inc(s_in, 16)
            sp.dma_start(bmsg[:], a["L2_gnn_b_msg"].rearrange("(a n) -> a n", a=1).to_broadcast([TYPES, D])).then_inc(s_in, 16)
            sp.dma_start(m.boutrow[:], a["L3_gnn_b"].rearrange("(a n) -> a n", a=1).to_broadcast([128, D])).then_inc(s_in, 16)
            sp.dma_start(m.b3row[:], a["L0_gnn_b_self3"].rearrange("(a n) -> a n", a=1).to_broadcast([128, D])).then_inc(s_in, 16)

            sp.wait_ge(s_b, 8)
            for k in range(3):
                sp.dma_start(m.embed[k * TYPES:(k + 1) * TYPES, :], piece[k][:]).then_inc(s_in, 16)
                sp.dma_start(m.type_id[k * TYPES:(k + 1) * TYPES, :], ids[:]).then_inc(s_in, 16)
            sp.wait_ge(s_in, 16 * (len(mats) + len(cols) + 10))

        @block.gpsimd
        def _(pool):
            nc.gpsimd.memset(m.ident[:], 0.0).then_inc(s_ms, 1)
            nc.gpsimd.memset(m.ones[:], 1.0).then_inc(s_ms, 1)
            nc.gpsimd.memset(m.col["eps"], LN_EPS).then_inc(s_ms, 1)
            nc.gpsimd.memset(m.minus_half[:], -0.5).then_inc(s_ms, 1)
            nc.gpsimd.iota(ids[:], [[0, 1]], base=0, channel_multiplier=1, allow_small_or_imprecise_dtypes=True).then_inc(s_ms, 1)
            pool.wait_ge(s_ms, 5)
            nc.gpsimd.affine_select(out=m.ident[:], in_=m.ident[:], compare_op=ALU.not_equal, fill=1.0, base=0,
                                    pattern=[[-1, 128]], channel_multiplier=1).then_inc(s_id, 1)

        @block.tensor
        def _(pe):
            pe.wait_ge(s_id, 1)
            pe.wait_ge(s_in, 16 * (len(mats) + len(cols) + 4))
            for k in range(len(mats)):
                if k >= 8:
                    pe.wait_ge(s_c, k - 7)
                nc.tensor.transpose(m.bank[k % 8][:, 0:128], raw[:, k, :], m.ident[:]).then_inc(s_t, 1)

        @block.vector
        def _(dve):
            for k in range(len(mats)):
                dve.wait_ge(s_t, k + 1)
                nc.vector.tensor_copy(m.WT[:, k, :], m.bank[k % 8][:, 0:128]).then_inc(s_c, 1)
            nc.vector.tensor_tensor(m.col["b_r"], m.col["bih_r"], m.col["bhh_r"], ALU.add).then_inc(s_b, 1)
            nc.vector.tensor_tensor(m.col["b_z"], m.col["bih_z"], m.col["bhh_z"], ALU.add).then_inc(s_b, 1)
            nc.vector.tensor_tensor(rest[0][:], rest[0][:], bmsg[:], ALU.add).then_inc(s_b, 1)
            for k in range(3):
                dve.wait_ge(s_b, 3 + 2 * k)
                nc.vector.tensor_copy(piece[k][:], rest[k][:]).then_inc(s_b, 1)
                if k < 2:
                    dve.wait_ge(s_b, 4 + 2 * k)
                    nc.vector.tensor_tensor(rest[k + 1][:], rest[k][:], piece[k][:], ALU.subtract).then_inc(s_b, 1)
    early.close()



class Phase:

    def __init__(self, m, name):
        self.m, self.name, self.stack, self.used = m, name, ExitStack(), []

    def sb(self, name, shape, dt=F32):
        return self.stack.enter_context(self.m.nc.sbuf_tensor(f"{self.name}_{name}", shape, dt))

    def slots(self, name, shape, dt=F32, count=4):
        return [self.sb(f"{name}_{k}", shape, dt) for k in range(count)]

    def sem(self, name):
        self.used.append(self.m.nc.alloc_semaphore(f"{self.name}_{name}"))
        return self.used[-1]

    def sems(self, name, count=4):
        return [self.sem(f"{name}_{k}") for k in range(count)]

    def __enter__(self):
        return self

    def __exit__(self, *err):
        self.stack.close()
        self.m.nc.clear_and_free_semaphores(self.used)
        self.m.nc.all_engine_barrier()


class Flow:

    def __init__(self, eng, has, m=None):
        self.eng, self.has, self.m = eng, has, m

    def wait(self, sem, value):
        if self.m is None or isinstance(value, int):
            self.eng.wait_ge(sem, value)
        else:
            self.m.hold(self.eng, sem, value)

    def after(self, sem, g):
        if self.has(g):
            self.wait(sem, g + 1)

    def landed(self, sems, g, v, per=16):
        if self.has(g):
            self.wait(sems[v % 4], (g - v % 4) * (per // 4) + per)


def edge_rows(table, i):
    return table[bass.ds(i * EG, EG), :].rearrange("(c p) f -> p c f", p=EP)


def finish(eng, sems, n, per=16):
    for v in range(4):
        if len(range(v, n, 4)):
            eng.wait_ge(sems[v], per * len(range(v, n, 4)))


class DenseFirst:
    def __init__(self, nc, m, a, P, first_group, n):
        N = m.N
        x_dram = a["x"]
        sb, groups = P.sb, -(-N // ROWS)
        last_chunk = first_group + n == groups
        x = [sb(f"x{k}", [128, TILE, D]) for k in range(4)]
        xb = [sb(f"xb{k}", [128, TILE, D]) for k in range(4)]
        n1 = [sb(f"n1_{k}", [128, TILE, D]) for k in range(2)]
        n2 = [sb(f"n2_{k}", [128, TILE, D]) for k in range(2)]
        h0T = [sb(f"h0T{k}", [128, ROWS]) for k in range(2)]
        a1T = [sb(f"a1T{k}", [128, ROWS]) for k in range(2)]
        a2T = [sb(f"a2T{k}", [128, ROWS]) for k in range(2)]
        hT = [sb(f"hT{k}", [128, ROWS]) for k in range(2)]
        xg = [sb(f"xg{k}", [128, TILE, 2 * D]) for k in range(4)]
        st = [sb(f"st{k}", [128, 8, 6]) for k in range(2)]
        mv = [sb(f"mv{k}", [128, 8, 2]) for k in range(2)]
        sd = [sb(f"sd{k}", [128, 8]) for k in range(2)]
        rs = [sb(f"rs{k}", [128, 8]) for k in range(2)]
        nb = [sb(f"nb{k}", [128, 8]) for k in range(2)]
        pT1, pA, pB, pC, pG, pT2 = m.bank[0:6]

        s_x = P.sems("d1_x_in")
        s_st = P.sems("d1_xg_out")
        s_xb, s_n1, s_n2 = P.sem("d1_xb"), P.sem("d1_n1"), P.sem("d1_n2")
        s_T1, s_A, s_B, s_C, s_G, s_T2 = (P.sem("d1_" + k) for k in ("T1", "A", "B", "C", "G", "T2"))
        s_h0, s_a1, s_a2, s_h, s_g = (P.sem("d1_" + k) for k in ("h0T", "a1T", "a2T", "hT", "g"))
        s_x1, s_sd, s_dv, s_mv = P.sem("d1_x1"), P.sem("d1_sd"), P.sem("d1_dve"), P.sem("d1_mv")
        FIRST, LAST = -3, n + 2

        def base_of(g):
            return min((first_group + g) * ROWS, N - ROWS) if isinstance(g, int) else (first_group + g) * ROWS

        def sync(sp):
            def body(i, u, has):
                if has(i + 3):
                    if has(i - 1):
                        sp.wait_ge(s_n1, i)
                        sp.wait_ge(s_xb, i)
                    v = (u + 3) % 4
                    sp.dma_start(x[v][:], x_dram[bass.ds(base_of(i + 3), ROWS), :].rearrange("(p j) f -> p j f", j=TILE))\
                      .then_inc(s_x[v], 16)
                if has(i - 3):
                    v = (u + 1) % 4
                    sp.wait_ge(s_g, i - 2)
                    sp.wait_ge(s_x1, i - 2)
                    lo = 0
                    if last_chunk and isinstance(i, int) and i - 3 == n - 1:
                        lo = ((groups - 1) * ROWS - (N - ROWS)) // TILE
                    sp.dma_start(m.XG[bass.ds(base_of(i - 3) + lo * TILE, ROWS - lo * TILE), :].rearrange("(p j) f -> p j f", j=TILE),
                                 xg[v][lo:128, :, :]).then_inc(s_st[v], 16)

            return FIRST, n, LAST, 1, body

        def stored(sp):
            finish(sp, s_st, n)

        def vector(dve):
            def body(i, u, has):
                p, q = u % 2, (u + 1) % 2
                if has(i + 1) or has(i - 2):
                    dve.wait_ge(s_sd, i + 2)
                    if has(i - 4):
                        dve.wait_ge(s_n2, i - 3)
                    nc.vector.reciprocal(rs[q][:], sd[q][:]).then_inc(s_dv, 1)
                    dve.wait_ge(s_dv, 2 * (i + 2) + 1)
                    nc.vector.scalar_tensor_tensor(nb[q][:], mv[q][:, :, 0], -1.0, rs[q][:], ALU.mult, ALU.mult).then_inc(s_dv, 1)
                    dve.wait_ge(s_dv, 2 * (i + 2) + 2)
                if has(i + 1):
                    if has(i - 1):
                        dve.wait_ge(s_T1, i)
                    for j in range(TILE):
                        last = nc.vector.tensor_scalar(n1[q][:, j, :], x[(u + 1) % 4][:, j, :], rs[q][:, 4 + j:5 + j],
                                                       nb[q][:, 4 + j:5 + j], ALU.mult, ALU.add)
                    last.then_inc(s_n1, 1)
                if has(i - 1):
                    v = (u + 3) % 4
                    dve.wait_ge(s_C, i)
                    dve.wait_ge(s_xb, i)
                    if has(i - 5):
                        dve.wait_ge(s_st[v], slot_value(i - 5, v))
                    nc.vector.tensor_tensor(xg[v][:, :, 0:D], pC[:].rearrange("p (j f) -> p j f", j=TILE), xb[v][:], ALU.add)\
                      .then_inc(s_x1, 1)
                    dve.wait_ge(s_x1, i)
                if has(i + 2):
                    dve.wait_ge(s_x[(u + 2) % 4], slot_value(i + 2, (u + 2) % 4))
                for j in range(TILE):
                    if has(i - 1):
                        last = nc.vector.bn_stats(st[p][:, j, :], xg[(u + 3) % 4][:, j, 0:D])
                    if has(i + 2):
                        last = nc.vector.bn_stats(st[p][:, 4 + j, :], x[(u + 2) % 4][:, j, :])
                if has(i - 1) or has(i + 2):
                    last.then_inc(s_mv, 1)
                    m.hold(dve, s_mv, 2 * (i + 2) + 1)
                    for j in range(8):
                        if has(i - 1) if j < 4 else has(i + 2):
                            last = nc.vector.bn_aggr(mv[p][:, j, :], st[p][:, j, :])
                    last.then_inc(s_mv, 1)

            def setup():
                nc.vector.memset(mv[0][:], 1.0).then_inc(s_dv, 1)
                nc.vector.memset(mv[1][:], 1.0).then_inc(s_dv, 1)
                dve.wait_ge(s_dv, 2)

            setup()
            return FIRST + 1, n, LAST, 1, body

        def scalar(act):
            def evac(out, in_, func, ready, g, sem, **kw):
                act.wait_ge(ready, g + 1)
                nc.scalar.activation(out, in_, func, **kw).then_inc(sem, 1)

            def body(i, u, has):
                p = u % 2
                if has(i):
                    if has(i - 2):
                        act.wait_ge(s_A, i - 1)
                    evac(h0T[p][:], pT1[:], ACT.Relu, s_T1, i, s_h0)
                    if has(i - 2):
                        act.wait_ge(s_B, i - 1)
                    evac(a1T[p][:], pA[:], ACT.Relu, s_A, i, s_a1, bias=m.col["b1"])
                if has(i - 2):
                    if has(i - 4):
                        act.wait_ge(s_T2, i - 3)
                    act.wait_ge(s_dv, 2 * (i + 2) + 2)
                    q = (u + 1) % 2
                    for j in range(TILE):
                        last = nc.scalar.activation(n2[p][:, j, :], xg[(u + 2) % 4][:, j, 0:D], ACT.Relu, scale=rs[q][:, j:j + 1],
                                                    bias=nb[q][:, j:j + 1])
                    last.then_inc(s_n2, 1)
                if has(i - 3):
                    act.wait_ge(s_x1, i - 2)
                    evac(xg[(u + 1) % 4][:, :, D:2 * D], pG[:].rearrange("p (j f) -> p j f", j=TILE), ACT.Copy,
                         s_G, i - 3, s_g, scale=1.0 / 3.0)
                if has(i):
                    if has(i - 2):
                        act.wait_ge(s_C, i - 1)
                    evac(a2T[p][:], pB[:], ACT.Relu, s_B, i, s_a2, bias=m.col["b2"])
                if has(i - 2):
                    if has(i - 4):
                        act.wait_ge(s_G, i - 3)
                    evac(hT[p][:], pT2[:], ACT.Copy, s_T2, i - 2, s_h)
                if has(i - 1) or has(i + 2):
                    act.wait_ge(s_mv, 2 * (i + 3))
                    nc.scalar.activation(sd[p][:], mv[p][:, :, 1], ACT.Sqrt, bias=m.col["eps"]).then_inc(s_sd, 1)

            return FIRST + 1, n, LAST, 1, body

        def gpsimd(pool):
            def body(i, u, has):
                if has(i + 2):
                    v = (u + 2) % 4
                    if has(i - 2):
                        pool.wait_ge(s_x1, i - 1)
                    pool.wait_ge(s_x[v], slot_value(i + 2, v))
                    nc.gpsimd.tensor_tensor(xb[v][:], x[v][:], m.b3row[:].unsqueeze(1).to_broadcast([128, TILE, D]), ALU.add)\
                      .then_inc(s_xb, 1)

            return FIRST + 1, n, LAST, 1, body

        def tensor(pe):
            def body(i, u, has):
                p, q = u % 2, (u + 1) % 2
                if has(i):
                    pe.wait_ge(s_n1, i + 1)
                    if has(i - 1):
                        pe.wait_ge(s_h0, i)
                    for j in range(TILE):
                        last = nc.tensor.transpose(pT1[:, j * 128:(j + 1) * 128], n1[p][:, j, :], m.ident[:])
                    last.then_inc(s_T1, 1)
                if has(i - 1):
                    pe.wait_ge(s_a2, i)
                    if has(i - 2):
                        pe.wait_ge(s_x1, i - 1)
                    for j in range(TILE):
                        last = nc.tensor.matmul(pC[:, j * D:(j + 1) * D], a2T[q][:, j * 128:(j + 1) * 128], m.w["self3"],
                                                start=True, stop=True)
                    last.then_inc(s_C, 1)
                if has(i):
                    pe.wait_ge(s_h0, i + 1)
                    if has(i - 1):
                        pe.wait_ge(s_a1, i)
                    nc.tensor.matmul(pA[:], m.w["self1"], h0T[p][:], start=True, stop=True).then_inc(s_A, 1)
                if has(i - 3):
                    pe.wait_ge(s_h, i - 2)
                    if has(i - 4):
                        pe.wait_ge(s_g, i - 3)
                    for j in range(TILE):
                        last = nc.tensor.matmul(pG[:, j * D:(j + 1) * D], hT[q][:, j * 128:(j + 1) * 128], m.w["S"],
                                                start=True, stop=True)
                    last.then_inc(s_G, 1)
                if has(i):
                    pe.wait_ge(s_a1, i + 1)
                    if has(i - 1):
                        pe.wait_ge(s_a2, i)
                    nc.tensor.matmul(pB[:], m.w["self2"], a1T[p][:], start=True, stop=True).then_inc(s_B, 1)
                if has(i - 2):
                    pe.wait_ge(s_n2, i - 1)
                    if has(i - 3):
                        pe.wait_ge(s_h, i - 2)
                    for j in range(TILE):
                        last = nc.tensor.transpose(pT2[:, j * 128:(j + 1) * 128], n2[p][:, j, :], m.ident[:])
                    last.then_inc(s_T2, 1)

            return FIRST + 1, n, LAST, 1, body

        self.sync, self.vector, self.scalar, self.gpsimd, self.tensor, self.stored = sync, vector, scalar, gpsimd, tensor, stored


def beside(nc, m, a, P, chunk, sync=None, vector=None, gpsimd=None, tensor=None, sync_once=None, sync_end=None, vector_end=None,
           gpsimd_end=None):
    groups = -(-m.N // ROWS)
    first = chunk * groups // CHUNKS
    dense = DenseFirst(nc, m, a, P, first, (chunk + 1) * groups // CHUNKS - first)

    def sweeps(eng, own, other):
        together(eng, [own(eng)] + ([other(eng)] if other else []), back=7, ahead=3)

    with nc.Block() as block:
        @block.sync
        def _(sp):
            if sync_once:
                sync_once(sp)
            sweeps(sp, dense.sync, sync)
            dense.stored(sp)
            if sync_end:
                sync_end(sp)

        @block.vector
        def _(dve):
            sweeps(dve, dense.vector, vector)
            if vector_end:
                vector_end(dve)

        @block.scalar
        def _(act):
            sweeps(act, dense.scalar, None)

        @block.gpsimd
        def _(pool):
            sweeps(pool, dense.gpsimd, gpsimd)
            if gpsimd_end:
                gpsimd_end(pool)

        @block.tensor
        def _(pe):
            sweeps(pe, dense.tensor, tensor)


def order_edges(nc, m, a):
    E = m.E
    T = E // EP
    n = T // TILE
    SPAN = E // EP
    PIECE = E // 5
    COPIES = 10
    tables = {k: nc.dram_tensor("sorted_" + k, [E, 1], I32, kind="Internal").ap() for k in ("dst", "src", "edge_type_9")}
    m.edge = {k: t.rearrange("e o -> (e o)") for k, t in tables.items()}
    m.edge["ea"] = nc.dram_tensor("sorted_edge_attr", [E, D], F32, kind="Internal").ap()
    m.ea_copied = 16 * COPIES
    m.s_ea = m.nc.alloc_semaphore("edge_attr_copied")
    with Phase(m, "order") as P:
        d, late = P.sb("keys", [EP, SPAN], I32), P.sb("descents", [EP, SPAN])
        b, blate = P.sb("borders", [EP - 1, 2], I32), P.sb("border_descents", [EP - 1, 1])
        total, flag = P.sb("descents_of_row", [EP, 1]), P.sb("unsorted", [1, 1], I32)
        s_d, s_v, s_t, s_c = P.sem("keys"), P.sem("dve"), P.sem("pe"), P.sem("copied")
        with nc.Block() as block:
            @block.sync
            def _(sp):
                sp.dma_start(d[:], a["dst"].rearrange("(p t) -> p t", p=EP)).then_inc(s_d, 16)
                sp.dma_start(b[:], a["dst"][SPAN - 1:SPAN - 1 + (EP - 1) * SPAN].rearrange("(p t) -> p t", t=SPAN)[:, 0:2]).then_inc(s_d, 16)
                for k in ("dst", "src", "edge_type_9"):
                    sp.dma_start(m.edge[k].rearrange("(p t) -> p t", p=EP), a[k].rearrange("(p t) -> p t", p=EP)).then_inc(s_c, 16)
                for k in range(COPIES):
                    r = slice(k * E // COPIES, (k + 1) * E // COPIES)
                    sp.dma_start(m.edge["ea"][r, :], a["edge_attr_128"][r, :]).then_inc(m.s_ea, 16)
                sp.wait_ge(s_c, 48)

            @block.vector
            def _(dve):
                dve.wait_ge(s_d, 32)
                nc.vector.tensor_tensor(late[:, 0:SPAN - 1], d[:, 1:SPAN], d[:, 0:SPAN - 1], ALU.is_lt).then_inc(s_v, 1)
                nc.vector.tensor_tensor(blate[:], b[:, 1:2], b[:, 0:1], ALU.is_lt).then_inc(s_v, 1)
                dve.wait_ge(s_v, 2)
                nc.vector.tensor_reduce(total[:], late[:, 0:SPAN - 1], op=ALU.add, axis=AX.X).then_inc(s_v, 1)
                dve.wait_ge(s_t, 1)
                nc.vector.tensor_scalar(flag[:], m.bank[0][0:1, 0:1], 1.0, None, ALU.min).then_inc(s_v, 1)
                dve.wait_ge(s_v, 4)

            @block.tensor
            def _(pe):
                pe.wait_ge(s_v, 3)
                nc.tensor.matmul(m.bank[0][0:1, 0:1], total[:], m.ones[0:EP, 0:1], start=True, stop=False)
                nc.tensor.matmul(m.bank[0][0:1, 0:1], blate[:], m.ones[0:EP - 1, 0:1], start=False, stop=True).then_inc(s_t, 1)

        unsorted = nc.values_load(flag[0:1, 0:1], min_val=0, max_val=1)
        keys, less = P.sb("all_keys", [EP, E]), P.sb("less", [EP, PIECE])
        raw = P.sb("raw_keys", [EP, PIECE], I32)
        cols = {k: P.sb("column_" + k, [EP, T], I32) for k in ("dst", "src", "edge_type_9")}
        kcol = P.sb("key_columns", [EP, T])
        earlier = P.sb("earlier", [EP, EP])
        part, rank, rank_i = P.sb("rank_parts", [EP, 6]), P.sb("rank", [EP, T]), P.sb("rank_i", [EP, T], I32)
        idx = P.sb("idx", [EP, TILE], I32)
        word = {k: P.sb("words_" + k, [EP, TILE], I32) for k in tables}
        ea = P.sb("ea", [EP, TILE, D])
        s_l, s_r, s_k, s_p, s_q, s_a, s_e, s_o = (P.sem("r_" + k) for k in ("cols", "raw", "keys", "ones", "rank", "all", "ea", "out"))
        s_w = P.sem("r_words")
        with nc.Block() as block:
            @block.sync
            def _(sp):
                with sp.If(unsorted > 0):
                    sp.wait_ge(m.s_ea, 16 * COPIES)
                    for k in tables:
                        sp.dma_start(cols[k][:], a[k].rearrange("(p t) -> p t", p=EP)).then_inc(s_l, 16)
                    for c in range(5):
                        if c:
                            sp.wait_ge(s_k, c)
                        sp.dma_start(raw[:], a["dst"][c * PIECE:(c + 1) * PIECE].rearrange("(a n) -> a n", a=1).to_broadcast([EP, PIECE]))\
                          .then_inc(s_r, 16)
                    with sp.Fori(0, n) as i:
                        sp.wait_ge(s_w, i * 2 + 1)
                        sp.dma_start(ea[:], a["edge_attr_128"].rearrange("(p t) f -> p t f", t=T)[:, bass.ds(i * TILE, TILE), :]).then_inc(s_e, 16)

            @block.vector
            def _(dve):
                with dve.If(unsorted > 0):
                    dve.wait_ge(s_p, 2)
                    dve.wait_ge(s_l, 16 * 3)
                    nc.vector.tensor_copy(kcol[:], cols["dst"][:])
                    for c in range(5):
                        dve.wait_ge(s_r, 16 * (c + 1))
                        nc.vector.tensor_copy(keys[:, c * PIECE:(c + 1) * PIECE], raw[:]).then_inc(s_k, 1)
                    dve.wait_ge(s_k, 5)
                    by_column = keys[:].rearrange("q (p t) -> q p t", t=T)
                    with dve.Fori(0, T) as t:
                        tc = bass.ds(t, 1)
                        own = by_column[:, :, tc].rearrange("q p o -> q (p o)")
                        for c in range(5):
                            nc.vector.tensor_scalar(less[:], keys[:, c * PIECE:(c + 1) * PIECE], kcol[:, tc], None, ALU.is_lt, ALU.add,
                                                    accum_out=part[:, c:c + 1]).then_inc(s_q, 1)
                            dve.wait_ge(s_q, t * 8 + c + 1)
                        nc.vector.scalar_tensor_tensor(less[:, 0:EP], own, kcol[:, tc], earlier[:], ALU.is_equal, ALU.mult,
                                                       accum_out=part[:, 5:6]).then_inc(s_q, 1)
                        dve.wait_ge(s_q, t * 8 + 6)
                        nc.vector.tensor_reduce(rank[:, tc], part[:], op=ALU.add, axis=AX.X).then_inc(s_q, 1)
                        nc.vector.tensor_scalar(own, own, -0.5, None, ALU.add).then_inc(s_q, 1)
                        dve.wait_ge(s_q, t * 8 + 8)
                    nc.vector.tensor_copy(rank_i[:], rank[:]).then_inc(s_a, 1)

            @block.gpsimd
            def _(pool):
                with pool.If(unsorted > 0):
                    nc.gpsimd.memset(earlier[:], 1.0).then_inc(s_p, 1)
                    pool.wait_ge(s_p, 1)
                    nc.gpsimd.affine_select(out=earlier[:], in_=earlier[:], compare_op=ALU.is_gt, fill=0.0, base=0,
                                            pattern=[[-1, EP]], channel_multiplier=1).then_inc(s_p, 1)
                    pool.wait_ge(s_a, 1)
                    with pool.Fori(0, n) as i:
                        nc.gpsimd.memset(idx[:], 0).then_inc(s_w, 1)
                        m.hold(pool, s_w, i * 2 + 1)
                        nc.gpsimd.tensor_copy(idx[:], rank_i[:, bass.ds(i * TILE, TILE)]).then_inc(s_a, 1)
                        for k in tables:
                            nc.gpsimd.tensor_copy(word[k][:], cols[k][:, bass.ds(i * TILE, TILE)]).then_inc(s_a, 1)
                        m.hold(pool, s_a, i * 4 + 5)
                        m.hold(pool, s_e, i * 16 + 16)
                        for c in range(TILE):
                            to = bass.IndirectOffsetOnAxis(ap=idx[:, c:c + 1], axis=0)
                            for k, table in tables.items():
                                pool.indirect_dma_start(out=table, out_offset=to, in_=word[k][:, c:c + 1], in_offset=None).then_inc(s_o, 16)
                            pool.indirect_dma_start(out=m.edge["ea"], out_offset=to, in_=ea[:, c, :], in_offset=None).then_inc(s_o, 16)
                        m.hold(pool, s_o, i * 256 + 256)
                        nc.gpsimd.memset(idx[:], 0).then_inc(s_w, 1)
                        m.hold(pool, s_w, i * 2 + 2)


def edges_setup(nc, m, a):
    N, E = m.N, m.E
    T = E // EP
    TC = T // 2
    LOW = 256
    NH = -(-N // LOW)
    BIG = float(1 << 22)
    m.T, m.TC = T, TC
    m.kext = m.sb("dst_keys", [128, T])
    m.inv_d = m.sb("inverse_degree_dst", [128, T])
    m.inv_s = m.sb("inverse_degree_src", [128, T])
    m.ind = m.sb("first_last_indicators", [128, T, 2])
    m.M1 = [m.sb(f"earlier_tiles{c}", [TC, T]) for c in range(2)]
    m.M2 = [m.sb(f"later_tiles{c}", [TC, T]) for c in range(2)]
    m.csrc = m.sb("src_keys", [EP, T])
    m.ccorr = m.sb("edges_in_other_tiles", [EP, T])
    m.before = m.sb("before", [EP, TILE, EG])
    m.i_src = m.sb("i_src", [EP, T], I32)
    m.i_dst = m.sb("i_dst", [EP, T], I32)
    m.i_src2 = m.sb("i_src2", [EP, T], I32)
    m.i_dst2f = m.sb("i_dst2f", [EP, T], I32)
    m.i_dst2f1 = m.sb("i_dst2f1", [EP, T], I32)
    m.i_dstf = m.sb("i_dstf", [EP, T], I32)
    m.i_tb = m.sb("i_tb", [EP, T], I32)
    m.i_src2f1 = m.sb("i_src2f1", [EP, T], I32)
    m.i_srcf = m.sb("i_srcf", [EP, T], I32)
    m.VT = nc.dram_tensor("values", [T * 128, D], F32, kind="Internal").ap()
    m.XD = nc.dram_tensor("x_of_dst", [E, D], F32, kind="Internal").ap()
    m.H1 = nc.dram_tensor("h1_of_dst", [E, D], F32, kind="Internal").ap()
    m.LT = nc.dram_tensor("leaving_values", [E, D], F32, kind="Internal").ap()
    m.TB1 = nc.dram_tensor("layer1_rows", [2 * E, D], F32, kind="Internal").ap()
    m.TB2 = nc.dram_tensor("layer2_rows", [2 * E, D], F32, kind="Internal").ap()
    m.HDa = nc.dram_tensor("hidden_a", [T // TILE * 128, EG], F32, kind="Internal").ap()
    m.HDb = nc.dram_tensor("hidden_b", [T // TILE * 128, EG], F32, kind="Internal").ap()
    m.KD = nc.dram_tensor("keys_dst", [T, EP], F32, kind="Internal").ap()
    m.KS = nc.dram_tensor("keys_src", [T, EP], F32, kind="Internal").ap()
    m.KT = nc.dram_tensor("keys_type", [T, EP], F32, kind="Internal").ap()
    NODES = nc.dram_tensor("degree_and_position", [LOW * NH, 2], F32, kind="Internal").ap()

    keep = ExitStack()

    def sb(name, shape, dt=F32):
        return keep.enter_context(nc.sbuf_tensor("es_" + name, shape, dt))

    ri = [[sb(f"r_{k}{c}", [TC, EP], I32) for c in range(2)] for k in ("dst", "src", "typ", "prev")]
    rf = [[sb(f"f_{k}{c}", [TC, EP]) for c in range(2)] for k in ("dst", "src", "typ", "prev")]
    notfirst = [sb(f"notfirst{c}", [TC, EP]) for c in range(2)]
    corr = [sb(f"corr{c}", [TC, EP]) for c in range(2)]
    corr2 = [sb(f"corrb{c}", [TC, EP]) for c in range(2)]
    ish = [sb(f"ish{c}", [TC, EP]) for c in range(2)]
    ist = [sb(f"ist{c}", [TC, EP]) for c in range(2)]
    hcnt = [sb(f"hcnt{c}", [TC, 1]) for c in range(2)]
    lcnt = [sb(f"lcnt{c}", [TC, 1]) for c in range(2)]
    pq = [sb(f"pq{c}", [TC, 2]) for c in range(2)]
    headT = [sb(f"head{c}", [TC, TC]) for c in range(2)]
    tailT = [sb(f"tail{c}", [TC, TC]) for c in range(2)]
    cdst, cnf = (sb(k, [EP, T]) for k in ("cdst", "cnf"))
    ccorr, before = m.ccorr, m.before
    csrc = m.csrc
    total = sb("total", [EP, T])
    t1, t2, t3 = (sb(k, [EP, T]) for k in ("t1", "t2", "t3"))
    posf, epos = sb("posf", [EP, T]), sb("epos", [EP, T])
    tb = sb("tb", [EP, T])
    lo_i, hi_i = sb("lo_i", [EP, T], I32), sb("hi_i", [EP, T], I32)
    lo_f, hi_f = sb("lo_f", [EP, T]), sb("hi_f", [EP, T])
    i_row, i_position = sb("i_row", [EP, T], I32), sb("i_position", [EP, T], I32)
    dhi_i, dlo_i, dhi_f, dlo_f = sb("dhi_i", [EP, T], I32), sb("dlo_i", [EP, T], I32), sb("dhi_f", [EP, T]), sb("dlo_f", [EP, T])
    io_lo, io_hi = sb("io_lo", [128, LOW]), sb("io_hi", [128, NH])
    oh_lo = [sb(f"oh_lo{k}", [EP, TILE, LOW], BF16) for k in range(2)]
    oh_hi = [sb(f"oh_hi{k}", [EP, TILE, NH], BF16) for k in range(2)]
    hist = sb("hist", [128, 2, NH])
    nodes = sb("nodes", [128, 2, NH, 2])
    n = T // TILE

    s_ld = m.sem("es_ld")
    s_p, s_v, s_t, s_st = m.sem("es_pool"), m.sem("es_dve"), m.sem("es_pe"), m.sem("es_out")
    s_ms = m.sem("es_nodes")
    V_MASKS = 30
    ccr = [sb(f"ccr{c}", [TC, EP]) for c in range(2)]
    c_pos = [sb(f"c_pos{k}", [EP, TILE]) for k in range(4)]
    with nc.Block() as block:
        @block.sync
        def _(sp):
            for c in range(2):
                for k, name in enumerate(("dst", "src", "edge_type_9")):
                    sp.dma_start(ri[k][c][:], m.edge[name].rearrange("(t p) -> t p", p=EP)[c * TC:(c + 1) * TC, :]).then_inc(s_ld, 16)
            sp.wait_ge(s_p, 1)
            flat = m.edge["dst"]
            sp.dma_start(ri[3][0][0:1, 1:EP], flat[0:EP - 1].rearrange("(a n) -> a n", a=1)).then_inc(s_ld, 16)
            sp.dma_start(ri[3][0][1:TC, :], flat[EP - 1:EP - 1 + (TC - 1) * EP].rearrange("(t p) -> t p", p=EP)).then_inc(s_ld, 16)
            sp.dma_start(ri[3][1][:, :], flat[TC * EP - 1:TC * EP - 1 + TC * EP].rearrange("(t p) -> t p", p=EP)).then_inc(s_ld, 16)
            sp.wait_ge(s_v, 8)
            for c in range(2):
                for k, table in ((0, m.KD), (1, m.KS), (2, m.KT)):
                    sp.dma_start(table[c * TC:(c + 1) * TC, :], rf[k][c][:]).then_inc(s_st, 16)
            sp.wait_ge(s_st, 16 * 6)

        @block.gpsimd
        def _(pool):
            nc.gpsimd.memset(ri[3][0][0:1, :], -1).then_inc(s_p, 1)
            nc.gpsimd.memset(nodes[:], -1.0).then_inc(s_ms, 1)
            nc.gpsimd.iota(posf[:], [[EP, T]], base=0, channel_multiplier=1, allow_small_or_imprecise_dtypes=True).then_inc(s_p, 1)
            nc.gpsimd.iota(epos[:], [[EP, T]], base=E, channel_multiplier=1, allow_small_or_imprecise_dtypes=True).then_inc(s_p, 1)
            nc.gpsimd.iota(io_lo[:], [[1, LOW]], base=0, channel_multiplier=0, allow_small_or_imprecise_dtypes=True).then_inc(s_p, 1)
            nc.gpsimd.iota(io_hi[:], [[1, NH]], base=0, channel_multiplier=0, allow_small_or_imprecise_dtypes=True).then_inc(s_p, 1)
            nc.gpsimd.memset(before[:], 1.0).then_inc(s_p, 1)
            nc.gpsimd.memset(m.kext[:], -5.0).then_inc(s_p, 1)
            nc.gpsimd.memset(m.inv_d[:], 0.0).then_inc(s_p, 1)
            nc.gpsimd.memset(m.ind[:], 0.0).then_inc(s_p, 1)
            pool.wait_ge(s_p, 9)
            for c in range(TILE):
                nc.gpsimd.affine_select(out=before[:, c, :], in_=before[:, c, :], compare_op=ALU.is_gt, fill=0.0,
                                        base=c * EP, pattern=[[-1, EG]], channel_multiplier=1).then_inc(s_p, 1)
            pool.wait_ge(s_v, V_MASKS)
            for c in range(2):
                nc.gpsimd.affine_select(out=m.M1[c][:], in_=m.M1[c][:], compare_op=ALU.is_gt, fill=0.0,
                                        base=-c * TC, pattern=[[1, T]], channel_multiplier=-1).then_inc(s_p, 1)
                nc.gpsimd.affine_select(out=m.M2[c][:], in_=m.M2[c][:], compare_op=ALU.is_gt, fill=0.0,
                                        base=c * TC, pattern=[[-1, T]], channel_multiplier=1).then_inc(s_p, 1)

        @block.vector
        def _(dve):
            dve.wait_ge(s_ld, 16 * 9)
            for k in range(4):
                for c in range(2):
                    if k == 2:
                        nc.vector.tensor_scalar(rf[k][c][:], ri[k][c][:], 0.0, TYPES - 1.0, ALU.max, ALU.min).then_inc(s_v, 1)
                    else:
                        nc.vector.tensor_copy(rf[k][c][:], ri[k][c][:]).then_inc(s_v, 1)
            dve.wait_ge(s_v, 8)
            for c in range(2):
                nc.vector.tensor_tensor(notfirst[c][:], rf[0][c][:], rf[3][c][:], ALU.is_equal).then_inc(s_v, 1)
                nc.vector.tensor_scalar(ish[c][:], rf[0][c][:], rf[0][c][:, 0:1], None, ALU.is_equal).then_inc(s_v, 1)
                nc.vector.tensor_scalar(ist[c][:], rf[0][c][:], rf[0][c][:, EP - 1:EP], None, ALU.is_equal).then_inc(s_v, 1)
                dve.wait_ge(s_v, 8 + 5 * c + 3)
                nc.vector.tensor_reduce(hcnt[c][:], ish[c][:], op=ALU.add, axis=AX.X).then_inc(s_v, 1)
                nc.vector.tensor_reduce(lcnt[c][:], ist[c][:], op=ALU.add, axis=AX.X).then_inc(s_v, 1)
            dve.wait_ge(s_t, 4)
            for c in range(2):
                nc.vector.tensor_copy(headT[c][:], m.bank[c][0:TC, 0:TC]).then_inc(s_v, 1)
                nc.vector.tensor_copy(tailT[c][:], m.bank[2 + c][0:TC, 0:TC]).then_inc(s_v, 1)
            dve.wait_ge(s_v, 22)
            for c in range(2):
                for d in range(2):
                    nc.vector.tensor_scalar(m.M1[c][:, d * TC:(d + 1) * TC], headT[d][:], rf[0][c][:, EP - 1:EP], None, ALU.is_equal).then_inc(s_v, 1)
                    nc.vector.tensor_scalar(m.M2[c][:, d * TC:(d + 1) * TC], tailT[d][:], rf[0][c][:, 0:1], None, ALU.is_equal).then_inc(s_v, 1)
            dve.wait_ge(s_t, 6)
            for c in range(2):
                nc.vector.tensor_copy(pq[c][:], m.bank[4 + c][0:TC, 0:2]).then_inc(s_v, 1)
            dve.wait_ge(s_v, 32)
            for c in range(2):
                nc.vector.tensor_scalar(corr[c][:], ish[c][:], pq[c][:, 0:1], None, ALU.mult).then_inc(s_v, 1)
                nc.vector.tensor_scalar(corr2[c][:], ist[c][:], pq[c][:, 1:2], None, ALU.mult).then_inc(s_v, 1)
            dve.wait_ge(s_v, 36)
            for c in range(2):
                nc.vector.tensor_tensor(ccr[c][:], corr[c][:], corr2[c][:], ALU.add).then_inc(s_v, 1)
            dve.wait_ge(s_t, 7)
            b = m.bank[0]
            cols = (cdst, csrc, cnf, ccorr)
            for k in range(4):
                nc.vector.tensor_copy(cols[k][:], m.bank[k][0:EP, 0:T]).then_inc(s_v, 1)
            dve.wait_ge(s_p, 9)
            nc.vector.tensor_copy(m.kext[0:EP, :], m.bank[0][0:EP, 0:T]).then_inc(s_v, 1)
            for k in range(2):
                nc.vector.tensor_copy(m.ind[0:EP, :, k], m.bank[4 + k][0:EP, 0:T]).then_inc(s_v, 1)
            dve.wait_ge(s_v, 45)
            nc.vector.tensor_copy(m.i_src[:], csrc[:]).then_inc(s_v, 1)
            nc.vector.tensor_copy(m.i_dst[:], cdst[:]).then_inc(s_v, 1)
            nc.vector.tensor_scalar(m.i_src2[:], csrc[:], 2.0, None, ALU.mult).then_inc(s_v, 1)
            nc.vector.tensor_scalar(t1[:], cnf[:], BIG, None, ALU.mult).then_inc(s_v, 1)
            dve.wait_ge(s_v, 49)
            nc.vector.tensor_tensor(m.i_dstf[:], cdst[:], t1[:], ALU.add).then_inc(s_v, 1)
            nc.vector.scalar_tensor_tensor(t2[:], cdst[:], 2.0, t1[:], ALU.mult, ALU.add).then_inc(s_v, 1)
            dve.wait_ge(s_v, 51)
            nc.vector.tensor_copy(m.i_dst2f[:], t2[:]).then_inc(s_v, 1)
            nc.vector.tensor_scalar(m.i_dst2f1[:], t2[:], 1.0, None, ALU.add).then_inc(s_v, 1)
            nc.vector.tensor_scalar(hi_i[:], m.i_src[:], 8, None, ALU.logical_shift_right).then_inc(s_v, 1)
            nc.vector.tensor_scalar(lo_i[:], m.i_src[:], LOW - 1, None, ALU.bitwise_and).then_inc(s_v, 1)
            dve.wait_ge(s_v, 55)
            nc.vector.tensor_copy(hi_f[:], hi_i[:]).then_inc(s_v, 1)
            nc.vector.tensor_copy(lo_f[:], lo_i[:]).then_inc(s_v, 1)
            dve.wait_ge(s_v, 57)
            nc.vector.scalar_tensor_tensor(i_row[:], lo_f[:], float(NH), hi_f[:], ALU.mult, ALU.add).then_inc(s_v, 1)
            nc.vector.tensor_scalar(dhi_i[:], m.i_dst[:], 8, None, ALU.logical_shift_right).then_inc(s_v, 1)
            nc.vector.tensor_scalar(dlo_i[:], m.i_dst[:], LOW - 1, None, ALU.bitwise_and).then_inc(s_v, 1)
            dve.wait_ge(s_v, 60)
            nc.vector.tensor_copy(dhi_f[:], dhi_i[:]).then_inc(s_v, 1)
            nc.vector.tensor_copy(dlo_f[:], dlo_i[:]).then_inc(s_v, 1)
            dve.wait_ge(s_v, 62)
            nc.vector.scalar_tensor_tensor(t3[:], dlo_f[:], float(NH), dhi_f[:], ALU.mult, ALU.add).then_inc(s_v, 1)
            dve.wait_ge(s_v, 63)
            nc.vector.scalar_tensor_tensor(t2[:], t3[:], 2.0, t1[:], ALU.mult, ALU.add).then_inc(s_v, 1)
            dve.wait_ge(s_v, 64)
            nc.vector.tensor_scalar(i_position[:], t2[:], 1.0, None, ALU.add).then_inc(s_v, 1)

        @block.tensor
        def _(pe):
            pe.wait_ge(s_v, 18)
            for c in range(2):
                nc.tensor.matmul(m.bank[c][0:TC, 0:TC], rf[0][c][:, 0:1].to_broadcast([TC, TC]), m.ident[0:TC, 0:TC],
                                 start=True, stop=True).then_inc(s_t, 1)
                nc.tensor.matmul(m.bank[2 + c][0:TC, 0:TC], rf[0][c][:, EP - 1:EP].to_broadcast([TC, TC]), m.ident[0:TC, 0:TC],
                                 start=True, stop=True).then_inc(s_t, 1)
            pe.wait_ge(s_p, 17)
            for c in range(2):
                cs = slice(c * TC, (c + 1) * TC)
                for k, (mask, cnt) in enumerate(((m.M1, lcnt), (m.M2, hcnt))):
                    nc.tensor.matmul(m.bank[4 + c][0:TC, k:k + 1], mask[0][:, cs], cnt[0][:], start=True, stop=False)
                    last = nc.tensor.matmul(m.bank[4 + c][0:TC, k:k + 1], mask[1][:, cs], cnt[1][:], start=False, stop=True)
                last.then_inc(s_t, 1)
            pe.wait_ge(s_v, 38)
            for k, rows in enumerate((rf[0], rf[1], notfirst, ccr, ish, ist)):
                for c in range(2):
                    last = nc.tensor.transpose(m.bank[k][0:EP, c * TC:(c + 1) * TC], rows[c][:], m.ident[0:TC, 0:TC])
            last.then_inc(s_t, 1)

    s_oh, s_hm, s_c = m.sem("es_onehot"), m.sem("es_hist"), m.sem("es_chain")
    c_dst = [sb(f"i_pos{k}", [EP, TILE], I32) for k in range(4)]
    with nc.Block() as block:
        @block.vector
        def _(dve):
            def body(i, u, has):
                f = Flow(dve, has)
                p = u % 2
                f.after(s_hm, i - 2)
                for c in range(TILE):
                    t = bass.ds(i * TILE + c, 1)
                    nc.vector.tensor_scalar(oh_lo[p][:, c, :], io_lo[0:EP, :], lo_f[:, t], None, ALU.is_equal)
                    last = nc.vector.tensor_scalar(oh_hi[p][:, c, :], io_hi[0:EP, :], hi_f[:, t], None, ALU.is_equal)
                last.then_inc(s_oh, 1)

            sweep(dve, 0, n, n - 1, body, back=4, ahead=0, special=0)
            dve.wait_ge(s_hm, n)
            for h in range(2):
                nc.vector.tensor_scalar(hist[:, h, :], m.bank[h][:, 0:NH], 1.0, None, ALU.max).then_inc(s_c, 1)
            dve.wait_ge(s_c, 2)
            nc.vector.reciprocal(nodes[:, :, :, 0], hist[:]).then_inc(s_c, 1)

        @block.tensor
        def _(pe):
            def body(i, u, has):
                f = Flow(pe, has)
                p = u % 2
                f.after(s_oh, i)
                for c in range(TILE):
                    first = isinstance(i, int) and i == 0 and c == 0
                    end = isinstance(i, int) and i == n - 1 and c == TILE - 1
                    for h in range(2):
                        last = nc.tensor.matmul(m.bank[h][:, 0:NH], oh_lo[p][:, c, h * 128:(h + 1) * 128], oh_hi[p][:, c, :],
                                                start=first, stop=end, skip_group_check=True)
                last.then_inc(s_hm, 1)

            sweep(pe, 0, n, n - 1, body, back=4, ahead=0, special=1)

    with Phase(m, "positions") as P:
        s_ext, s_pi, s_pg = P.sem("rows_125_126"), P.sem("idx"), P.sems("stored")

        def store_positions(pool):
            def body(i, u, has):
                if isinstance(i, int) and i == 0:
                    pool.wait_ge(s_ext, 16 * 3)
                f = Flow(pool, has, m)
                f.landed(s_pg, i - 4, u, 64)
                nc.gpsimd.tensor_copy(c_dst[u][:], i_position[:, bass.ds(i * TILE, TILE)]).then_inc(s_pi, 1)
                nc.gpsimd.tensor_copy(c_pos[u][:], posf[:, bass.ds(i * TILE, TILE)]).then_inc(s_pi, 1)
                f.wait(s_pi, i * 2 + 2)
                for c in range(TILE):
                    pool.indirect_dma_start(out=NODES.rearrange("n (k o) -> (n k) o", o=1),
                                            out_offset=bass.IndirectOffsetOnAxis(ap=c_dst[u][:, c:c + 1], axis=0),
                                            in_=c_pos[u][:, c:c + 1], in_offset=None, bounds_check=2 * LOW * NH - 1, oob_is_err=False)\
                        .then_inc(s_pg[u], 16)

            return 0, n, n - 1, 0, body

        def fill(sp):
            sp.dma_start(NODES.rearrange("(h p a) k -> p h (a k)", h=2, p=128), nodes[:].rearrange("p h a k -> p h (a k)")).then_inc(s_ext, 16)
            sp.dma_start(m.kext[EP:EP + 1, :], m.kext[0:1, :]).then_inc(s_ext, 16)
            sp.dma_start(m.kext[EP + 1:EP + 2, :], m.kext[EP - 1:EP, :]).then_inc(s_ext, 16)

        beside(nc, m, a, P, 0, gpsimd=store_positions, gpsimd_end=lambda pool: finish(pool, s_pg, n, 64), sync_once=fill,
               sync_end=lambda sp: sp.wait_ge(s_ext, 16 * 3))

    with Phase(m, "lookup") as P:
        s_i2, s_lk, s_cp, s_f = P.sem("idx"), P.sems("got"), P.sem("copied"), P.sem("table_rows")
        got = P.slots("row", [EP, TILE, 2])

        def look_up(pool):
            def body(i, u, has):
                f = Flow(pool, has, m)
                f.after(s_cp, i - 4)
                gather(nc, pool, f, i_row, c_dst, s_i2, i, u, NODES, got, s_lk)

            return 0, n, n - 1, 0, body

        def copy(dve):
            def body(i, u, has):
                if has(i - 1):
                    v = (u - 1) % 4
                    f = Flow(dve, has)
                    f.landed(s_lk, i - 1, v, 64)
                    nc.vector.tensor_copy(tb[:, bass.ds((i - 1) * TILE, TILE)], got[v][:, :, 1])
                    nc.vector.tensor_copy(m.inv_s[0:EP, bass.ds((i - 1) * TILE, TILE)], got[v][:, :, 0]).then_inc(s_cp, 1)

            return 1, n, n, 0, body

        def table_rows(dve):
            dve.wait_ge(s_cp, n)
            nc.vector.tensor_scalar(t2[:], tb[:], -0.5, None, ALU.is_gt).then_inc(s_f, 1)
            nc.vector.tensor_tensor(t3[:], tb[:], epos[:], ALU.subtract).then_inc(s_f, 1)
            dve.wait_ge(s_f, 2)
            nc.vector.tensor_tensor(total[:], t2[:], t3[:], ALU.mult).then_inc(s_f, 1)
            dve.wait_ge(s_f, 3)
            nc.vector.tensor_tensor(m.i_tb[:], total[:], epos[:], ALU.add).then_inc(s_f, 1)

        beside(nc, m, a, P, 1, vector=copy, vector_end=table_rows, gpsimd=look_up)
    keep.close()


def gather(nc, pool, f, index, idx, s_idx, i, u, table, rows, landed):
    nc.gpsimd.tensor_copy(idx[u][:], index[:, bass.ds(i * TILE, TILE)]).then_inc(s_idx, 1)
    f.after(s_idx, i)
    for c in range(TILE):
        pool.indirect_dma_start(out=rows[u][0:EP, c, :], out_offset=None, in_=table,
                                in_offset=bass.IndirectOffsetOnAxis(ap=idx[u][:, c:c + 1], axis=0)).then_inc(landed[u], 16)


def scatter(nc, pool, f, index, idx, s_idx, i, u, table, rows, landed, add=False):
    nc.gpsimd.tensor_copy(idx[u][:], index[:, bass.ds(i * TILE, TILE)]).then_inc(s_idx, 1)
    f.after(s_idx, i)
    if add:
        f.landed(landed, i - 1, u - 1, 64)
    for c in range(TILE):
        pool.indirect_dma_start(out=table, out_offset=bass.IndirectOffsetOnAxis(ap=idx[u][:, c:c + 1], axis=0),
                                in_=rows[u][0:EP, c, :], in_offset=None, bounds_check=table.shape[0] - 1, oob_is_err=False,
                                **({"compute_op": ALU.add} if add else {})).then_inc(landed[u], 16)


def value_tiles(m, i):
    return m.VT[bass.ds(i * TILE * 128, TILE * 128), :].rearrange("(c p) f -> p c f", p=128)


def turned(table, i):
    return table[bass.ds(i * 128, 128), :]


def first_last_sums(nc, m, V, i):
    for c in range(TILE):
        last = nc.tensor.matmul(m.bank[7][:, bass.ds((i * TILE + c) * 2, 2)], V[0:EP, c, :],
                                m.ind[0:EP, bass.ds(i * TILE + c, 1), :].rearrange("p a k -> p (a k)"),
                                start=True, stop=True, skip_group_check=True)
    return last


def share_segments(nc, m, name):
    TC, T = m.TC, m.T
    with Phase(m, name) as P:
        HL = P.sb("first_last", [128, 2, T])
        X = [[P.sb(f"rows{k}{c}", [TC, D]) for c in range(2)] for k in range(2)]
        R = [[P.sb(f"shared{k}{c}", [TC, D]) for c in range(2)] for k in range(2)]
        s_hl, s_t, s_x, s_m, s_r, s_out = (P.sem(k) for k in ("hl", "turned", "rows", "summed", "shared", "out"))
        with nc.Block() as block:
            @block.vector
            def _(dve):
                nc.vector.tensor_copy(HL[:].rearrange("p k t -> p t k"), m.bank[7][:, 0:2 * T].rearrange("p (t k) -> p t k", k=2))\
                  .then_inc(s_hl, 1)
                for k in range(2):
                    for c in range(2):
                        dve.wait_ge(s_t, 2 * k + c + 1)
                        nc.vector.tensor_copy(X[k][c][:], m.bank[2 * k + c][0:TC, 0:D]).then_inc(s_x, 1)
                for k in range(2):
                    for c in range(2):
                        dve.wait_ge(s_m, 2 * k + c + 1)
                        nc.vector.tensor_copy(R[k][c][:], m.bank[4 * (1 - k) + c][0:TC, 0:D]).then_inc(s_r, 1)

            @block.tensor
            def _(pe):
                pe.wait_ge(s_hl, 1)
                for k in range(2):
                    for c in range(2):
                        nc.tensor.transpose(m.bank[2 * k + c][0:TC, 0:D], HL[:, k, c * TC:(c + 1) * TC], m.ident[:]).then_inc(s_t, 1)
                pe.wait_ge(s_x, 4)
                for k, masks in ((0, m.M1), (1, m.M2)):
                    for c in range(2):
                        for e in range(2):
                            last = nc.tensor.matmul(m.bank[4 * (1 - k) + c][0:TC, 0:D], masks[e][:, c * TC:(c + 1) * TC],
                                                    X[1 - k][e][:], start=(e == 0), stop=(e == 1), skip_group_check=True)
                        last.then_inc(s_m, 1)

            @block.sync
            def _(sp):
                table = m.VT.rearrange("(t p) f -> t p f", p=128)
                for k in range(2):
                    for c in range(2):
                        sp.wait_ge(s_r, 2 * k + c + 1)
                        sp.dma_start(table[c * TC:(c + 1) * TC, EP + k, :], R[k][c][:]).then_inc(s_out, 16)
                sp.wait_ge(s_out, 64)


class Norm:

    def __init__(self, nc, m, P, tiles, name="ln"):
        self.nc, self.m, self.tiles = nc, m, tiles
        self.st = P.slots(name + "_st", [128, tiles, 6])
        self.mv = P.slots(name + "_mv", [128, tiles, 2])
        self.sd = P.slots(name + "_sd", [128, tiles])
        self.rs = P.slots(name + "_rs", [128, tiles])
        self.nb = P.slots(name + "_nb", [128, tiles])
        self.s_st, self.s_mv, self.s_sd, self.s_rs, self.s_nb = (P.sem(f"{name}_{k}") for k in ("st", "mv", "sd", "rs", "nb"))

    def stats(self, dve, f, i, v, rows, np_=EP):
        nc = self.nc
        for j, r in enumerate(rows):
            last = nc.vector.bn_stats(self.st[v][0:np_, j, :], r)
        last.then_inc(self.s_st, 1)
        Flow(dve, f.has, self.m).after(self.s_st, i)
        for j in range(self.tiles):
            last = nc.vector.bn_aggr(self.mv[v][0:np_, j, :], self.st[v][0:np_, j, :])
        last.then_inc(self.s_mv, 1)

    def root(self, f, i, v, np_=EP):
        f.after(self.s_mv, i)
        self.nc.scalar.activation(self.sd[v][0:np_, :], self.mv[v][0:np_, :, 1], ACT.Sqrt, bias=self.m.col["eps"][0:np_, :])\
            .then_inc(self.s_sd, 1)

    def finish(self, f, i, v, np_=EP):
        nc = self.nc
        f.after(self.s_sd, i)
        nc.vector.reciprocal(self.rs[v][0:np_, :], self.sd[v][0:np_, :]).then_inc(self.s_rs, 1)
        f.after(self.s_rs, i)
        nc.vector.scalar_tensor_tensor(self.nb[v][0:np_, :], self.mv[v][0:np_, :, 0], -1.0, self.rs[v][0:np_, :], ALU.mult, ALU.mult)\
            .then_inc(self.s_nb, 1)

    def relu(self, out, rows, v, first=0, np_=EP):
        for j, r in enumerate(rows):
            k = first + j
            last = self.nc.scalar.activation(out[0:np_, j, :], r, ACT.Relu, scale=self.rs[v][0:np_, k:k + 1],
                                             bias=self.nb[v][0:np_, k:k + 1])
        return last


def edges_start(nc, m, a):
    n, E = m.T // TILE, m.E
    with Phase(m, "A") as P:
        idx_s, idx_d = P.slots("idx_s", [EP, TILE], I32), P.slots("idx_d", [EP, TILE], I32)
        xs, xd = P.slots("x_src", [EP, TILE, D]), P.slots("x_dst", [EP, TILE, D])
        hs, hd = P.slots("h_src", [EP, TILE, D]), P.slots("h_dst", [EP, TILE, D])
        hsT, hdT = P.slots("h_srcT", [128, EG]), P.slots("h_dstT", [128, EG])
        a1T, a2T = P.slots("a1T", [128, EG]), P.slots("a2T", [128, EG])
        a1, a2 = P.slots("a1", [EP, TILE, D]), P.slots("a2", [EP, TILE, D])
        ln = Norm(nc, m, P, 2 * TILE)
        krow, srow, hits = P.slots("krow", [EP, EG]), P.slots("srow", [EP, EG]), P.sb("hits", [EP, TILE, EG])
        khits = P.sb("khits", [EP, EG])
        within, seen, total, t2, t3 = (P.sb(k, [EP, m.T]) for k in ("within", "seen", "total", "t2", "t3"))
        s_kr, s_sr, s_c, s_fin, s_ext = P.sems("krow"), P.sems("srow"), P.sem("counts"), P.sem("finish"), P.sem("ext")
        s_is, s_id, s_gs, s_gd = P.sem("idx_s"), P.sem("idx_d"), P.sems("got_src"), P.sems("got_dst")
        s_xo, s_vo, s_ho, s_1o, s_2o = (P.sems(k) for k in ("xd_out", "v_out", "hd_out", "a1_out", "a2_out"))
        s_h, s_T, s_hsT, s_hdT, s_hl = (P.sem(k) for k in ("h", "T", "hsT", "hdT", "firstlast"))
        s_m1, s_a1T, s_m2, s_a2T, s_b1, s_a1, s_b2, s_a2 = (P.sem(k) for k in ("m1", "a1T", "m2", "a2T", "b1", "a1", "b2", "a2"))
        bS, bD, b1, b2, r1, r2 = m.bank[0:6]
        with nc.Block() as block:
            @block.gpsimd
            def _(pool):
                def body(i, u, has):
                    f = Flow(pool, has, m)
                    f.after(s_h, i - 4)
                    f.landed(s_xo, i - 4, u)
                    gather(nc, pool, f, m.i_src, idx_s, s_is, i, u, a["x"], xs, s_gs)
                    gather(nc, pool, f, m.i_dst, idx_d, s_id, i, u, a["x"], xd, s_gd)

                sweep(pool, 0, n, n - 1, body, back=4, ahead=0, special=0)

            @block.sync
            def _(sp):
                def load(f, i, u):
                    if f.has(i - 4):
                        f.wait(s_c, (i - 3) * 2 * TILE)
                    kd = m.KD.rearrange("t p -> (t p)")[bass.ds(i * EG, EG)].rearrange("(a n) -> a n", a=1)
                    ks = m.KS.rearrange("t p -> (t p)")[bass.ds(i * EG, EG)].rearrange("(a n) -> a n", a=1)
                    sp.dma_start(krow[u][:], kd.to_broadcast([EP, EG])).then_inc(s_kr[u], 16)
                    sp.dma_start(srow[u][:], ks.to_broadcast([EP, EG])).then_inc(s_sr[u], 16)

                def body(i, u, has):
                    f = Flow(sp, has)
                    if has(i + 3):
                        load(f, i + 3, (u + 3) % 4)
                    if has(i):
                        f.landed(s_gd, i, u, 64)
                        sp.dma_start(edge_rows(m.XD, i), xd[u][:]).then_inc(s_xo[u], 16)
                    if has(i - 1):
                        v = (u - 1) % 4
                        f.after(s_h, i - 1)
                        sp.dma_start(value_tiles(m, i - 1)[0:EP], hs[v][:]).then_inc(s_vo[v], 16)
                    if has(i - 2):
                        v = (u - 2) % 4
                        f.after(s_hdT, i - 2)
                        sp.dma_start(turned(m.HDa, i - 2), hdT[v][:]).then_inc(s_ho[v], 16)
                    if has(i - 4):
                        v = u
                        f.after(s_a1, i - 4)
                        sp.dma_start(edge_rows(m.TB1[E:2 * E, :], i - 4), a1[v][:]).then_inc(s_1o[v], 16)
                    if has(i - 5):
                        v = (u - 5) % 4
                        f.after(s_a2, i - 5)
                        sp.dma_start(edge_rows(m.TB2[E:2 * E, :], i - 5), a2[v][:]).then_inc(s_2o[v], 16)

                sweep(sp, -3, n, n + 4, body, back=5, ahead=3, special=0)
                sp.wait_ge(s_fin, 6)
                sp.dma_start(m.inv_d[EP:EP + 1, :], m.inv_d[0:1, :]).then_inc(s_ext, 16)
                sp.dma_start(m.inv_d[EP + 1:EP + 2, :], m.inv_d[EP - 1:EP, :]).then_inc(s_ext, 16)
                sp.wait_ge(s_ext, 32)
                for sems in (s_xo, s_vo, s_ho, s_1o, s_2o):
                    finish(sp, sems, n)

            @block.vector
            def _(dve):
                def body(i, u, has):
                    f = Flow(dve, has)
                    if has(i):
                        f.landed(s_gs, i, u, 64)
                        f.landed(s_gd, i, u, 64)
                        ln.stats(dve, f, i, u, [t[u][:, c, :] for t in (xs, xd) for c in range(TILE)])
                    if has(i - 1):
                        ln.finish(f, i - 1, (u - 1) % 4)
                    if has(i):
                        f.landed(s_kr, i, u)
                        f.landed(s_sr, i, u)
                        if has(i - 1):
                            f.wait(s_c, i * 2 * TILE)
                        for c in range(TILE):
                            t = bass.ds(i * TILE + c, 1)
                            cs, e = slice(c * EP, (c + 1) * EP), (c + 1) * EP
                            nc.vector.tensor_scalar(khits[:, cs], krow[u][:, cs], m.kext[0:EP, t], None, ALU.is_equal, ALU.add,
                                                    accum_out=within[:, t]).then_inc(s_c, 1)
                            nc.vector.scalar_tensor_tensor(hits[:, c, 0:e], srow[u][:, 0:e], m.csrc[:, t], m.before[:, c, 0:e],
                                                           ALU.is_equal, ALU.mult, accum_out=seen[:, t]).then_inc(s_c, 1)
                    if has(i - 2):
                        v = (u - 2) % 4
                        f.after(s_T, i - 2)
                        f.landed(s_ho, i - 6, v)
                        nc.vector.tensor_copy(hdT[v][:], bD[:, 0:EG]).then_inc(s_hdT, 1)
                    if has(i - 4):
                        f.after(s_b1, i - 4)
                        f.landed(s_1o, i - 8, u)
                        nc.vector.tensor_copy(a1[u][:], r1[0:EP, :].rearrange("p (c f) -> p c f", c=TILE)).then_inc(s_a1, 1)
                    if has(i - 5):
                        v = (u - 5) % 4
                        f.after(s_b2, i - 5)
                        f.landed(s_2o, i - 9, v)
                        nc.vector.tensor_copy(a2[v][:], r2[0:EP, :].rearrange("p (c f) -> p c f", c=TILE)).then_inc(s_a2, 1)

                sweep(dve, 0, n, n + 4, body, back=9, ahead=0, special=0)
                dve.wait_ge(s_c, 2 * TILE * n)
                nc.vector.tensor_tensor(total[:], within[:], m.ccorr[:], ALU.add).then_inc(s_fin, 1)
                nc.vector.tensor_scalar(t3[:], seen[:], 0.5, float(1 << 22), ALU.is_gt, ALU.mult).then_inc(s_fin, 1)
                dve.wait_ge(s_fin, 2)
                nc.vector.reciprocal(m.inv_d[0:EP, :], total[:]).then_inc(s_fin, 1)
                nc.vector.tensor_tensor(m.i_srcf[:], m.csrc[:], t3[:], ALU.add).then_inc(s_fin, 1)
                nc.vector.scalar_tensor_tensor(t2[:], m.csrc[:], 2.0, t3[:], ALU.mult, ALU.add).then_inc(s_fin, 1)
                dve.wait_ge(s_fin, 5)
                nc.vector.tensor_scalar(m.i_src2f1[:], t2[:], 1.0, None, ALU.add).then_inc(s_fin, 1)

            @block.scalar
            def _(act):
                def body(i, u, has):
                    f = Flow(act, has)
                    if has(i):
                        ln.root(f, i, u)
                    if has(i - 1):
                        v = (u - 1) % 4
                        f.after(ln.s_nb, i - 1)
                        f.after(s_T, i - 5)
                        f.after(s_hl, i - 5)
                        f.landed(s_vo, i - 5, v)
                        ln.relu(hs[v], [xs[v][:, c, :] for c in range(TILE)], v)
                        ln.relu(hd[v], [xd[v][:, c, :] for c in range(TILE)], v, TILE).then_inc(s_h, 1)
                    if has(i - 2):
                        v = (u - 2) % 4
                        f.after(s_T, i - 2)
                        f.after(s_m1, i - 6)
                        nc.scalar.activation(hsT[v][:], bS[:, 0:EG], ACT.Copy).then_inc(s_hsT, 1)
                    if has(i - 3):
                        v = (u - 3) % 4
                        f.after(s_m1, i - 3)
                        f.after(s_b1, i - 7)
                        nc.scalar.activation(a1T[v][:], b1[:, 0:EG], ACT.Relu, bias=m.col["b1"]).then_inc(s_a1T, 1)
                    if has(i - 4):
                        f.after(s_m2, i - 4)
                        f.after(s_b2, i - 8)
                        nc.scalar.activation(a2T[u][:], b2[:, 0:EG], ACT.Relu, bias=m.col["b2"]).then_inc(s_a2T, 1)

                sweep(act, 0, n, n + 3, body, back=8, ahead=0, special=0)

            @block.tensor
            def _(pe):
                def body(i, u, has):
                    f = Flow(pe, has)
                    if has(i - 4):
                        f.after(s_a1T, i - 4)
                        f.after(s_a2T, i - 5)
                        nc.tensor.matmul(b2[:, 0:EG], m.w["self2"], a1T[u][:], start=True, stop=True).then_inc(s_m2, 1)
                    if has(i - 3):
                        f.after(s_hsT, i - 3)
                        f.after(s_a1T, i - 4)
                        nc.tensor.matmul(b1[:, 0:EG], m.w["self1"], hsT[(u - 3) % 4][:], start=True, stop=True).then_inc(s_m1, 1)
                    if has(i - 2):
                        v = (u - 2) % 4
                        f.after(s_h, i - 2)
                        f.after(s_hsT, i - 3)
                        f.after(s_hdT, i - 3)
                        first_last_sums(nc, m, hs[v], i - 2).then_inc(s_hl, 1)
                        for c in range(TILE):
                            nc.tensor.transpose(bS[:, c * EP:(c + 1) * EP], hs[v][:, c, :], m.ident[0:EP, 0:EP])
                            last = nc.tensor.transpose(bD[:, c * EP:(c + 1) * EP], hd[v][:, c, :], m.ident[0:EP, 0:EP])
                        last.then_inc(s_T, 1)
                    if has(i - 4):
                        f.after(s_a1, i - 5)
                        for c in range(TILE):
                            last = nc.tensor.transpose(r1[0:EP, c * D:(c + 1) * D], a1T[u][:, c * EP:(c + 1) * EP], m.ident[:])
                        last.then_inc(s_b1, 1)
                    if has(i - 5):
                        f.after(s_a2T, i - 5)
                        f.after(s_a2, i - 6)
                        for c in range(TILE):
                            last = nc.tensor.transpose(r2[0:EP, c * D:(c + 1) * D], a2T[(u - 5) % 4][:, c * EP:(c + 1) * EP], m.ident[:])
                        last.then_inc(s_b2, 1)

                sweep(pe, 0, n, n + 4, body, back=6, ahead=0, special=0)
    share_segments(nc, m, "A_shared")


def sum_loads(sp, m, f, i, u, V, krow, s_V, s_k, s_sel, s_agg):
    f.after(s_agg, i - 4)
    sp.dma_start(V[u][:], value_tiles(m, i)[0:EP + 2]).then_inc(s_V[u], 16)
    f.after(s_sel, i - 4)
    keys = m.KD.rearrange("t p -> (t p)")[bass.ds(i * EG, EG)].rearrange("(a n) -> a n", a=1)
    sp.dma_start(krow[u][:], keys.to_broadcast([EP + 2, EG])).then_inc(s_k[u], 16)


def selectors(nc, m, f, i, u, krow, S, s_k, s_sel, s_agg, mean=True):
    f.landed(s_k, i, u)
    f.after(s_agg, i - 4)
    for c in range(TILE):
        t = bass.ds(i * TILE + c, 1)
        cs = slice(c * EP, (c + 1) * EP)
        if mean:
            last = nc.vector.tensor_scalar(S[u][:, cs], krow[u][:, cs], m.kext[0:EP + 2, t], m.inv_d[0:EP + 2, t], ALU.is_equal, ALU.mult)
        else:
            last = nc.vector.tensor_scalar(S[u][:, cs], krow[u][:, cs], m.kext[0:EP + 2, t], None, ALU.is_equal)
    last.then_inc(s_sel, 1)


def add_up(nc, m, f, i, u, V, S, bank, s_V, s_sel, s_agg):
    f.landed(s_V, i, u)
    f.after(s_sel, i)
    for c in range(TILE):
        cs = slice(c * EP, (c + 1) * EP)
        last = nc.tensor.matmul(bank[:, cs], V[u][:, c, :], S[u][:, cs], start=True, stop=True)
    last.then_inc(s_agg, 1)


def layer(nc, m, k, H_in, H_out, table):
    n = m.T // TILE
    with Phase(m, f"B{k}") as P:
        V, krow, S = P.slots("V", [EP + 2, TILE, D]), P.slots("krow", [EP + 2, EG]), P.slots("S", [EP + 2, EG])
        h, agg, o, rows = P.slots("h", [128, EG]), P.slots("agg", [128, EG]), P.slots("o", [128, EG]), P.slots("rows", [EP, TILE, D])
        s_V, s_k, s_h, s_oo, s_ro = (P.sems(x) for x in ("V", "k", "h", "o_out", "rows_out"))
        s_sel, s_agg, s_ac, s_m, s_o, s_T, s_r = (P.sem(x) for x in ("sel", "agg", "aggcopy", "m", "o", "T", "r"))
        with nc.Block() as block:
            @block.sync
            def _(sp):
                def load(f, i, u):
                    sum_loads(sp, m, f, i, u, V, krow, s_V, s_k, s_sel, s_agg)
                    f.after(s_m, i - 4)
                    sp.dma_start(h[u][:], turned(H_in, i)).then_inc(s_h[u], 16)

                def body(i, u, has):
                    f = Flow(sp, has)
                    if has(i + 3):
                        load(f, i + 3, (u + 3) % 4)
                    if has(i - 3):
                        v = (u - 3) % 4
                        f.after(s_o, i - 3)
                        sp.dma_start(turned(H_out, i - 3), o[v][:]).then_inc(s_oo[v], 16)
                        f.after(s_r, i - 3)
                        sp.dma_start(edge_rows(table, i - 3), rows[v][:]).then_inc(s_ro[v], 16)

                sweep(sp, -3, n, n + 2, body, back=4, ahead=3, special=0)
                finish(sp, s_oo, n)
                finish(sp, s_ro, n)

            @block.vector
            def _(dve):
                def body(i, u, has):
                    f = Flow(dve, has)
                    if has(i + 1):
                        selectors(nc, m, f, i + 1, (u + 1) % 4, krow, S, s_k, s_sel, s_agg)
                    if has(i - 2):
                        v = (u - 2) % 4
                        f.after(s_T, i - 2)
                        f.landed(s_ro, i - 6, v)
                        nc.vector.tensor_copy(rows[v][:], m.bank[4 + v % 2][0:EP, :].rearrange("p (c f) -> p c f", c=TILE)).then_inc(s_r, 1)

                sweep(dve, -1, n, n + 1, body, back=6, ahead=1, special=0)

            @block.scalar
            def _(act):
                def body(i, u, has):
                    f = Flow(act, has)
                    if has(i):
                        f.after(s_agg, i)
                        f.after(s_m, i - 4)
                        nc.scalar.activation(agg[u][:], m.bank[u % 2][:, 0:EG], ACT.Copy).then_inc(s_ac, 1)
                    if has(i - 1):
                        v = (u - 1) % 4
                        f.after(s_m, i - 1)
                        f.after(s_T, i - 5)
                        f.landed(s_oo, i - 5, v)
                        nc.scalar.activation(o[v][:], m.bank[2 + v % 2][:, 0:EG], ACT.Relu, bias=m.col[f"b{k}"]).then_inc(s_o, 1)

                sweep(act, 0, n, n, body, back=5, ahead=0, special=0)

            @block.tensor
            def _(pe):
                def body(i, u, has):
                    f = Flow(pe, has)
                    if has(i):
                        f.after(s_ac, i - 2)
                        add_up(nc, m, f, i, u, V, S, m.bank[u % 2], s_V, s_sel, s_agg)
                    if has(i - 1):
                        v = (u - 1) % 4
                        f.landed(s_h, i - 1, v)
                        f.after(s_ac, i - 1)
                        f.after(s_o, i - 3)
                        nc.tensor.matmul(m.bank[2 + v % 2][:, 0:EG], m.w[f"self{k}"], h[v][:], start=True, stop=False)
                        nc.tensor.matmul(m.bank[2 + v % 2][:, 0:EG], m.w[f"neigh{k}"], agg[v][:], start=False, stop=True).then_inc(s_m, 1)
                    if has(i - 2):
                        v = (u - 2) % 4
                        f.after(s_o, i - 2)
                        f.after(s_r, i - 4)
                        for c in range(TILE):
                            last = nc.tensor.transpose(m.bank[4 + v % 2][0:EP, c * D:(c + 1) * D], o[v][:, c * EP:(c + 1) * EP], m.ident[:])
                        last.then_inc(s_T, 1)

                sweep(pe, 0, n, n + 1, body, back=4, ahead=0, special=0)


def take(nc, m, a, k, table, chunk):
    n = m.T // TILE
    with Phase(m, f"G{k}") as P:
        idx, V = P.slots("idx", [EP, TILE], I32), P.slots("V", [EP, TILE, D])
        s_i, s_g, s_vo, s_hl = P.sem("idx"), P.sems("got"), P.sems("v_out"), P.sem("firstlast")

        def gpsimd(pool):
            def body(i, u, has):
                f = Flow(pool, has, m)
                f.landed(s_vo, i - 4, u)
                f.after(s_hl, i - 4)
                gather(nc, pool, f, m.i_tb, idx, s_i, i, u, table, V, s_g)

            return 0, n, n - 1, 0, body

        def sync(sp):
            def body(i, u, has):
                if has(i - 1):
                    f = Flow(sp, has)
                    v = (u - 1) % 4
                    f.landed(s_g, i - 1, v, 64)
                    sp.dma_start(value_tiles(m, i - 1)[0:EP], V[v][:]).then_inc(s_vo[v], 16)

            return 1, n, n, 0, body

        def tensor(pe):
            def body(i, u, has):
                if has(i - 1):
                    f = Flow(pe, has)
                    f.landed(s_g, i - 1, u - 1, 64)
                    first_last_sums(nc, m, V[(u - 1) % 4], i - 1).then_inc(s_hl, 1)

            return 1, n, n, 0, body

        beside(nc, m, a, P, chunk, sync=sync, gpsimd=gpsimd, tensor=tensor, sync_end=lambda sp: finish(sp, s_vo, n))
    share_segments(nc, m, f"G{k}_shared")


def third_layer(nc, m, a):
    n = m.T // TILE
    with Phase(m, "B3") as P:
        V, krow, S = P.slots("V", [EP + 2, TILE, D]), P.slots("krow", [EP + 2, EG]), P.slots("S", [EP + 2, EG])
        h, agg = P.slots("h", [128, EG]), P.slots("agg", [128, EG])
        xd, xb, x1, h1 = (P.slots(x, [EP, TILE, D]) for x in ("xd", "xb", "x1", "h1"))
        h1T = P.slots("h1T", [128, EG])
        idx = P.slots("idx", [EP, TILE], I32)
        ln = Norm(nc, m, P, TILE)
        s_V, s_k, s_h, s_x, s_ho, s_To, s_sc = (P.sems(x) for x in ("V", "k", "h", "x", "h1_out", "h1T_out", "x1_out"))
        s_sel, s_agg, s_ac, s_m, s_xb, s_x1, s_h1, s_T, s_hT, s_i = \
            (P.sem(x) for x in ("sel", "agg", "aggcopy", "m", "xb", "x1", "h1", "T", "h1T", "idx"))
        with nc.Block() as block:
            @block.sync
            def _(sp):
                def load(f, i, u):
                    sum_loads(sp, m, f, i, u, V, krow, s_V, s_k, s_sel, s_agg)
                    f.after(s_m, i - 4)
                    sp.dma_start(h[u][:], turned(m.HDa, i)).then_inc(s_h[u], 16)
                    f.after(s_xb, i - 4)
                    sp.dma_start(xd[u][:], edge_rows(m.XD, i)).then_inc(s_x[u], 16)

                def body(i, u, has):
                    f = Flow(sp, has)
                    if has(i + 3):
                        load(f, i + 3, (u + 3) % 4)
                    if has(i - 4):
                        f.after(s_h1, i - 4)
                        sp.dma_start(edge_rows(m.H1, i - 4), h1[u][:]).then_inc(s_ho[u], 16)
                    if has(i - 5):
                        v = (u - 5) % 4
                        f.after(s_hT, i - 5)
                        sp.dma_start(turned(m.HDb, i - 5), h1T[v][:]).then_inc(s_To[v], 16)

                sweep(sp, -3, n, n + 4, body, back=5, ahead=3, special=0)
                finish(sp, s_ho, n)
                finish(sp, s_To, n)

            @block.gpsimd
            def _(pool):
                def body(i, u, has):
                    if has(i - 3):
                        f = Flow(pool, has, m)
                        f.after(s_x1, i - 3)
                        f.landed(s_sc, i - 7, u + 1, 64)
                        scatter(nc, pool, f, m.i_dst2f, idx, s_i, i - 3, (u - 3) % 4, m.XH, x1, s_sc)

                sweep(pool, 0, n, n + 2, body, back=7, ahead=0, special=0)
                finish(pool, s_sc, n, 64)

            @block.vector
            def _(dve):
                def body(i, u, has):
                    f = Flow(dve, has)
                    if has(i - 1):
                        v = (u - 1) % 4
                        f.after(s_agg, i - 1)
                        f.after(s_m, i - 5)
                        nc.vector.tensor_copy(agg[v][:], m.bank[v % 2][:, 0:EG]).then_inc(s_ac, 1)
                    if has(i + 1):
                        selectors(nc, m, f, i + 1, (u + 1) % 4, krow, S, s_k, s_sel, s_agg)
                    if has(i):
                        f.landed(s_x, i, u)
                        f.after(s_x1, i - 4)
                        nc.vector.tensor_tensor(xb[u][:], xd[u][:], m.b3row[0:EP, :].unsqueeze(1).to_broadcast([EP, TILE, D]), ALU.add)\
                          .then_inc(s_xb, 1)
                    if has(i - 3):
                        ln.finish(f, i - 3, (u - 3) % 4)
                    if has(i - 2):
                        v = (u - 2) % 4
                        f.after(s_m, i - 2)
                        f.after(s_xb, i - 2)
                        f.landed(s_sc, i - 6, v, 64)
                        f.after(s_h1, i - 6)
                        nc.vector.tensor_tensor(x1[v][:], m.bank[2 + v % 2][0:EP, :].rearrange("p (c f) -> p c f", c=TILE), xb[v][:], ALU.add)\
                          .then_inc(s_x1, 1)
                        f.after(s_x1, i - 2)
                        ln.stats(dve, f, i - 2, v, [x1[v][:, c, :] for c in range(TILE)])

                sweep(dve, -1, n, n + 2, body, back=6, ahead=1, special=0)

            @block.scalar
            def _(act):
                def body(i, u, has):
                    f = Flow(act, has)
                    if has(i - 2):
                        ln.root(f, i - 2, (u - 2) % 4)
                    if has(i - 3):
                        v = (u - 3) % 4
                        f.after(ln.s_nb, i - 3)
                        f.after(s_T, i - 7)
                        f.landed(s_ho, i - 7, v)
                        ln.relu(h1[v], [x1[v][:, c, :] for c in range(TILE)], v).then_inc(s_h1, 1)
                    if has(i - 4):
                        f.after(s_T, i - 4)
                        f.landed(s_To, i - 8, u)
                        nc.scalar.activation(h1T[u][:], m.bank[4 + u % 2][:, 0:EG], ACT.Copy).then_inc(s_hT, 1)

                sweep(act, 0, n, n + 3, body, back=8, ahead=0, special=0)

            @block.tensor
            def _(pe):
                def body(i, u, has):
                    f = Flow(pe, has)
                    if has(i):
                        f.after(s_ac, i - 2)
                        add_up(nc, m, f, i, u, V, S, m.bank[u % 2], s_V, s_sel, s_agg)
                    if has(i - 1):
                        v = (u - 1) % 4
                        f.landed(s_h, i - 1, v)
                        f.after(s_ac, i - 1)
                        f.after(s_x1, i - 3)
                        for c in range(TILE):
                            cs, o = slice(c * EP, (c + 1) * EP), m.bank[2 + v % 2][0:EP, c * D:(c + 1) * D]
                            nc.tensor.matmul(o, h[v][:, cs], m.w["self3"], start=True, stop=False)
                            last = nc.tensor.matmul(o, agg[v][:, cs], m.w["neigh3"], start=False, stop=True)
                        last.then_inc(s_m, 1)
                    if has(i - 4):
                        f.after(s_h1, i - 4)
                        f.after(s_hT, i - 6)
                        for c in range(TILE):
                            last = nc.tensor.transpose(m.bank[4 + u % 2][:, c * EP:(c + 1) * EP], h1[u][:, c, :], m.ident[0:EP, 0:EP])
                        last.then_inc(s_T, 1)

                sweep(pe, 0, n, n + 3, body, back=6, ahead=0, special=0)


def incoming(nc, m, a):
    n = m.T // TILE
    with Phase(m, "G3") as P:
        idx, x, h, V, ea = P.slots("idx", [EP, TILE], I32), *(P.slots(k, [EP, TILE, D]) for k in ("x", "h", "V", "ea"))
        ln = Norm(nc, m, P, TILE)
        s_i, s_h, s_v, s_hl = (P.sem(k) for k in ("idx", "h", "v", "firstlast"))
        s_g, s_e, s_vo = (P.sems(k) for k in ("got", "ea", "v_out"))
        with nc.Block() as block:
            @block.gpsimd
            def _(pool):
                def body(i, u, has):
                    f = Flow(pool, has, m)
                    f.after(s_h, i - 4)
                    gather(nc, pool, f, m.i_src2, idx, s_i, i, u, m.XH, x, s_g)

                sweep(pool, 0, n, n - 1, body, back=4, ahead=0, special=0)

            @block.sync
            def _(sp):
                def load(f, i, u):
                    f.after(s_v, i - 4)
                    sp.dma_start(ea[u][:], edge_rows(m.edge["ea"], i)).then_inc(s_e[u], 16)

                def body(i, u, has):
                    f = Flow(sp, has)
                    if has(i + 3):
                        load(f, i + 3, (u + 3) % 4)
                    if has(i - 3):
                        v = (u - 3) % 4
                        f.after(s_v, i - 3)
                        sp.dma_start(value_tiles(m, i - 3)[0:EP], V[v][:]).then_inc(s_vo[v], 16)

                sp.wait_ge(m.s_ea, m.ea_copied)
                sweep(sp, -3, n, n + 2, body, back=4, ahead=3, special=0)
                finish(sp, s_vo, n)

            @block.vector
            def _(dve):
                def body(i, u, has):
                    f = Flow(dve, has)
                    if has(i - 1):
                        ln.finish(f, i - 1, (u - 1) % 4)
                    if has(i):
                        f.landed(s_g, i, u, 64)
                        ln.stats(dve, f, i, u, [x[u][:, c, :] for c in range(TILE)])
                    if has(i - 2):
                        v = (u - 2) % 4
                        f.after(s_h, i - 2)
                        f.landed(s_e, i - 2, v)
                        f.landed(s_vo, i - 6, v)
                        f.after(s_hl, i - 6)
                        nc.vector.tensor_tensor(V[v][:], h[v][:], ea[v][:], ALU.subtract).then_inc(s_v, 1)

                sweep(dve, 0, n, n + 1, body, back=6, ahead=0, special=0)

            @block.scalar
            def _(act):
                def body(i, u, has):
                    f = Flow(act, has)
                    if has(i):
                        ln.root(f, i, u)
                    if has(i - 1):
                        v = (u - 1) % 4
                        f.after(ln.s_nb, i - 1)
                        f.after(s_v, i - 5)
                        ln.relu(h[v], [x[v][:, c, :] for c in range(TILE)], v).then_inc(s_h, 1)

                sweep(act, 0, n, n, body, back=5, ahead=0, special=0)

            @block.tensor
            def _(pe):
                def body(i, u, has):
                    f = Flow(pe, has)
                    f.after(s_v, i)
                    first_last_sums(nc, m, V[u], i).then_inc(s_hl, 1)

                sweep(pe, 0, n, n - 1, body, back=4, ahead=0, special=0)
    share_segments(nc, m, "G3_shared")


def outgoing_self(nc, m, a):
    n = m.T // TILE
    with Phase(m, "B4") as P:
        V, krow, S = P.slots("V", [EP + 2, TILE, D]), P.slots("krow", [EP + 2, EG]), P.slots("S", [EP + 2, EG])
        h, agg, g = P.slots("h", [128, EG]), P.slots("agg", [128, EG]), P.slots("g", [EP, TILE, D])
        idx = P.slots("idx", [EP, TILE], I32)
        s_V, s_k, s_h, s_sc = (P.sems(x) for x in ("V", "k", "h", "g_out"))
        s_sel, s_agg, s_ac, s_m, s_g, s_i = (P.sem(x) for x in ("sel", "agg", "aggcopy", "m", "g", "idx"))
        with nc.Block() as block:
            @block.sync
            def _(sp):
                def body(i, u, has):
                    f = Flow(sp, has)
                    sum_loads(sp, m, f, i, u, V, krow, s_V, s_k, s_sel, s_agg)
                    f.after(s_m, i - 4)
                    sp.dma_start(h[u][:], turned(m.HDb, i)).then_inc(s_h[u], 16)

                sweep(sp, 0, n, n - 1, body, back=4, ahead=0, special=0)

            @block.gpsimd
            def _(pool):
                def body(i, u, has):
                    f = Flow(pool, has, m)
                    f.after(s_g, i)
                    f.landed(s_sc, i - 4, u, 64)
                    scatter(nc, pool, f, m.i_dst2f1, idx, s_i, i, u, m.XH, g, s_sc)

                sweep(pool, 0, n, n - 1, body, back=4, ahead=0, special=0)
                finish(pool, s_sc, n, 64)

            @block.vector
            def _(dve):
                def body(i, u, has):
                    f = Flow(dve, has)
                    if has(i - 1):
                        v = (u - 1) % 4
                        f.after(s_agg, i - 1)
                        f.after(s_m, i - 5)
                        nc.vector.tensor_copy(agg[v][:], m.bank[v % 2][:, 0:EG]).then_inc(s_ac, 1)
                    if has(i + 1):
                        selectors(nc, m, f, i + 1, (u + 1) % 4, krow, S, s_k, s_sel, s_agg)

                sweep(dve, -1, n, n, body, back=5, ahead=1, special=0)

            @block.scalar
            def _(act):
                def body(i, u, has):
                    f = Flow(act, has)
                    f.after(s_m, i)
                    f.landed(s_sc, i - 4, u, 64)
                    nc.scalar.activation(g[u][:], m.bank[2 + u % 2][0:EP, :].rearrange("p (c f) -> p c f", c=TILE), ACT.Copy,
                                         scale=1.0 / 3.0).then_inc(s_g, 1)

                sweep(act, 0, n, n - 1, body, back=4, ahead=0, special=0)

            @block.tensor
            def _(pe):
                def body(i, u, has):
                    f = Flow(pe, has)
                    if has(i):
                        f.after(s_ac, i - 2)
                        add_up(nc, m, f, i, u, V, S, m.bank[u % 2], s_V, s_sel, s_agg)
                    if has(i - 1):
                        v = (u - 1) % 4
                        f.landed(s_h, i - 1, v)
                        f.after(s_ac, i - 1)
                        f.after(s_g, i - 3)
                        for c in range(TILE):
                            cs, o = slice(c * EP, (c + 1) * EP), m.bank[2 + v % 2][0:EP, c * D:(c + 1) * D]
                            nc.tensor.matmul(o, h[v][:, cs], m.w["S"], start=True, stop=False)
                            last = nc.tensor.matmul(o, agg[v][:, cs], m.w["O"], start=False, stop=True)
                        last.then_inc(s_m, 1)

                sweep(pe, 0, n, n, body, back=4, ahead=0, special=0)


def add_to_src(nc, m, name, load, table, index, weight=None):
    n = m.T // TILE
    with Phase(m, name) as P:
        r = P.slots("r", [EP, TILE, D])
        ea = P.slots("ea", [EP, TILE, D]) if weight else None
        val = P.slots("val", [EP, TILE, D]) if weight else r
        out = P.slots("out", [EP, TILE, D])
        krow, eq = P.slots("srow", [EP, EG]), P.slots("eq", [EP, TILE, EG])
        sumT = P.slots("sumT", [128, EG])
        idx = P.slots("idx", [EP, TILE], I32)
        s_l, s_e, s_k, s_sc = (P.sems(x) for x in ("r", "ea", "k", "out"))
        s_v, s_eq, s_m, s_sT, s_w, s_o, s_i = (P.sem(x) for x in ("val", "eq", "m", "sumT", "w", "o", "idx"))
        with nc.Block() as block:
            @block.sync
            def _(sp):
                def body(i, u, has):
                    f = Flow(sp, has)
                    f.after(s_v if weight else s_m, i - 4)
                    sp.dma_start(r[u][:], edge_rows(load, i)).then_inc(s_l[u], 16)
                    if weight:
                        sp.dma_start(ea[u][:], edge_rows(m.edge["ea"], i)).then_inc(s_e[u], 16)
                    Flow(sp, has, m).after(s_eq, i - 4)
                    keys = m.KS.rearrange("t p -> (t p)")[bass.ds(i * EG, EG)].rearrange("(a n) -> a n", a=1)
                    sp.dma_start(krow[u][:], keys.to_broadcast([EP, EG])).then_inc(s_k[u], 16)

                sweep(sp, 0, n, n - 1, body, back=4, ahead=0, special=0)

            @block.vector
            def _(dve):
                def body(i, u, has):
                    f = Flow(dve, has)
                    f.landed(s_k, i, u)
                    f.after(s_m, i - 4)
                    for c in range(TILE):
                        t = bass.ds(i * TILE + c, 1)
                        last = nc.vector.tensor_scalar(eq[u][:, c, :], krow[u][:], m.csrc[:, t], m.inv_s[0:EP, t], ALU.is_equal, ALU.mult)
                    last.then_inc(s_eq, 1)
                    if weight:
                        f.landed(s_l, i, u)
                        f.landed(s_e, i, u)
                        f.after(s_m, i - 4)
                        nc.vector.tensor_tensor(val[u][:], r[u][:], ea[u][:], ALU.subtract).then_inc(s_v, 1)

                sweep(dve, 0, n, n - 1, body, back=4, ahead=0, special=0)

            @block.tensor
            def _(pe):
                def body(i, u, has):
                    f = Flow(pe, has)
                    if has(i):
                        f.after(s_eq, i)
                        if weight:
                            f.after(s_v, i)
                            f.after(s_sT, i - 2)
                            for c in range(TILE):
                                last = nc.tensor.matmul(m.bank[u % 2][:, 0:EG], val[u][:, c, :], eq[u][:, c, :],
                                                        start=(c == 0), stop=(c == TILE - 1))
                        else:
                            f.landed(s_l, i, u)
                            f.after(s_o, i - 2)
                            for d in range(TILE):
                                for c in range(TILE):
                                    last = nc.tensor.matmul(m.bank[2 + u % 2][0:EP, d * D:(d + 1) * D], eq[u][:, c, d * EP:(d + 1) * EP],
                                                            r[u][:, c, :], start=(c == 0), stop=(c == TILE - 1))
                        last.then_inc(s_m, 1)
                    if weight and has(i - 1):
                        v = (u - 1) % 4
                        f.after(s_sT, i - 1)
                        f.after(s_o, i - 3)
                        for c in range(TILE):
                            last = nc.tensor.matmul(m.bank[2 + v % 2][0:EP, c * D:(c + 1) * D], sumT[v][:, c * EP:(c + 1) * EP],
                                                    weight, start=True, stop=True)
                        last.then_inc(s_w, 1)

                sweep(pe, 0, n, n if weight else n - 1, body, back=4, ahead=0, special=0)

            @block.scalar
            def _(act):
                def body(i, u, has):
                    f = Flow(act, has)
                    if weight and has(i):
                        f.after(s_m, i)
                        f.after(s_w, i - 4)
                        nc.scalar.activation(sumT[u][:], m.bank[u % 2][:, 0:EG], ACT.Copy, scale=1.0 / 3.0).then_inc(s_sT, 1)
                    if has(i - 1):
                        v = (u - 1) % 4
                        f.after(s_w if weight else s_m, i - 1)
                        f.landed(s_sc, i - 5, v, 64)
                        nc.scalar.activation(out[v][:], m.bank[2 + v % 2][0:EP, :].rearrange("p (c f) -> p c f", c=TILE), ACT.Copy)\
                          .then_inc(s_o, 1)

                sweep(act, 0, n, n, body, back=5, ahead=0, special=0)

            @block.gpsimd
            def _(pool):
                def body(i, u, has):
                    f = Flow(pool, has, m)
                    f.after(s_o, i)
                    f.landed(s_sc, i - 4, u, 64)
                    scatter(nc, pool, f, index, idx, s_i, i, u, table, out, s_sc, add=True)

                sweep(pool, 0, n, n - 1, body, back=4, ahead=0, special=0)
                finish(pool, s_sc, n, 64)


def batch_norm(nc, m, a):
    N = m.N
    n = -(-N // ROWS)
    with Phase(m, "BN") as P:
        g, st = P.slots("g", [128, TILE, D]), P.sb("stats", [128, n * 6])
        mv, c = P.sb("mv", [128, 2]), P.sb("c", [128, 8])
        s_in, s_T, s_s, s_v, s_a, s_r = P.sems("g_in"), P.sem("turned"), P.sem("stats"), P.sem("chain"), P.sem("sqrt"), P.sem("rows")
        rest = N - (n - 1) * ROWS

        def rows_of(i):
            count = rest if isinstance(i, int) and i == n - 1 else ROWS
            return m.XG[bass.ds(i * ROWS, count), D:2 * D].rearrange("(p j) f -> p j f", j=TILE), count // TILE

        with nc.Block() as block:
            @block.sync
            def _(sp):
                def body(i, u, has):
                    f = Flow(sp, has)
                    f.after(s_T, i - 4)
                    rows, q = rows_of(i)
                    sp.dma_start(g[u][0:q], rows).then_inc(s_in[u], 16)

                sweep(sp, 0, n, n - 1, body, back=4, ahead=0, special=1)

            @block.tensor
            def _(pe):
                def body(i, u, has):
                    f = Flow(pe, has)
                    f.landed(s_in, i, u)
                    f.after(s_s, i - 4)
                    q = rows_of(i)[1]
                    for j in range(TILE):
                        last = nc.tensor.transpose(m.bank[u][:, j * q:(j + 1) * q], g[u][0:q, j, :], m.ident[0:q, 0:q])
                    last.then_inc(s_T, 1)

                sweep(pe, 0, n, n - 1, body, back=4, ahead=0, special=1)
                pe.wait_ge(s_v, 8)
                for k in range(2):
                    last = nc.tensor.matmul(m.bank[4][:, k * D:(k + 1) * D], c[:, 3 + k:4 + k].to_broadcast([128, 128]), m.ident[:],
                                            start=True, stop=True)
                last.then_inc(s_r, 1)

            @block.vector
            def _(dve):
                def body(i, u, has):
                    f = Flow(dve, has)
                    f.after(s_T, i)
                    nc.vector.bn_stats(st[:, bass.ds(i * 6, 6)], m.bank[u][:, 0:TILE * rows_of(i)[1]]).then_inc(s_s, 1)

                sweep(dve, 0, n, n - 1, body, back=4, ahead=0, special=1)
                dve.wait_ge(s_s, n)
                nc.vector.bn_aggr(mv[:], st[:]).then_inc(s_v, 1)
                nc.vector.tensor_tensor(c[:, 5:6], m.col["bO"], m.col["bI"], ALU.add).then_inc(s_v, 1)
                dve.wait_ge(s_v, 2)
                nc.vector.tensor_tensor(c[:, 6:7], c[:, 5:6], m.col["bS"], ALU.add).then_inc(s_v, 1)
                dve.wait_ge(s_a, 1)
                nc.vector.reciprocal(c[:, 1:2], c[:, 0:1]).then_inc(s_v, 1)
                dve.wait_ge(s_v, 4)
                nc.vector.tensor_tensor(c[:, 3:4], c[:, 1:2], m.col["gamma"], ALU.mult).then_inc(s_v, 1)
                nc.vector.scalar_tensor_tensor(c[:, 2:3], c[:, 6:7], 1.0 / 3.0, mv[:, 0:1], ALU.mult, ALU.add).then_inc(s_v, 1)
                dve.wait_ge(s_v, 6)
                nc.vector.scalar_tensor_tensor(c[:, 7:8], c[:, 6:7], 1.0 / 3.0, c[:, 2:3], ALU.mult, ALU.subtract).then_inc(s_v, 1)
                dve.wait_ge(s_v, 7)
                nc.vector.scalar_tensor_tensor(c[:, 4:5], c[:, 7:8], c[:, 3:4], m.col["beta"], ALU.mult, ALU.add).then_inc(s_v, 1)
                dve.wait_ge(s_r, 1)
                nc.vector.tensor_copy(m.Arow[:], m.bank[4][:, 0:D])
                nc.vector.tensor_copy(m.Brow[:], m.bank[4][:, D:2 * D]).then_inc(s_v, 1)

            @block.scalar
            def _(act):
                act.wait_ge(s_v, 1)
                nc.scalar.activation(c[:, 0:1], mv[:, 1:2], ACT.Sqrt, bias=m.col["eps"]).then_inc(s_a, 1)


def messages(nc, m, a):
    n = m.T // TILE
    with Phase(m, "G4") as P:
        idx, x = P.slots("idx", [EP, TILE], I32), P.slots("x", [EP, TILE, 2 * D])
        t, t2, x2, h, V = (P.slots(k, [EP, TILE, D]) for k in ("t", "t2", "x2", "h", "V"))
        hT, trow, one = P.slots("hT", [128, EG]), P.slots("types", [3 * TYPES, EG]), P.slots("onehot", [3 * TYPES, EG], BF16)
        ln = Norm(nc, m, P, TILE)
        s_i, s_t, s_x2, s_h, s_T, s_hT, s_m, s_one, s_v, s_hl = \
            (P.sem(k) for k in ("idx", "t", "x2", "h", "T", "hT", "m", "onehot", "v", "firstlast"))
        s_g, s_ty, s_vo = (P.sems(k) for k in ("got", "types", "v_out"))
        rows = lambda r: r[0:EP, :].unsqueeze(1).to_broadcast([EP, TILE, D])
        with nc.Block() as block:
            @block.gpsimd
            def _(pool):
                def body(i, u, has):
                    f = Flow(pool, has, m)
                    f.after(s_x2, i - 4)
                    gather(nc, pool, f, m.i_src, idx, s_i, i, u, m.XG, x, s_g)

                sweep(pool, 0, n, n - 1, body, back=4, ahead=0, special=0)

            @block.sync
            def _(sp):
                def load(f, i, u):
                    f.after(s_one, i - 4)
                    keys = m.KT.rearrange("t p -> (t p)")[bass.ds(i * EG, EG)].rearrange("(a n) -> a n", a=1)
                    sp.dma_start(trow[u][:], keys.to_broadcast([3 * TYPES, EG])).then_inc(s_ty[u], 16)

                def body(i, u, has):
                    f = Flow(sp, has)
                    if has(i + 3):
                        load(f, i + 3, (u + 3) % 4)
                    if has(i - 4):
                        f.after(s_v, i - 4)
                        sp.dma_start(value_tiles(m, i - 4)[0:EP], V[u][:]).then_inc(s_vo[u], 16)

                sweep(sp, -3, n, n + 3, body, back=4, ahead=3, special=0)
                finish(sp, s_vo, n)

            @block.vector
            def _(dve):
                def body(i, u, has):
                    f = Flow(dve, has)
                    if has(i - 1):
                        ln.finish(f, i - 1, (u - 1) % 4)
                    if has(i):
                        f.landed(s_g, i, u, 64)
                        nc.vector.tensor_tensor(t[u][:], x[u][:, :, D:2 * D], rows(m.Arow), ALU.mult).then_inc(s_t, 1)
                        dve.wait_ge(s_t, 2 * i + 1)
                        nc.vector.tensor_tensor(t2[u][:], t[u][:], rows(m.Brow), ALU.add).then_inc(s_t, 1)
                        dve.wait_ge(s_t, 2 * i + 2)
                        nc.vector.tensor_tensor(x2[u][:], t2[u][:], x[u][:, :, 0:D], ALU.add).then_inc(s_x2, 1)
                        f.after(s_x2, i)
                        ln.stats(dve, f, i, u, [x2[u][:, c, :] for c in range(TILE)])
                        f.landed(s_ty, i, u)
                        f.after(s_m, i - 4)
                        nc.vector.tensor_scalar(one[u][:], trow[u][:], m.type_id[:], None, ALU.is_equal).then_inc(s_one, 1)

                sweep(dve, 0, n, n, body, back=5, ahead=0, special=0)

            @block.scalar
            def _(act):
                def body(i, u, has):
                    f = Flow(act, has)
                    if has(i):
                        ln.root(f, i, u)
                    if has(i - 1):
                        v = (u - 1) % 4
                        f.after(ln.s_nb, i - 1)
                        f.after(s_T, i - 5)
                        ln.relu(h[v], [x2[v][:, c, :] for c in range(TILE)], v).then_inc(s_h, 1)
                    if has(i - 2):
                        v = (u - 2) % 4
                        f.after(s_T, i - 2)
                        f.after(s_m, i - 6)
                        nc.scalar.activation(hT[v][:], m.bank[v % 2][:, 0:EG], ACT.Copy).then_inc(s_hT, 1)

                    if has(i - 3):
                        v = (u - 3) % 4
                        f.after(s_m, i - 3)
                        f.landed(s_vo, i - 7, v)
                        f.after(s_hl, i - 7)
                        nc.scalar.activation(V[v][:], m.bank[2 + v % 2][0:EP, :].rearrange("p (c f) -> p c f", c=TILE), ACT.Copy).then_inc(s_v, 1)

                sweep(act, 0, n, n + 2, body, back=7, ahead=0, special=0)

            @block.tensor
            def _(pe):
                def body(i, u, has):
                    f = Flow(pe, has)
                    if has(i - 2):
                        v = (u - 2) % 4
                        f.after(s_h, i - 2)
                        f.after(s_hT, i - 4)
                        for c in range(TILE):
                            last = nc.tensor.transpose(m.bank[v % 2][:, c * EP:(c + 1) * EP], h[v][:, c, :], m.ident[0:EP, 0:EP])
                        last.then_inc(s_T, 1)
                    if has(i - 3):
                        v = (u - 3) % 4
                        f.after(s_hT, i - 3)
                        f.after(s_one, i - 3)
                        f.after(s_v, i - 5)
                        for c in range(TILE):
                            cs, o = slice(c * EP, (c + 1) * EP), m.bank[2 + v % 2][0:EP, c * D:(c + 1) * D]
                            nc.tensor.matmul(o, hT[v][:, cs], m.w["msg"], start=True, stop=False)
                            last = nc.tensor.matmul(o, one[v][:, cs], m.embed[:], start=False, stop=True)
                        last.then_inc(s_m, 1)
                    if has(i - 4):
                        f.after(s_v, i - 4)
                        first_last_sums(nc, m, V[u], i - 4).then_inc(s_hl, 1)

                sweep(pe, 0, n, n + 3, body, back=5, ahead=0, special=0)
    share_segments(nc, m, "G4_shared")


def gru(nc, m, a, sparse):
    N = m.N
    np_, W = (EP, EG) if sparse else (128, ROWS)
    n = m.T // TILE if sparse else -(-N // ROWS)
    span = W // TILE
    with Phase(m, "B5" if sparse else "P3") as P:
        x = P.slots("x", [np_, TILE, 2 * D])
        xb, t, h = (P.slots(k, [np_, TILE, D], count=2) for k in ("xb", "gA", "h"))
        x2 = P.slots("x2", [np_, TILE, D], count=8)
        out = P.slots("out", [np_, TILE, D])
        hT, r, z, rn, nT, dT, q, hn = (P.slots(k, [128, W], count=4 if k in ("hT", "z", "n") else 2)
                                       for k in ("hT", "r", "z", "rn", "n", "d", "q", "hnew"))
        st, mv, ve = P.slots("st", [np_, TILE, 6]), P.slots("mv", [np_, TILE, 2]), P.slots("ve", [np_, TILE])
        rs, nb = P.slots("rs", [np_, TILE]), P.slots("nb", [np_, TILE])
        s_x, s_o = P.sems("x_in"), P.sems("out")
        names = ("xb", "t", "x2", "st", "mv", "ve", "rs", "nb", "h", "T", "hT", "r_sum", "z_sum", "gates", "r", "z", "rn", "n", "d", "q", "hnew", "back", "fin")
        s = {k: P.sem(k) for k in names}
        bT, bB = m.bank[0:2]
        bR, bZ, bN = (m.bank[2:3], m.bank[3:4], m.bank[4:5]) if sparse else (m.bank[2:4], m.bank[4:6], m.bank[6:8])
        bI, bA = m.bank[5:7]
        B = len(bR)
        if sparse:
            V, krow, S = (P.slots("V", [EP + 2, TILE, D]), P.slots("krow", [EP + 2, EG]), P.slots("S", [EP + 2, EG]))
            agg, idx = P.slots("agg", [128, EG]), P.slots("idx", [EP, TILE], I32)
            hnm = P.slots("rnm", [128, W], count=2)
            s["t2"] = P.sem("t2")
            s_V, s_k = P.sems("V"), P.sems("k")
            s_sel, s_agg, s_ac, s_i = (P.sem(k) for k in ("sel", "agg", "aggcopy", "idx"))
        rows = lambda w: w[0:np_, :].unsqueeze(1).to_broadcast([np_, TILE, D])

        def base_of(g):
            return min(g * ROWS, N - ROWS) if isinstance(g, int) else g * ROWS

        special = 0 if sparse else 1
        per = 64 if sparse else 16
        with nc.Block() as block:
            @block.sync
            def _(sp):
                def load(f, i, u):
                    if sparse:
                        sum_loads(sp, m, f, i, u % 4, V, krow, s_V, s_k, s_sel, s_agg)
                    else:
                        f.after(s["x2"], i - 4)
                        sp.dma_start(x[u % 4][:], m.XG[bass.ds(base_of(i), ROWS), :].rearrange("(p j) f -> p j f", j=TILE))\
                          .then_inc(s_x[u % 4], 16)

                def body(i, u, has):
                    f = Flow(sp, has)
                    if has(i + 3):
                        load(f, i + 3, (u + 3) % 4)
                    if has(i - 8):
                        v = u % 4
                        f.after(s["fin"], i - 8)
                        if sparse:
                            sp.dma_start(edge_rows(m.XD, i - 8), out[v][:]).then_inc(s_o[v], 16)
                        else:
                            lo = ((n - 1) * ROWS - (N - ROWS)) // TILE if isinstance(i, int) and i - 8 == n - 1 else 0
                            sp.dma_start(m.out[bass.ds(base_of(i - 8) + lo * TILE, ROWS - lo * TILE), :].rearrange("(p j) f -> p j f", j=TILE),
                                         out[v][lo:128]).then_inc(s_o[v], 16)

                sweep(sp, -3, n, n + 7, body, unroll=8, back=8, ahead=3, special=special)
                finish(sp, s_o, n)

            @block.gpsimd
            def _(pool):
                def body(i, u, has):
                    f = Flow(pool, has)
                    if has(i - 1):
                        v = (u - 1) % 4
                        f.after(s["h"], i - 5)
                        f.after(s["ve"], i - 1)
                        nc.gpsimd.tensor_tensor(rs[v][:], ve[v][:], m.minus_half[0:np_, :], ALU.pow).then_inc(s["rs"], 1)
                    if has(i - 5):
                        v = (u - 5) % 4
                        f.after(s["n"], i - 5)
                        f.after(s["q"], i - 7)
                        nc.gpsimd.tensor_tensor(dT[v % 2][:], hT[v][:], nT[v][:], ALU.subtract).then_inc(s["d"], 1)
                    if has(i + 1):
                        v = (u + 1) % 4
                        if not sparse:
                            f.after(s["x2"], i - 1)
                            f.landed(s_x, i + 1, v, per)
                            nc.gpsimd.tensor_tensor(xb[v % 2][:], x[v][:, :, 0:D], rows(m.Brow), ALU.add).then_inc(s["xb"], 1)
                            nc.gpsimd.tensor_tensor(t[v % 2][:], x[v][:, :, D:2 * D], rows(m.Arow), ALU.mult).then_inc(s["t"], 1)
                    if sparse and has(i + 2):
                        g = Flow(pool, has, m)
                        g.after(s["x2"], i - 2)
                        gather(nc, pool, g, m.i_dst, idx, s_i, i + 2, (u + 2) % 4, m.XG, x, s_x)

                sweep(pool, -2 if sparse else -1, n, n + 4, body, unroll=8, back=7, ahead=2, special=special)

            @block.vector
            def _(dve):
                def body(i, u, has):
                    f = Flow(dve, has)
                    if has(i - 8):
                        v = u % 4
                        f.after(s["back"], i - 8)
                        f.landed(s_o, i - 12, v)
                        nc.vector.tensor_tensor(out[v][:], bB[0:np_, :].rearrange("p (c f) -> p c f", c=TILE), x2[u][:], ALU.add)\
                          .then_inc(s["fin"], 1)
                    if sparse and has(i + 1):
                        selectors(nc, m, f, i + 1, (u + 1) % 4, krow, S, s_k, s_sel, s_agg, mean=False)
                    if has(i):
                        v = u % 4
                        if sparse:
                            f.landed(s_x, i, v, per)
                            nc.vector.tensor_tensor(t[v % 2][:], x[v][:, :, D:2 * D], rows(m.Arow), ALU.mult).then_inc(s["t"], 1)
                            nc.vector.tensor_tensor(xb[v % 2][:], x[v][:, :, 0:D], rows(m.Brow), ALU.add).then_inc(s["xb"], 1)
                        f.after(s["t"], i)
                        f.after(s["xb"], i)
                        f.after(s["fin"], i - 8)
                        nc.vector.tensor_tensor(x2[u][:], t[v % 2][:], xb[v % 2][:], ALU.add).then_inc(s["x2"], 1)
                    if has(i - 6):
                        v = (u - 6) % 4
                        f.after(s["d"], i - 6)
                        nc.vector.tensor_tensor(q[v % 2][:], z[v][:], dT[v % 2][:], ALU.mult).then_inc(s["q"], 1)
                    if has(i):
                        v = u % 4
                        f.after(s["x2"], i)
                        for j in range(TILE):
                            last = nc.vector.bn_stats(st[v][:, j, :], x2[u][:, j, :])
                        last.then_inc(s["st"], 1)
                    if has(i - 6):
                        v = (u - 6) % 4
                        f.after(s["q"], i - 6)
                        f.after(s["back"], i - 8)
                        nc.vector.tensor_tensor(hn[v % 2][:], nT[v][:], q[v % 2][:], ALU.add).then_inc(s["hnew"], 1)
                    if has(i):
                        v = u % 4
                        Flow(dve, has, m).after(s["st"], i)
                        for j in range(TILE):
                            last = nc.vector.bn_aggr(mv[v][:, j, :], st[v][:, j, :])
                        last.then_inc(s["mv"], 1)
                        f.after(s["mv"], i)
                        nc.vector.tensor_scalar(ve[v][:], mv[v][:, :, 1], LN_EPS, None, ALU.add).then_inc(s["ve"], 1)
                    if has(i - 1):
                        v = (u - 1) % 4
                        f.after(s["rs"], i - 1)
                        nc.vector.scalar_tensor_tensor(nb[v][:], mv[v][:, :, 0], -1.0, rs[v][:], ALU.mult, ALU.mult).then_inc(s["nb"], 1)
                    if has(i - 4):
                        v = u % 4
                        f.after(s["r"], i - 4)
                        f.after(s["gates"], i - 4)
                        f.after(s["n"], i - 6)
                        rn_of = s["t2"] if sparse else s["rn"]
                        nc.vector.scalar_tensor_tensor(rn[v % 2][:], bN[v % B][:, 0:W], m.col["bhh_n"], r[v % 2][:], ALU.add, ALU.mult)\
                          .then_inc(rn_of, 1)
                        if sparse:
                            f.after(s["t2"], i - 4)
                            nc.vector.tensor_tensor(hnm[v % 2][:], rn[v % 2][:], bI[:, 0:W], ALU.add).then_inc(s["rn"], 1)

                sweep(dve, -1, n, n + 7, body, unroll=8, back=12, ahead=1, special=special)

            @block.scalar
            def _(act):
                def body(i, u, has):
                    f = Flow(act, has)
                    if sparse and has(i - 1):
                        v = (u - 1) % 4
                        f.after(s_agg, i - 1)
                        f.after(s["gates"], i - 5)
                        nc.scalar.activation(agg[v][:], bA[:, 0:EG], ACT.Copy).then_inc(s_ac, 1)
                    if has(i - 3):
                        v = (u - 3) % 4
                        f.after(s["T"], i - 3)
                        f.after(s["d"], i - 7)
                        nc.scalar.activation(hT[v][:], bT[:, 0:W], ACT.Copy).then_inc(s["hT"], 1)
                    if has(i - 5):
                        v = (u - 5) % 4
                        f.after(s["rn"], i - 5)
                        f.after(s["hnew"], i - 9)
                        nc.scalar.activation(nT[v][:], (hnm if sparse else rn)[v % 2][:], ACT.Tanh, bias=m.col["bih_n"]).then_inc(s["n"], 1)
                    if has(i - 2):
                        v = (u - 2) % 4
                        f.after(s["nb"], i - 2)
                        f.after(s["T"], i - 4)
                        for j in range(TILE):
                            last = nc.scalar.activation(h[v % 2][:, j, :], x2[(u - 2) % 8][:, j, :], ACT.Relu, scale=rs[v][:, j:j + 1], bias=nb[v][:, j:j + 1])
                        last.then_inc(s["h"], 1)
                    if has(i - 4):
                        v = u % 4
                        f.after(s["r_sum"], i - 4)
                        f.after(s["rn"], i - 6)
                        nc.scalar.activation(r[v % 2][:], bR[v % B][:, 0:W], ACT.Sigmoid, bias=m.col["b_r"]).then_inc(s["r"], 1)
                        f.after(s["z_sum"], i - 4)
                        f.after(s["q"], i - 8)
                        nc.scalar.activation(z[v][:], bZ[v % B][:, 0:W], ACT.Sigmoid, bias=m.col["b_z"]).then_inc(s["z"], 1)

                sweep(act, 0, n, n + 4, body, unroll=8, back=9, ahead=0, special=special)

            @block.tensor
            def _(pe):
                def body(i, u, has):
                    f = Flow(pe, has)
                    if has(i - 3):
                        v = (u - 3) % 4
                        f.after(s["h"], i - 3)
                        f.after(s["hT"], i - 4)
                        for c in range(TILE):
                            last = nc.tensor.transpose(bT[:, c * span:(c + 1) * span], h[v % 2][:, c, :], m.ident[0:span, 0:span])
                        last.then_inc(s["T"], 1)
                    if sparse and has(i):
                        f.after(s_ac, i - 1)
                        add_up(nc, m, f, i, u % 4, V, S, bA, s_V, s_sel, s_agg)
                    if has(i - 4):
                        v = u % 4
                        f.after(s["hT"], i - 4)
                        f.after(s["z"], i - 4 - B)
                        f.after(s["rn"], i - 4 - B)
                        if sparse:
                            f.after(s_ac, i - 4)
                        for bank, gate in ((bR, "r"), (bZ, "z"), (bN, "n")):
                            with_m = sparse and gate != "n"
                            last = nc.tensor.matmul(bank[v % B][:, 0:W], m.w["hh_" + gate], hT[v][:], start=True, stop=not with_m)
                            if with_m:
                                last = nc.tensor.matmul(bank[v % B][:, 0:W], m.w["ih_" + gate], agg[v][:], start=False, stop=True)
                            if sparse and gate == "n":
                                last = nc.tensor.matmul(bI[:, 0:W], m.w["ih_n"], agg[v][:], start=True, stop=True)
                            last.then_inc(s[{"r": "r_sum", "z": "z_sum", "n": "gates"}[gate]], 1)
                    if has(i - 7):
                        v = (u - 7) % 4
                        f.after(s["hnew"], i - 7)
                        f.after(s["fin"], i - 8)
                        for c in range(TILE):
                            last = nc.tensor.transpose(bB[0:np_, c * D:(c + 1) * D], hn[v % 2][:, c * span:(c + 1) * span], m.ident[:])
                        last.then_inc(s["back"], 1)

                sweep(pe, 0, n, n + 6, body, unroll=8, back=8, ahead=0, special=special)


def leaving(nc, m, a):
    n = m.T // TILE
    with Phase(m, "O1") as P:
        idx, x, h, L = P.slots("idx", [EP, TILE], I32), *(P.slots(k, [EP, TILE, D]) for k in ("x", "h", "L"))
        hT = P.slots("hT", [128, EG])
        ln = Norm(nc, m, P, TILE)
        s_i, s_h, s_T, s_hT, s_m, s_l = (P.sem(k) for k in ("idx", "h", "T", "hT", "m", "l"))
        s_x, s_lo, s_sc = (P.sems(k) for k in ("x", "l_out", "x3_out"))
        with nc.Block() as block:
            @block.gpsimd
            def _(pool):
                def body(i, u, has):
                    f = Flow(pool, has, m)
                    f.landed(s_x, i, u)
                    scatter(nc, pool, f, m.i_dstf, idx, s_i, i, u, m.out, x, s_sc)

                sweep(pool, 0, n, n - 1, body, back=4, ahead=0, special=0)
                finish(pool, s_sc, n, 64)

            @block.sync
            def _(sp):
                def load(f, i, u):
                    f.after(s_h, i - 4)
                    f.landed(s_sc, i - 4, u, 64)
                    sp.dma_start(x[u][:], edge_rows(m.XD, i)).then_inc(s_x[u], 16)

                def body(i, u, has):
                    f = Flow(sp, has)
                    if has(i + 3):
                        load(f, i + 3, (u + 3) % 4)
                    if has(i - 4):
                        f.after(s_l, i - 4)
                        sp.dma_start(edge_rows(m.LT, i - 4), L[u][:]).then_inc(s_lo[u], 16)

                sweep(sp, -3, n, n + 3, body, back=4, ahead=3, special=0)
                finish(sp, s_lo, n)

            @block.vector
            def _(dve):
                def body(i, u, has):
                    f = Flow(dve, has)
                    if has(i - 1):
                        ln.finish(f, i - 1, (u - 1) % 4)
                    if has(i):
                        f.landed(s_x, i, u)
                        ln.stats(dve, f, i, u, [x[u][:, c, :] for c in range(TILE)])
                    if has(i - 3):
                        v = (u - 3) % 4
                        f.after(s_m, i - 3)
                        f.landed(s_lo, i - 7, v)
                        nc.vector.tensor_tensor(L[v][:], m.bank[2 + v % 2][0:EP, :].rearrange("p (c f) -> p c f", c=TILE),
                                                m.boutrow[0:EP, :].unsqueeze(1).to_broadcast([EP, TILE, D]), ALU.add).then_inc(s_l, 1)

                sweep(dve, 0, n, n + 2, body, back=7, ahead=0, special=0)

            @block.scalar
            def _(act):
                def body(i, u, has):
                    f = Flow(act, has)
                    if has(i):
                        ln.root(f, i, u)
                    if has(i - 1):
                        v = (u - 1) % 4
                        f.after(ln.s_nb, i - 1)
                        f.after(s_T, i - 5)
                        ln.relu(h[v], [x[v][:, c, :] for c in range(TILE)], v).then_inc(s_h, 1)
                    if has(i - 2):
                        v = (u - 2) % 4
                        f.after(s_T, i - 2)
                        f.after(s_m, i - 6)
                        nc.scalar.activation(hT[v][:], m.bank[v % 2][:, 0:EG], ACT.Copy).then_inc(s_hT, 1)

                sweep(act, 0, n, n + 1, body, back=6, ahead=0, special=0)

            @block.tensor
            def _(pe):
                def body(i, u, has):
                    f = Flow(pe, has)
                    if has(i - 2):
                        v = (u - 2) % 4
                        f.after(s_h, i - 2)
                        f.after(s_hT, i - 4)
                        for c in range(TILE):
                            last = nc.tensor.transpose(m.bank[v % 2][:, c * EP:(c + 1) * EP], h[v][:, c, :], m.ident[0:EP, 0:EP])
                        last.then_inc(s_T, 1)
                    if has(i - 3):
                        v = (u - 3) % 4
                        f.after(s_hT, i - 3)
                        f.after(s_l, i - 5)
                        for c in range(TILE):
                            last = nc.tensor.matmul(m.bank[2 + v % 2][0:EP, c * D:(c + 1) * D], hT[v][:, c * EP:(c + 1) * EP], m.w["out"],
                                                    start=True, stop=True)
                        last.then_inc(s_m, 1)

                sweep(pe, 0, n, n + 2, body, back=5, ahead=0, special=0)


def network(nc, m, a):
    with ExitStack() as ctx:
        m.ctx = ctx
        m.bank = [ctx.enter_context(nc.psum_tensor(f"bank{k}", [128, 512], F32)) for k in range(8)]
        m.XG = nc.dram_tensor("node_table", [m.N, 2 * D], F32, kind="Internal").ap()
        m.XH = m.XG.rearrange("n (h f) -> (n h) f", h=2)
        load_weights(nc, m, a)
        order_edges(nc, m, a)
        edges_setup(nc, m, a)
        edges_start(nc, m, a)
        layer(nc, m, 1, m.HDa, m.HDb, m.TB1[0:m.E, :])
        take(nc, m, a, 1, m.TB1, 2)
        layer(nc, m, 2, m.HDb, m.HDa, m.TB2[0:m.E, :])
        take(nc, m, a, 2, m.TB2, 3)
        third_layer(nc, m, a)
        incoming(nc, m, a)
        outgoing_self(nc, m, a)
        add_to_src(nc, m, "H", m.H1, m.XH, m.i_src2f1, weight=m.w["I"])
        batch_norm(nc, m, a)
        messages(nc, m, a)
        gru(nc, m, a, False)
        gru(nc, m, a, True)
        leaving(nc, m, a)
        add_to_src(nc, m, "O2", m.LT, m.out, m.i_srcf)


def kernel(**inputs):
    import numpy as _np
    import concourse.bacc as _bacc
    from concourse import mybir as _mybir
    from concourse.bass_utils import run_bass_kernel_spmd as _run

    nc = _bacc.Bacc("TRN2", target_bir_lowering=False, num_devices=1)
    arrays, a = {}, {}
    for name, value in inputs.items():
        arrays[name] = _np.ascontiguousarray(value)
        a[name] = nc.dram_tensor(name, list(arrays[name].shape), _mybir.dt.from_np(arrays[name].dtype), kind="ExternalInput").ap()
    N, E = arrays["x"].shape[0], arrays["src"].shape[0]
    m = Net(nc, None, N, E)
    m.out = nc.dram_tensor("out", [N, D], _mybir.dt.float32, kind="ExternalOutput").ap()
    network(nc, m, a)
    r = _run(nc, [arrays], core_ids=[0])
    return r.results[0]["out"]
```
